# Optimizing a Trainium2 kernel written in Bass

```python
import numpy as np
import jax
import jax.numpy as jnp

def _softmax(x, axis=-1):
    return jax.nn.softmax(x, axis=axis)

def _gelu(x):
    return jax.nn.gelu(x, approximate=True)

def _silu(x):
    return jax.nn.silu(x)

def _sigmoid(x):
    return jax.nn.sigmoid(x)

def _layernorm(x, axis=-1, eps=1e-05):
    m = jnp.mean(x, axis=axis, keepdims=True)
    v = jnp.var(x, axis=axis, keepdims=True)
    return (x - m) / jnp.sqrt(v + eps)

def _scatter_add(tgt, idx, src, axis=0):
    return tgt.at[idx].add(src)

def _segment_sum(src, seg, n):
    return jax.ops.segment_sum(src, seg, n)
kernel_name = 'mk_gps_d1_gnn_r8_5c211b'

def setup_inputs(seed: int=0):
    np.random.seed(seed)
    _w = jnp.asarray

    def _rec_inputs():
        import jax
        import jax.numpy as jnp
        _gk = jax.random.key(seed)
        x = -8.776e-05 + 1 * jax.random.normal(jax.random.fold_in(_gk, 1), (6250, 256), jnp.float32)
        src = jax.random.randint(jax.random.fold_in(_gk, 2), (200000,), 0, 6250, jnp.int32)
        dst = jnp.minimum((6250 * jax.random.uniform(jax.random.fold_in(_gk, 3), (200000,)) ** 2.0).astype(jnp.int32), 49999)
        _o = jnp.argsort(dst, stable=True)
        src = src[_o]
        dst = dst[_o]
        edge_attr_10 = jax.random.uniform(jax.random.fold_in(_gk, 13), (200000, 10), jnp.float32, 0.0, 1)
        edge_attr_4 = 0.000924777 + 0.999162 * jax.random.normal(jax.random.fold_in(_gk, 14), (200000, 4), jnp.float32)
        node_vec1 = jax.random.uniform(jax.random.fold_in(_gk, 15), (6250, 1), jnp.float32, 0.0, 1)
        return (x, src, dst, edge_attr_10, edge_attr_4, node_vec1)
    x, src, dst, edge_attr_10, edge_attr_4, node_vec1 = _rec_inputs()

    def _L0_gnn_setup():
        import jax, jax.numpy as jnp
        import numpy as np
        import math
        N_NODES = 2500
        N_EDGES = 40000
        MUL = 64
        N_BASIS = 10
        N_HID = 100
        W_NUMEL = 4 * MUL

        def _split(x):
            s = x[..., :MUL]
            v = x[..., MUL:].reshape(x.shape[:-1] + (MUL, 3))
            return (s, v)

        def _fctp(s, v, W0, W1, attr, fan_in):
            inv = 1.0 / math.sqrt(fan_in)
            o0 = jnp.einsum('nu,uk->nk', s, W0) * attr * inv
            o1 = jnp.einsum('num,uk->nkm', v, W1) * attr[..., None] * inv
            return (o0, o1)
        key = jax.random.key(seed)
        ks = jax.random.split(key, 16)
        node_input = jax.random.normal(ks[0], (N_NODES, 4 * MUL), dtype=jnp.float32)
        node_attr = jnp.ones((N_NODES, 1), dtype=jnp.float32)
        node_deg = jax.random.randint(ks[1], (N_NODES, 1), 1, 33).astype(jnp.float32)
        edge_src = jax.random.randint(ks[2], (N_EDGES,), 0, N_NODES)
        edge_dst = jax.random.randint(ks[3], (N_EDGES,), 0, N_NODES)
        edge_attr = jax.random.normal(ks[4], (N_EDGES, 4), dtype=jnp.float32)
        edge_length_embedded = jax.random.uniform(ks[5], (N_EDGES, N_BASIS), dtype=jnp.float32)
        W_li0 = jax.random.normal(ks[6], (MUL, MUL), dtype=jnp.float32)
        W_li1 = jax.random.normal(ks[7], (MUL, MUL), dtype=jnp.float32)
        W_lm0 = jax.random.normal(ks[8], (MUL, MUL), dtype=jnp.float32)
        W_lm1 = jax.random.normal(ks[9], (MUL, MUL), dtype=jnp.float32)
        W_mlp1 = jax.random.normal(ks[10], (N_BASIS, N_HID), dtype=jnp.float32)
        W_mlp2 = jax.random.normal(ks[11], (N_HID, W_NUMEL), dtype=jnp.float32)
        W_lo0 = jax.random.normal(ks[12], (2 * MUL, MUL), dtype=jnp.float32)
        W_lo1 = jax.random.normal(ks[13], (2 * MUL, MUL), dtype=jnp.float32)
        return dict(node_input=node_input, node_attr=node_attr, node_deg=node_deg, edge_attr=edge_attr, edge_length_embedded=edge_length_embedded, W_li0=W_li0, W_li1=W_li1, W_lm0=W_lm0, W_lm1=W_lm1, W_mlp1=W_mlp1, W_mlp2=W_mlp2, W_lo0=W_lo0, W_lo1=W_lo1, edge_src=edge_src, edge_dst=edge_dst)
    _L0_gnn_all = _L0_gnn_setup()
    _L0_gnn_in = {k: v for k, v in _L0_gnn_all.items() if k in ('W_li0', 'W_li1', 'W_lm0', 'W_lm1', 'W_mlp1', 'W_mlp2', 'W_lo0', 'W_lo1')}
    del _L0_gnn_all

    def _L0_mix_setup():
        import jax, jax.numpy as jnp
        import numpy as np
        NUM_HEADS = 8
        key = jax.random.key(seed)
        ks = jax.random.split(key, 5)
        B, N, C = (8, 2048, 256)
        x = jax.random.normal(ks[0], (B, N, C), dtype=jnp.float32)
        Wq = jax.random.normal(ks[1], (C, C), dtype=jnp.float32) * 0.02
        Wkv = jax.random.normal(ks[2], (2 * C, C), dtype=jnp.float32) * 0.02
        Wproj = jax.random.normal(ks[3], (C, C), dtype=jnp.float32) * 0.02
        bproj = jnp.zeros((C,), dtype=jnp.float32)
        return {'x': x, 'Wq': Wq, 'Wkv': Wkv, 'Wproj': Wproj, 'bproj': bproj}
    _L0_mix_all = _L0_mix_setup()
    _L0_mix_in = {k: v for k, v in _L0_mix_all.items() if k in ('Wq', 'Wkv', 'Wproj', 'bproj')}
    del _L0_mix_all

    def _L0_ffn_setup():
        import jax, jax.numpy as jnp
        import numpy as np
        TOP_K = 2
        LN_EPS = 1e-05
        key = jax.random.key(seed)
        ks = jax.random.split(key, 8)
        B, S, D, E, H = (16, 1024, 256, 8, 1024)
        x = jax.random.normal(ks[0], (B, S, D), dtype=jnp.float32)
        Wr = jax.random.normal(ks[1], (D, E), dtype=jnp.float32) * 0.1
        br = jnp.zeros((E,), dtype=jnp.float32)
        ln_g = jnp.ones((E, D), dtype=jnp.float32)
        ln_b = jnp.zeros((E, D), dtype=jnp.float32)
        W1 = jax.random.normal(ks[2], (E, D, H), dtype=jnp.float32) * (1.0 / np.sqrt(D))
        b1 = jnp.zeros((E, H), dtype=jnp.float32)
        W2 = jax.random.normal(ks[3], (E, H, D), dtype=jnp.float32) * (1.0 / np.sqrt(H))
        b2 = jnp.zeros((E, D), dtype=jnp.float32)
        return {'x': x, 'Wr': Wr, 'br': br, 'ln_g': ln_g, 'ln_b': ln_b, 'W1': W1, 'b1': b1, 'W2': W2, 'b2': b2}
    _L0_ffn_all = _L0_ffn_setup()
    _L0_ffn_in = {k: v for k, v in _L0_ffn_all.items() if k in ('Wr', 'br', 'ln_g', 'ln_b', 'W1', 'b1', 'W2', 'b2')}
    del _L0_ffn_all
    return {'x': x, 'src': src, 'dst': dst, 'edge_attr_10': edge_attr_10, 'edge_attr_4': edge_attr_4, 'node_vec1': node_vec1, 'L0_gnn_W_li0': _L0_gnn_in['W_li0'], 'L0_gnn_W_li1': _L0_gnn_in['W_li1'], 'L0_gnn_W_lm0': _L0_gnn_in['W_lm0'], 'L0_gnn_W_lm1': _L0_gnn_in['W_lm1'], 'L0_gnn_W_mlp1': _L0_gnn_in['W_mlp1'], 'L0_gnn_W_mlp2': _L0_gnn_in['W_mlp2'], 'L0_gnn_W_lo0': _L0_gnn_in['W_lo0'], 'L0_gnn_W_lo1': _L0_gnn_in['W_lo1'], 'L0_mix_Wq': _L0_mix_in['Wq'], 'L0_mix_Wkv': _L0_mix_in['Wkv'], 'L0_mix_Wproj': _L0_mix_in['Wproj'], 'L0_mix_bproj': _L0_mix_in['bproj'], 'L0_ffn_Wr': _L0_ffn_in['Wr'], 'L0_ffn_br': _L0_ffn_in['br'], 'L0_ffn_ln_g': _L0_ffn_in['ln_g'], 'L0_ffn_ln_b': _L0_ffn_in['ln_b'], 'L0_ffn_W1': _L0_ffn_in['W1'], 'L0_ffn_b1': _L0_ffn_in['b1'], 'L0_ffn_W2': _L0_ffn_in['W2'], 'L0_ffn_b2': _L0_ffn_in['b2']}

def reference(x, src, dst, edge_attr_10, edge_attr_4, node_vec1, L0_gnn_W_li0, L0_gnn_W_li1, L0_gnn_W_lm0, L0_gnn_W_lm1, L0_gnn_W_mlp1, L0_gnn_W_mlp2, L0_gnn_W_lo0, L0_gnn_W_lo1, L0_mix_Wq, L0_mix_Wkv, L0_mix_Wproj, L0_mix_bproj, L0_ffn_Wr, L0_ffn_br, L0_ffn_ln_g, L0_ffn_ln_b, L0_ffn_W1, L0_ffn_b1, L0_ffn_W2, L0_ffn_b2):
    import jax
    import jax.numpy as jnp

    def _L0_gnn_ref(node_input, node_attr, node_deg, edge_attr, edge_length_embedded, W_li0, W_li1, W_lm0, W_lm1, W_mlp1, W_mlp2, W_lo0, W_lo1, edge_src, edge_dst):
        import jax, jax.numpy as jnp
        import numpy as np
        import math
        N_NODES = 2500
        N_EDGES = 40000
        MUL = 64
        N_BASIS = 10
        N_HID = 100
        W_NUMEL = 4 * MUL

        def _split(x):
            s = x[..., :MUL]
            v = x[..., MUL:].reshape(x.shape[:-1] + (MUL, 3))
            return (s, v)

        def _fctp(s, v, W0, W1, attr, fan_in):
            inv = 1.0 / math.sqrt(fan_in)
            o0 = jnp.einsum('nu,uk->nk', s, W0) * attr * inv
            o1 = jnp.einsum('num,uk->nkm', v, W1) * attr[..., None] * inv
            return (o0, o1)
        N = node_input.shape[0]
        x0, x1 = _split(node_input)
        f0, f1 = _fctp(x0, x1, W_li0, W_li1, node_attr, MUL)
        deg_isqrt = 1.0 / jnp.sqrt(node_deg)
        f0 = f0 * deg_isqrt
        f1 = f1 * deg_isqrt[..., None]
        m0, m1 = _fctp(x0, x1, W_lm0, W_lm1, node_attr, MUL)
        h = jax.nn.silu(edge_length_embedded @ W_mlp1 / math.sqrt(N_BASIS))
        ew = h @ W_mlp2 / math.sqrt(N_HID)
        wa, wb, wc, wd = (ew[:, :MUL], ew[:, MUL:2 * MUL], ew[:, 2 * MUL:3 * MUL], ew[:, 3 * MUL:])
        g0 = f0[edge_src]
        g1 = f1[edge_src]
        y0 = edge_attr[:, 0]
        y1 = edge_attr[:, 1:4]
        m0a = wa * g0 * y0[:, None]
        m0b = wb * jnp.einsum('eum,em->eu', g1, y1) / math.sqrt(3.0)
        m1a = wc[:, :, None] * g0[:, :, None] * y1[:, None, :]
        m1b = wd[:, :, None] * g1 * y0[:, None, None]
        s_mid = jax.ops.segment_sum(jnp.concatenate([m0a, m0b], axis=1), edge_dst, num_segments=N)
        v_mid = jax.ops.segment_sum(jnp.concatenate([m1a, m1b], axis=1), edge_dst, num_segments=N)
        s_mid = s_mid * deg_isqrt
        v_mid = v_mid * deg_isqrt[..., None]
        o0, o1 = _fctp(s_mid, v_mid, W_lo0, W_lo1, node_attr, 2 * MUL)
        c_s, c_x = (math.sin(math.pi / 8), math.cos(math.pi / 8))
        out0 = c_s * m0 + c_x * o0
        out1 = c_s * m1 + c_x * o1
        return jnp.concatenate([out0, out1.reshape(N, 3 * MUL)], axis=1)

    def _L0_mix_ref(x, Wq, Wkv, Wproj, bproj):
        import jax, jax.numpy as jnp
        import numpy as np
        NUM_HEADS = 8
        B, N, C = x.shape
        h = NUM_HEADS
        d = C // h
        q = jnp.einsum('bnc,oc->bno', x, Wq).reshape(B, N, h, d).transpose(0, 2, 1, 3)
        kv = jnp.einsum('bnc,oc->bno', x, Wkv).reshape(B, N, 2, h, d)
        k = kv[:, :, 0].transpose(0, 2, 1, 3)
        v = kv[:, :, 1].transpose(0, 2, 1, 3)
        q = jax.nn.elu(q) + 1.0
        k = jax.nn.elu(k) + 1.0
        k_sum = k.sum(axis=2)
        D_inv = 1.0 / jnp.maximum(jnp.einsum('bhnd,bhd->bhn', q, k_sum), 1e-06)
        context = jnp.einsum('bhnd,bhne->bhde', k, v)
        attn = jnp.einsum('bhnd,bhde->bhne', q, context) * D_inv[..., None]
        out = attn.transpose(0, 2, 1, 3).reshape(B, N, C)
        out = jnp.einsum('bnc,oc->bno', out, Wproj) + bproj
        return out

    def _L0_ffn_ref(x, Wr, br, ln_g, ln_b, W1, b1, W2, b2):
        import jax, jax.numpy as jnp
        import numpy as np
        TOP_K = 2
        LN_EPS = 1e-05
        B, S, D = x.shape
        N = B * S
        xt = x.reshape(N, D)
        logits = xt @ Wr + br
        probs = jax.nn.softmax(logits, axis=-1)
        top_p, top_idx = jax.lax.top_k(probs, TOP_K)
        weights = top_p / top_p.sum(axis=-1, keepdims=True)
        mu = xt.mean(axis=-1, keepdims=True)
        var = ((xt - mu) ** 2).mean(axis=-1, keepdims=True)
        xn = (xt - mu) * jax.lax.rsqrt(var + LN_EPS)
        xe = xn[None, :, :] * ln_g[:, None, :] + ln_b[:, None, :]
        h = jax.nn.gelu(jnp.einsum('end,edh->enh', xe, W1) + b1[:, None, :], approximate=False)
        y = jnp.einsum('enh,ehd->end', h, W2) + b2[:, None, :]
        y_tok = jnp.transpose(y, (1, 0, 2))
        sel = jnp.take_along_axis(y_tok, top_idx[:, :, None], axis=1)
        out = (weights[:, :, None] * sel).sum(axis=1)
        return out.reshape(B, S, D)
    deg = jnp.maximum(jax.ops.segment_sum(jnp.ones(dst.shape, jnp.float32), dst, num_segments=6250), 1.0)
    xn = _layernorm(x, axis=-1)
    x = x + _L0_gnn_ref(xn, node_vec1, deg[:, None], edge_attr_4, edge_attr_10, L0_gnn_W_li0, L0_gnn_W_li1, L0_gnn_W_lm0, L0_gnn_W_lm1, L0_gnn_W_mlp1, L0_gnn_W_mlp2, L0_gnn_W_lo0, L0_gnn_W_lo1, src, dst) + _L0_mix_ref(xn[None], L0_mix_Wq, L0_mix_Wkv, L0_mix_Wproj, L0_mix_bproj)[0]
    x = x + _L0_ffn_ref(_layernorm(x, axis=-1)[None], L0_ffn_Wr, L0_ffn_br, L0_ffn_ln_g, L0_ffn_ln_b, L0_ffn_W1, L0_ffn_b1, L0_ffn_W2, L0_ffn_b2)[0]
    return x

_drawn_inputs = setup_inputs


def setup_inputs(seed=0):
    import zlib

    import numpy as np

    out = dict(_drawn_inputs(seed))
    spreads = {'L0_mix_bproj': (0.0, 0.1),
     'L0_ffn_br': (0.0, 0.1),
     'L0_ffn_ln_g': (1.0, 0.2),
     'L0_ffn_ln_b': (0.0, 0.1),
     'L0_ffn_b1': (0.0, 0.1),
     'L0_ffn_b2': (0.0, 0.1)}
    factors = {'L0_mix_Wq': 8.0, 'L0_mix_Wkv': 5.66, 'L0_mix_Wproj': 5.597}
    for name, (base, spread) in spreads.items():
        noise = np.random.default_rng([zlib.crc32(name.encode()), seed]).standard_normal(out[name].shape)
        drawn = base * np.exp(spread * noise) if base else spread * noise
        out[name] = jnp.asarray(drawn.astype(out[name].dtype))
    for name, factor in factors.items():
        out[name] = (out[name] * factor).astype(out[name].dtype)
    return out
```

```python
from contextlib import ExitStack
import math

import concourse.bass as bass
from concourse import mybir

P = 128
N_NODES, D, MUL = 6250, 256, 64
NT = -(-N_NODES // P)
N_PAD = NT * P
N_EDGES = 200000
GE, GC = 512, 4
NG = -(-N_EDGES // GE)
NGP = 4 * P
NB = NT
NI = NG + NB
HID, BAS = 100, 10
HEADS, HD = 8, 32
E, H, TOP = 8, 1024, 2
SB = 256
NSB = (TOP * N_PAD + E * (SB - 1)) // SB
NSLOT = NSB * SB
EPS = 1e-5
C_S, C_X = math.sin(math.pi / 8), math.cos(math.pi / 8)

f32, bf16, i32 = mybir.dt.float32, mybir.dt.bfloat16, mybir.dt.int32
ALU, ACT, AX = mybir.AluOpType, mybir.ActivationFunctionType, mybir.AxisListType


def steps(eng, count, unroll, head, body):
    loops = (count - head) // unroll
    for n in range(head):
        body(n, n % unroll)
    if loops:
        with eng.Fori(0, loops) as i:
            for j in range(unroll):
                body(i * unroll + (head + j), (head + j) % unroll)
    for n in range(head + loops * unroll, count):
        body(n, n % unroll)


def wait_apart(eng, passed, *waits):
    for sem, v in waits:
        eng.wait_ge(sem, v)
    eng.sem_inc(passed, 1)


class Mem:

    def __init__(self, nc, ctx, prefix):
        self.nc, self.ctx, self.prefix = nc, ctx, prefix

    def sb(self, name, shape, dt=f32):
        return self.ctx.enter_context(self.nc.sbuf_tensor(f"{self.prefix}_{name}", shape, dt))

    def ps(self, name, banks=1):
        return self.ctx.enter_context(self.nc.psum_tensor(f"{self.prefix}_ps_{name}", [P, 512 * banks], f32))

    def sem(self, name):
        return self.nc.alloc_semaphore(f"{self.prefix}_{name}")


def setup(nc, A, K):
    with ExitStack() as ctx:
        m = Mem(nc, ctx, "setup")
        loaded, made, scaled = m.sem("loaded"), m.sem("made"), m.sem("scaled")
        block = ctx.enter_context(nc.Block())
        loads = [(K.w_nodeA[:, :], A["w_nodeA"]), (K.w_nodeB[:, :], A["w_nodeB"]),
                 (K.w_kvT[:, :, :], A["w_kvT"].rearrange("c p n -> p c n")),
                 (K.w_qT[:, :, :], A["w_qT"].rearrange("c p n -> p c n")),
                 (K.w_projT[:, :, :], A["w_projT"].rearrange("c p n -> p c n")),
                 (K.w_e1[:, :], A["w_e1"]), (K.w_e2[:, :], A["w_e2"]),
                 (K.w_lo0[:, :], A["w_lo0"]), (K.w_lo1[:, :], A["w_lo1"]),
                 (K.w_r[:, :, :], A["w_r"].rearrange("c p n -> p c n")),
                 (K.b_r[:, :], A["b_r"].to_broadcast([P, E])),
                 (K.b_proj[:, :], A["b_proj"].to_broadcast([P, D])),
                 (K.attr[:, :], A["attr"])]

        @block.sync
        def _(sp):
            for dst, src in loads:
                sp.dma_start(dst, src).then_inc(loaded, 16)
            sp.wait_ge(loaded, 16 * len(loads))

        @block.gpsimd
        def _(pool):
            g = nc.gpsimd
            g.memset(K.ones[:, :], 1.0).then_inc(made, 1)
            g.memset(K.zeros[:, :], 0.0).then_inc(made, 1)
            g.memset(K.minus_half[:, :], -0.5)
            g.memset(K.eps[:, :], EPS)
            pool.wait_ge(made, 2)
            g.affine_select(out=K.ident[:, :], in_=K.ones[:, :], compare_op=ALU.is_equal, fill=0.0, base=0,
                            pattern=[[-1, P]], channel_multiplier=1)
            g.affine_select(out=K.before[:, :], in_=K.ones[:, :], compare_op=ALU.is_gt, fill=0.0, base=0,
                            pattern=[[1, P]], channel_multiplier=-1)
            g.affine_select(out=K.upto[:, :], in_=K.ones[:, :], compare_op=ALU.is_ge, fill=0.0, base=0,
                            pattern=[[1, P]], channel_multiplier=-1)
            g.affine_select(out=K.valid_row[:, :], in_=K.ones[:, 0:NT], compare_op=ALU.is_ge, fill=0.0,
                            base=N_NODES - 1, pattern=[[-P, NT]], channel_multiplier=-1)
            g.affine_select(out=K.head_mask[:, :], in_=K.ones[:, :], compare_op=ALU.is_ge, fill=0.0, base=0,
                            pattern=[[-HD, P // HD], [0, HD]], channel_multiplier=1).then_inc(made, 1)
            pool.wait_ge(made, 3)
            g.affine_select(out=K.head_mask[:, :], in_=K.head_mask[:, :], compare_op=ALU.is_ge, fill=0.0,
                            base=HD - 1, pattern=[[HD, P // HD], [0, HD]], channel_multiplier=-1)
            g.iota(K.iota_f[:, :], [[1, P]], base=0, channel_multiplier=0, allow_small_or_imprecise_dtypes=True)
            g.iota(K.iota_b[:, :], [[1, P]], base=0, channel_multiplier=0, allow_small_or_imprecise_dtypes=True)

        @block.vector
        def _(dve):
            dve.wait_ge(loaded, 16 * len(loads))
            nc.vector.tensor_scalar(K.w_lo0[0:MUL, :], K.w_lo0[0:MUL, :], 1 / math.sqrt(3.0), None,
                                    ALU.mult).then_inc(scaled, 1)


def degrees(nc, A, K):
    U = 17
    NC = NG * GC
    NS = NC // U
    assert NS * U == NC
    with ExitStack() as ctx:
        m = Mem(nc, ctx, "deg")
        dst = m.sb("dst", [P, NC], i32); part = m.sb("part", [P, NC], i32)
        lo = m.sb("lo", [P, NC], bf16); hi = m.sb("hi", [P, NC], bf16)
        hot_lo = [m.sb(f"hot_lo{k}", [P, U, P], bf16) for k in range(2)]
        hot_hi = [m.sb(f"hot_hi{k}", [P, U, NB], bf16) for k in range(2)]
        deg = m.ps("deg")
        loaded, split, hot_ready, summed, scaled, rooted = (m.sem(x) for x in (
            "loaded", "split", "hot_ready", "summed", "scaled", "rooted"))
        block = ctx.enter_context(nc.Block())

        @block.sync
        def _(sp):
            sp.dma_start(dst[:, :], A["dst_cols"]).then_inc(loaded, 16)

        @block.vector
        def _(dve):
            v = nc.vector
            dve.wait_ge(loaded, 16)
            v.tensor_scalar(part[:, :], dst[:, :], P - 1, None, ALU.bitwise_and).then_inc(split, 1)
            dve.wait_ge(split, 1)
            v.tensor_copy(lo[:, :], part[:, :]).then_inc(split, 1)
            dve.wait_ge(split, 2)
            v.tensor_scalar(part[:, :], dst[:, :], 7, None, ALU.arith_shift_right).then_inc(split, 1)
            dve.wait_ge(split, 3)
            v.tensor_copy(hi[:, :], part[:, :]).then_inc(split, 1)
            dve.wait_ge(split, 4)

            def body(n, k):
                if not (isinstance(n, int) and n < 2):
                    dve.wait_ge(summed, n - 1)
                v.tensor_tensor(hot_lo[k][:, :, :], K.iota_b[:, :].unsqueeze(1).to_broadcast([P, U, P]),
                                lo[:, bass.ds(n * U, U)].unsqueeze(2).to_broadcast([P, U, P]),
                                ALU.is_equal)
                v.tensor_tensor(hot_hi[k][:, :, :], K.iota_b[:, 0:NB].unsqueeze(1).to_broadcast([P, U, NB]),
                                hi[:, bass.ds(n * U, U)].unsqueeze(2).to_broadcast([P, U, NB]),
                                ALU.is_equal).then_inc(hot_ready, 1)

            steps(dve, NS, 2, 2, body)
            dve.wait_ge(summed, NS)
            v.tensor_scalar(K.dis[:, :], deg[:, 0:NT], 1.0, None, ALU.max).then_inc(scaled, 1)
            dve.wait_ge(rooted, 1)
            v.scalar_tensor_tensor(K.sc_f[:, :], K.dis[:, :], 1 / 80.0, K.attr[:, :], ALU.mult, ALU.mult)
            v.scalar_tensor_tensor(K.sc_o[:, :], K.dis[:, :], C_X / math.sqrt(128.0), K.attr[:, :],
                                   ALU.mult, ALU.mult)
            v.tensor_scalar(K.sc_m[:, :], K.attr[:, :], C_S / 8.0, None, ALU.mult).then_inc(scaled, 1)

        @block.gpsimd
        def _(pool):
            pool.wait_ge(scaled, 1)
            nc.gpsimd.tensor_tensor(K.dis[:, :], K.dis[:, :], K.minus_half[:, 0:NT], ALU.pow).then_inc(rooted, 1)

        @block.tensor
        def _(pe):
            def body(n, k):
                pe.wait_ge(hot_ready, n + 1)
                for c in range(U):
                    first = isinstance(n, int) and n == 0 and c == 0
                    last = isinstance(n, int) and n == NS - 1 and c == U - 1
                    x = nc.tensor.matmul(deg[:, 0:NB], hot_lo[k][:, c, :], hot_hi[k][:, c, :],
                                         start=first, stop=last, skip_group_check=True)
                x.then_inc(summed, 1)

            steps(pe, NS, 2, 2, body)


def items(nc, A, K):
    with ExitStack() as ctx:
        m = Mem(nc, ctx, "items")
        dst = m.sb("dst", [P, 4, GE], i32)
        ends = m.sb("ends", [P, 2, 4], i32); endf = m.sb("endf", [P, 2, 4])
        count = m.sb("count", [P, 4]); start = m.sb("start", [P, 4]); end = m.sb("end", [P, 4])
        shift = m.sb("shift", [P, 4]); prefix = m.sb("prefix", [P, 4])
        group_id = m.sb("group_id", [P, 4]); real = m.sb("real", [P, 4])
        item = m.sb("item", [P, NI])
        begun = m.sb("begun", [P, 4, NI]); mine = m.sb("mine", [P, 4, NI])
        w_id = m.sb("w_id", [P, 4, P]); w_shift = m.sb("w_shift", [P, 4, P]); w_real = m.sb("w_real", [P, 4, P])
        row_b = m.sb("row_b", [P, NI])
        totals, p_id, p_shift, p_real = (m.ps(x) for x in ("totals", "id", "shift", "real"))
        loaded, iotas, d, summed = (m.sem(x) for x in ("loaded", "iotas", "vector_steps", "summed"))
        ready_at = {}
        block = ctx.enter_context(nc.Block())

        @block.sync
        def _(sp):
            sp.dma_start(dst[:, :, :], A["dst_rows"].rearrange("(g p) e -> p g e", p=P)).then_inc(loaded, 16)

        @block.gpsimd
        def _(pool):
            g = nc.gpsimd
            g.iota(group_id[:, :], [[P, 4]], base=0, channel_multiplier=1, allow_small_or_imprecise_dtypes=True)
            g.iota(item[:, :], [[1, NI]], base=0, channel_multiplier=0,
                   allow_small_or_imprecise_dtypes=True).then_inc(iotas, 1)

        @block.vector
        def _(dve):
            v, n = nc.vector, [0]

            def done(ins):
                n[0] += 1
                ins.then_inc(d, 1)
                dve.wait_ge(d, n[0])

            dve.wait_ge(loaded, 16)
            dve.wait_ge(iotas, 1)
            done(v.tensor_reduce(ends[:, 0, :], dst[:, :, :], AX.X, ALU.min))
            done(v.tensor_reduce(ends[:, 1, :], dst[:, :, :], AX.X, ALU.max))
            done(v.tensor_scalar(ends[:, :, :], ends[:, :, :], 7, None, ALU.arith_shift_right))
            done(v.tensor_copy(endf[:, :, :], ends[:, :, :]))
            done(v.scalar_tensor_tensor(count[:, :], endf[:, 1, :], 1.0, endf[:, 0, :], ALU.add, ALU.subtract))
            dve.wait_ge(summed, 1)
            done(v.tensor_copy(end[:, :], totals[:, 0:4]))
            done(v.tensor_copy(prefix[:, :], totals[:, 4:8]))
            for g in range(1, 4):
                for h in range(g):
                    done(v.tensor_tensor(end[:, g:g + 1], end[:, g:g + 1], prefix[:, h:h + 1], ALU.add))
            done(v.tensor_tensor(start[:, :], end[:, :], count[:, :], ALU.subtract))
            done(v.tensor_tensor(shift[:, :], endf[:, 0, :], start[:, :], ALU.subtract))
            done(v.tensor_scalar(real[:, :], group_id[:, :], float(NG), None, ALU.is_lt))
            for g in range(4):
                done(v.tensor_scalar(begun[:, g, :], item[:, :], start[:, g:g + 1], None, ALU.is_ge))
                done(v.tensor_scalar(mine[:, g, :], item[:, :], end[:, g:g + 1], None, ALU.is_lt))
                done(v.tensor_tensor(mine[:, g, :], mine[:, g, :], begun[:, g, :], ALU.mult))
                done(v.tensor_scalar(mine[:, g, :], mine[:, g, :], real[:, g:g + 1], None, ALU.mult))
                done(v.tensor_scalar(w_id[:, g, :], K.ones[:, :], group_id[:, g:g + 1], None, ALU.mult))
                done(v.tensor_scalar(w_shift[:, g, :], K.ones[:, :], shift[:, g:g + 1], None, ALU.mult))
                done(v.tensor_scalar(w_real[:, g, :], K.ones[:, :], real[:, g:g + 1], None, ALU.mult))
            ready_at["look-up"] = n[0]
            dve.wait_ge(summed, 2)
            done(v.tensor_copy(K.item_group[:, :], p_id[0:1, 0:NI]))
            done(v.scalar_tensor_tensor(row_b[:, :], p_shift[:, 0:NI], -float(NB), item[:, :], ALU.add, ALU.add))
            done(v.tensor_tensor(row_b[:, :], row_b[:, :], p_real[:, 0:NI], ALU.mult))
            done(v.tensor_scalar(row_b[:, :], row_b[:, :], float(NB), None, ALU.add))
            done(v.tensor_copy(K.item_block[:, :], row_b[0:1, :]))
            done(v.tensor_scalar(K.item_base[:, :], row_b[:, :], float(P), None, ALU.mult))

        @block.tensor
        def _(pe):
            pe.wait_ge(d, 5)
            nc.tensor.matmul(totals[:, 0:4], K.upto[:, :], count[:, :], start=True, stop=True)
            nc.tensor.matmul(totals[:, 4:8], K.ones[:, :], count[:, :], start=True, stop=True).then_inc(summed, 1)
            pe.wait_ge(d, ready_at["look-up"])
            for ps, w in ((p_id, w_id), (p_shift, w_shift), (p_real, w_real)):
                for g in range(4):
                    x = nc.tensor.matmul(ps[:, 0:NI], w[:, g, :], mine[:, g, :], start=g == 0, stop=g == 3)
            x.then_inc(summed, 1)


def nodes(nc, A, K):
    with ExitStack() as ctx:
        m = Mem(nc, ctx, "nodes")
        two = lambda name, shape: [m.sb(f"{name}{k}", shape) for k in range(2)]
        xs, xn, xnT, f_t, res, k_t, q_t = (two(x, [P, D]) for x in ("x", "xn", "xnT", "f", "res", "k", "q"))
        stats, mv, rstd = two("stats", [P, 6]), two("mv", [P, 2]), two("rstd", [P, 1])
        k_min, k_exp, q_min, q_exp = (two(x, [P, D]) for x in ("k_min", "k_exp", "q_min", "q_exp"))
        v_t = two("v", [P, 2, P + 1])
        ps_T, ps_f, ps_kv = ([m.ps(f"{x}{k}") for k in range(2)] for x in ("T", "f", "kv"))
        ps_q, ps_c = m.ps("q"), m.ps("ctx")
        c = {x: m.sem(x) for x in ("stats", "mean", "var", "rstd", "normed", "transposed", "xnT", "projected", "kv", "queries",
                                   "f", "res", "passed", "kmin", "qmin", "kexp", "qexp", "k", "q", "v", "context", "built")}
        x_in, f_out, res_out, q_out = ([m.sem(f"{x}{k}") for k in range(2)] for x in ("x_in", "f_out", "res_out", "q_out"))
        block = ctx.enter_context(nc.Block())
        old = lambda n: not (isinstance(n, int) and n < 2)

        @block.sync
        def _(sp):
            def body(n, k):
                if old(n):
                    sp.wait_ge(c["res"], n - 1)
                sp.dma_start(xs[k][:, :], A["x"][bass.ds(n, 1), :, :].rearrange("a p d -> (a p) d")
                             ).then_inc(x_in[k], 16)
            steps(sp, NT, 2, 2, body)

        @block.gpsimd
        def _(pool):
            def body(n, k):
                pool.wait_ge(c["mean"], n + 1)
                if old(n):
                    pool.wait_ge(c["normed"], n - 1)
                nc.gpsimd.tensor_tensor(rstd[k][:, :], mv[k][:, 1:2], K.eps[:, :], ALU.add).then_inc(c["var"], 1)
                pool.wait_ge(c["var"], n + 1)
                nc.gpsimd.tensor_tensor(rstd[k][:, :], rstd[k][:, :], K.minus_half[:, 0:1], ALU.pow).then_inc(c["rstd"], 1)
            steps(pool, NT, 2, 2, body)

        @block.vector
        def _(dve):
            v = nc.vector

            def body(n, k):
                dve.wait_ge(x_in[k], per(n, k))
                v.bn_stats(stats[k][:, :], xs[k][:, :]).then_inc(c["stats"], 1)
                wait_apart(dve, c["passed"], (c["stats"], n + 1))
                v.bn_aggr(mv[k][:, :], stats[k][:, :]).then_inc(c["mean"], 1)
                dve.wait_ge(c["rstd"], n + 1)
                if old(n):
                    dve.wait_ge(c["transposed"], n - 1)
                v.tensor_scalar(xn[k][:, :], xs[k][:, :], mv[k][:, 0:1], rstd[k][:, :], ALU.subtract,
                                ALU.mult).then_inc(c["normed"], 1)
                dve.wait_ge(c["projected"], n + 1)
                if old(n):
                    dve.wait_ge(f_out[k], per(n, k) - 16)
                pf = ps_f[k][:, :].rearrange("p (c h n) -> p c h n", c=2, h=2)
                v.tensor_scalar(f_t[k][:, :].rearrange("p (c n) -> p c n", c=2), pf[:, :, 0, :],
                                K.sc_f[:, bass.ds(n, 1)], None, ALU.mult).then_inc(c["f"], 1)
                if old(n):
                    dve.wait_ge(res_out[k], per(n, k) - 16)
                v.scalar_tensor_tensor(res[k][:, :].rearrange("p (c n) -> p c n", c=2), pf[:, :, 1, :],
                                       K.sc_m[:, bass.ds(n, 1)], xs[k][:, :].rearrange("p (c n) -> p c n", c=2),
                                       ALU.mult, ALU.add).then_inc(c["res"], 1)
                dve.wait_ge(c["kv"], n + 1)
                if old(n):
                    dve.wait_ge(c["kexp"], n - 1)
                v.tensor_scalar(k_min[k][:, :], ps_kv[k][:, 0:D], 0.0, None, ALU.min).then_inc(c["kmin"], 1)
                dve.wait_ge(c["queries"], n + 1)
                if old(n):
                    dve.wait_ge(c["qexp"], n - 1)
                v.tensor_scalar(q_min[k][:, :], ps_q[:, 0:D], 0.0, None, ALU.min).then_inc(c["qmin"], 1)
                if old(n):
                    dve.wait_ge(c["context"], n - 1)
                v.tensor_copy(v_t[k][:, :, 0:P], ps_kv[k][:, D:2 * D].rearrange("p (c n) -> p c n", c=2))
                v.tensor_copy(v_t[k][:, :, P:P + 1],
                              K.valid_row[:, bass.ds(n, 1)].unsqueeze(1).to_broadcast([P, 2, 1])).then_inc(c["v"], 1)
                dve.wait_ge(c["kexp"], n + 1)
                v.scalar_tensor_tensor(k_t[k][:, :], ps_kv[k][:, 0:D], 0.0, k_exp[k][:, :], ALU.max,
                                       ALU.add).then_inc(c["k"], 1)
                dve.wait_ge(c["qexp"], n + 1)
                if old(n):
                    dve.wait_ge(q_out[k], per(n, k) - 16)
                v.scalar_tensor_tensor(q_t[k][:, :], ps_q[:, 0:D], 0.0, q_exp[k][:, :], ALU.max,
                                       ALU.add).then_inc(c["q"], 1)

            steps(dve, NT, 2, 2, body)
            dve.wait_ge(c["context"], NT)
            pc = ps_c[:, 0:2 * (P + 1)].rearrange("p (c n) -> p c n", c=2)
            v.tensor_tensor(K.ctx_bd[:, :, :], pc[:, :, 0:P],
                            K.head_mask[:, :].unsqueeze(1).to_broadcast([P, 2, P]), ALU.mult)
            v.tensor_tensor(K.ksum_bd[:, :, :], pc[:, :, P:P + 1].to_broadcast([P, 2, P]),
                            K.head_mask[:, :].unsqueeze(1).to_broadcast([P, 2, P]), ALU.mult).then_inc(c["built"], 1)

        @block.scalar
        def _(act):
            def body(n, k):
                act.wait_ge(c["transposed"], n + 1)
                if old(n):
                    act.wait_ge(c["queries"], n - 1)
                nc.scalar.copy(xnT[k][:, :], ps_T[k][:, 0:D]).then_inc(c["xnT"], 1)
                act.wait_ge(c["kmin"], n + 1)
                if old(n):
                    act.wait_ge(c["k"], n - 1)
                nc.scalar.activation(k_exp[k][:, :], k_min[k][:, :], ACT.Exp).then_inc(c["kexp"], 1)
                act.wait_ge(c["qmin"], n + 1)
                if old(n):
                    act.wait_ge(c["q"], n - 1)
                nc.scalar.activation(q_exp[k][:, :], q_min[k][:, :], ACT.Exp).then_inc(c["qexp"], 1)
                act.wait_ge(c["f"], n + 1)
                one = lambda d, a="a p d -> (a p) d": d[bass.ds(n, 1), :, :].rearrange(a)
                act.dma_start(one(K.table_d), f_t[k][:, :]).then_inc(f_out[k], 16)
                act.wait_ge(c["res"], n + 1)
                act.dma_start(one(K.resid_d), res[k][:, :]).then_inc(res_out[k], 16)
                act.wait_ge(c["q"], n + 1)
                act.dma_start(one(K.qT_d), q_t[k][:, :]).then_inc(q_out[k], 16)

            steps(act, NT, 2, 2, body)
            for k in range(2):
                for out in (f_out, res_out, q_out):
                    act.wait_ge(out[k], 16 * ((NT + 1 - k) // 2))

        @block.tensor
        def _(pe):
            t = nc.tensor

            def context(n, k):
                pe.wait_ge(c["k"], n + 1)
                pe.wait_ge(c["v"], n + 1)
                first, last = (isinstance(n, int) and n == e for e in (0, NT - 1))
                for h in range(2):
                    x = t.matmul(ps_c[:, h * (P + 1):(h + 1) * (P + 1)], k_t[k][:, h * P:(h + 1) * P],
                                 v_t[k][:, h, :], start=first and h == 0, stop=last, skip_group_check=True)
                x.then_inc(c["context"], 1)

            def body(n, k):
                pe.wait_ge(c["normed"], n + 1)
                if old(n):
                    pe.wait_ge(c["xnT"], n - 1)
                for h in range(2):
                    x = t.transpose(ps_T[k][:, h * P:(h + 1) * P], xn[k][:, h * P:(h + 1) * P], K.ident[:, :])
                x.then_inc(c["transposed"], 1)
                pe.wait_ge(c["xnT"], n + 1)
                if old(n):
                    pe.wait_ge(c["res"], n - 1)
                xa, xb = xnT[k][:, 0:P], xnT[k][:, P:D]
                t.matmul(ps_f[k][:, 0:256], xa, K.w_nodeA[:, :], start=True, stop=True)
                t.matmul(ps_f[k][:, 256:512], xb, K.w_nodeB[:, :], start=True, stop=True).then_inc(c["projected"], 1)
                if old(n):
                    pe.wait_ge(c["k"], n - 1)
                t.matmul(ps_kv[k][:, :], xa, K.w_kvT[:, 0, :], start=True, stop=False)
                t.matmul(ps_kv[k][:, :], xb, K.w_kvT[:, 1, :], start=False, stop=True).then_inc(c["kv"], 1)
                if not (isinstance(n, int) and n == 0):
                    pe.wait_ge(c["q"], n)
                for o in range(2):
                    for h, xh in enumerate((xa, xb)):
                        x = t.matmul(ps_q[:, o * P:(o + 1) * P], K.w_qT[:, h, o * P:(o + 1) * P], xh,
                                     start=h == 0, stop=h == 1)
                x.then_inc(c["queries"], 1)
                context(n, k)

            steps(pe, NT, 2, 2, body)


def per(n, k, each=16, slots=2):
    if isinstance(n, int):
        return (n // slots + 1) * each
    if each % slots == 0:
        return (n - k + slots) * (each // slots)
    raise ValueError(each)


def edges(nc, A, K, acc):
    FREE = 4
    with ExitStack() as ctx:
        m = Mem(nc, ctx, "edges")
        four = lambda name, shape, dt=f32: [m.sb(f"{name}{k}", shape, dt) for k in range(4)]
        two = lambda name, shape, dt=f32: [m.sb(f"{name}{k}", shape, dt) for k in range(2)]
        el, src, dst = four("el", [BAS, GE]), four("src", [P, GC], i32), four("dst", [P, GC], i32)
        y, rows = four("y", [P, GC, 4]), four("rows", [P, GC, D])
        rel, hot, hT = two("rel", [P, GC]), two("hot", [P, GC, P]), two("hT", [HID, GE])
        dot3, dot2 = two("dot3", [P, GC, 3, MUL]), two("dot2", [P, GC, MUL])
        Z, msg = two("Z", [P, GC, 512]), two("msg", [P, GC, 512])
        ps_e = [m.ps(f"edge{k}", 2) for k in range(2)]
        ps_h, ps_s = ([m.ps(f"{x}{k}") for k in range(2)] for x in ("hidden", "sum"))
        loaded, gathered = ([m.sem(f"{x}{k}") for k in range(4)] for x in ("loaded", "gathered"))
        c = {x: m.sem(x) for x in ("cleared", "messages", "flushed", "hidden", "act", "weights", "factors", "rel",
                                   "dot3", "dot2", "dot", "hot", "summed", "zeroed", "passed")}
        block = ctx.enter_context(nc.Block())
        LD = 64

        @block.sync
        def _(sp):
            def body(n, k):
                sp.wait_ge(c["messages"], n + 1)
                t = sp.value_load(K.item_group[0:1, bass.ds(n, 1)], min_val=0, max_val=NG - 1)
                one = lambda a: a[bass.ds(t, 1), :, :].rearrange("a p n -> (a p) n")
                sp.dma_start(src[k][:, :], one(A["src"])).then_inc(loaded[k], 16)
                sp.dma_start(dst[k][:, :], one(A["dst"])).then_inc(loaded[k], 16)
                sp.dma_start(y[k][:, :, :].rearrange("p c n -> p (c n)"), one(A["y"])).then_inc(loaded[k], 16)
                sp.dma_start(el[k][:, :], one(A["el"])).then_inc(loaded[k], 16)
            steps(sp, NI, 4, 0, body)

        @block.gpsimd
        def _(pool):
            def body(n, k):
                wait_apart(pool, c["passed"], (c["messages"], n + 1), (loaded[k], per(n, k, LD, 4)))
                for j in range(GC):
                    nc.gpsimd.indirect_dma_start(
                        out=rows[k][:, j, :], out_offset=None, in_=K.table_d.rearrange("t p d -> (t p) d"),
                        in_offset=bass.IndirectOffsetOnAxis(ap=src[k][:, j:j + 1], axis=0),
                        bounds_check=N_PAD - 1, oob_is_err=False).then_inc(gathered[k], 16)
            steps(pool, NI, 4, 0, body)

        @block.scalar
        def _(act):
            def body(n, k):
                act.wait_ge(c["hidden"], n + 1)
                nc.scalar.activation(hT[k % 2][:, :], ps_h[k % 2][0:HID, :], ACT.Silu,
                                     scale=1 / math.sqrt(BAS)).then_inc(c["act"], 1)
                act.wait_ge(gathered[k], per(n, k, 64, 4))
                act.wait_ge(c["messages"], n + 3)
                z = Z[k % 2]
                for j in range(GC):
                    nc.scalar.activation(z[:, j, MUL:MUL + D], rows[k][:, j, :], ACT.Copy, scale=y[k][:, j, 0:1])
                    for i in range(3):
                        o = MUL + D + MUL * i
                        x = nc.scalar.activation(z[:, j, o:o + MUL], rows[k][:, j, 0:MUL], ACT.Copy,
                                                 scale=y[k][:, j, 1 + i:2 + i])
                x.then_inc(c["factors"], 1)
            act.dma_start(K.slot_d.rearrange("(p a) d -> p (a d)", p=P).rearrange("p (a n) -> p a n", n=512),
                          K.zeros[:, :].unsqueeze(1).to_broadcast([P, NSLOT * D // P // 512, 512])).then_inc(c["zeroed"], 16)
            steps(act, NI, 4, 0, body)
            act.wait_ge(c["zeroed"], 16)

        @block.vector
        def _(dve):
            v = nc.vector
            v.memset(acc[:, 0:(NB + 1) // 2, :], 0.0)
            v.memset(acc[:, (NB + 1) // 2:, :], 0.0).then_inc(c["cleared"], 1)
            dve.wait_ge(c["cleared"], 1)
            dve.sem_inc(c["messages"], FREE)
            dve.sem_inc(c["flushed"], 2)

            def flush(n, k):
                b = dve.value_load(K.item_block[0:1, bass.ds(n, 1)], min_val=0, max_val=NB)
                dve.wait_ge(c["flushed"], n + 2)
                dve.wait_ge(c["summed"], n + 1)
                a = acc[:, bass.ds(b, 1), :].rearrange("p a n -> p (a n)")
                v.tensor_tensor(a, a, ps_s[k % 2][:, :], ALU.add).then_inc(c["flushed"], 1)

            def body(n, k):
                h = k % 2
                dve.wait_ge(loaded[k], per(n, k, LD, 4))
                dve.wait_ge(c["hot"], n)
                v.tensor_scalar(rel[h][:, :], dst[k][:, :], K.item_base[:, bass.ds(n, 1)], None,
                                ALU.subtract).then_inc(c["rel"], 1)
                dve.wait_ge(c["rel"], n + 1)
                dve.wait_ge(c["flushed"], n + 1)
                v.tensor_tensor(hot[h][:, :, :], K.iota_f[:, :].unsqueeze(1).to_broadcast([P, GC, P]),
                                rel[h][:, :].unsqueeze(2).to_broadcast([P, GC, P]), ALU.is_equal).then_inc(c["hot"], 1)
                dve.wait_ge(gathered[k], per(n, k, 64, 4))
                dve.wait_ge(c["dot"], n)
                v.tensor_tensor(dot3[h][:, :, :, :], rows[k][:, :, MUL:D].rearrange("p c (i u) -> p c i u", i=3),
                                y[k][:, :, 1:4].unsqueeze(3).to_broadcast([P, GC, 3, MUL]),
                                ALU.mult).then_inc(c["dot3"], 1)
                dve.wait_ge(c["dot3"], n + 1)
                v.tensor_tensor(dot2[h][:, :, :], dot3[h][:, :, 0, :], dot3[h][:, :, 1, :],
                                ALU.add).then_inc(c["dot2"], 1)
                dve.wait_ge(c["dot2"], n + 1)
                dve.wait_ge(c["messages"], n + 3)
                v.tensor_tensor(Z[h][:, :, 0:MUL], dot2[h][:, :, :], dot3[h][:, :, 2, :], ALU.add).then_inc(c["dot"], 1)
                dve.wait_ge(c["dot"], n + 1)
                dve.wait_ge(c["factors"], n + 1)
                dve.wait_ge(c["weights"], n + 1)
                e = ps_e[h][:, :].rearrange("p (c n) -> p c n", c=GC)
                mg = msg[h][:, :, P:512].rearrange("p c (i d u) -> p c i d u", i=3, d=2)
                v.tensor_tensor(msg[h][:, :, 0:P], Z[h][:, :, 0:P], e[:, :, 0:P], ALU.mult)
                for d, o in ((0, P), (1, P + 3 * MUL)):
                    x = v.tensor_tensor(mg[:, :, :, d, :],
                                        Z[h][:, :, o:o + 3 * MUL].rearrange("p c (i u) -> p c i u", i=3),
                                        e[:, :, P + d * MUL:P + (d + 1) * MUL].unsqueeze(2).to_broadcast([P, GC, 3, MUL]),
                                        ALU.mult)
                x.then_inc(c["messages"], 1)

            def both(n, k):
                body(n, k)
                flush(n - 1, (k - 1) % 4)

            body(0, 0)
            steps_from(dve, 1, NI, 4, both)
            flush(NI - 1, (NI - 1) % 4)

        @block.tensor
        def _(pe):
            t = nc.tensor

            def hidden(n, k):
                pe.wait_ge(loaded[k], per(n, k, LD, 4))
                t.matmul(ps_h[k % 2][0:HID, :], K.w_e1[:, :], el[k][:, :], start=True, stop=True).then_inc(c["hidden"], 1)

            def weights(n, k):
                pe.wait_ge(c["messages"], n + 3)
                pe.wait_ge(c["act"], n + 1)
                for j in range(GC):
                    x = t.matmul(ps_e[k % 2][:, j * 256:(j + 1) * 256], hT[k % 2][:, j * P:(j + 1) * P],
                                 K.w_e2[:, :], start=True, stop=True)
                x.then_inc(c["weights"], 1)

            def sums(n, k):
                pe.wait_ge(c["flushed"], n + 1)
                pe.wait_ge(c["messages"], n + 1 + FREE)
                for j in range(GC):
                    x = t.matmul(ps_s[k % 2][:, :], hot[k % 2][:, j, :], msg[k % 2][:, j, :], start=j == 0, stop=j == GC - 1)
                x.then_inc(c["summed"], 1)

            def body(n, k):
                weights(n, k)
                hidden(n + 1, (k + 1) % 4)
                sums(n - 1, (k - 1) % 4)

            hidden(0, 0)
            weights(0, 0)
            hidden(1, 1)
            steps_from(pe, 1, NI - 1, 4, body)
            weights(NI - 1, (NI - 1) % 4)
            sums(NI - 2, (NI - 2) % 4)
            sums(NI - 1, (NI - 1) % 4)


def steps_from(eng, first, end, unroll, body):
    loops = (end - first) // unroll
    with eng.Fori(0, loops) as i:
        for j in range(unroll):
            body(i * unroll + (first + j), (first + j) % unroll)
    for n in range(first + loops * unroll, end):
        body(n, n % unroll)


def update(nc, A, K, acc):
    with ExitStack() as ctx:
        m = Mem(nc, ctx, "update")
        two = lambda name, shape, dt=f32: [m.sb(f"{name}{k}", shape, dt) for k in range(2)]
        resid, qT, mid, midT = two("resid", [P, D]), two("qT", [P, D]), two("mid", [P, 512]), two("midT", [P, 512])
        den, rec, attnT = two("den", [P, D]), two("rec", [P, D]), two("attnT", [P, D])
        base, part, x2, xt, xtT, tok = (two(x, [P, D]) for x in ("base", "part", "x2", "xt", "xtT", "tok"))
        stats, mv, rstd = two("stats", [P, 2, 6]), two("mv", [P, 2, 2]), two("rstd", [P, 2])
        lg, ex, top, low = two("lg", [P, E]), two("ex", [P, E]), two("top", [P, 2, 8]), two("low", [P, 4])
        idx, idxf = two("idx", [P, 8], mybir.dt.uint32), two("idxf", [P, TOP])
        ps_m, ps_a, ps_o, ps_x = ([m.ps(f"{x}{k}") for k in range(2)] for x in ("mid", "attn", "out", "x"))
        resid_in, q_in, x2_out, tok_out = ([m.sem(f"{x}{k}") for k in range(2)] for x in (
            "resid_in", "q_in", "x2_out", "tok_out"))
        c = {x: m.sem(x) for x in ("mid", "midT_ps", "midT", "attn", "den", "rec", "attnT", "out", "base", "part", "x2",
                                   "stats", "mean", "var", "rstd", "xt", "stats2", "mean2", "var2", "rstd2", "tok", "xtT_ps", "xtT",
                                   "logits", "lg", "lgmax", "negmax", "exp", "top", "idx", "idxf", "sum", "inv", "weight",
                                   "onehot", "passed")}
        block = ctx.enter_context(nc.Block())
        old = lambda n: not (isinstance(n, int) and n < 2)
        one = lambda d, n: d[bass.ds(n, 1), :, :].rearrange("a p d -> (a p) d")

        @block.sync
        def _(sp):
            def body(n, k):
                if old(n):
                    sp.wait_ge(c["base"], n - 1)
                sp.dma_start(resid[k][:, :], one(K.resid_d, n)).then_inc(resid_in[k], 16)
                if old(n):
                    sp.wait_ge(c["attn"], n - 1)
                sp.dma_start(qT[k][:, :], one(K.qT_d, n)).then_inc(q_in[k], 16)
            steps(sp, NT, 2, 2, body)

        @block.gpsimd
        def _(pool):
            def body(n, k):
                if old(n):
                    wait_apart(pool, c["passed"], (c["midT_ps"], n - 1))
                nc.gpsimd.tensor_copy(mid[k][:, :], acc[:, bass.ds(n, 1), :].rearrange("p a n -> p (a n)")
                                      ).then_inc(c["mid"], 1)
                if old(n):
                    pool.wait_ge(c["part"], n - 1)
                pool.wait_ge(resid_in[k], per(n, k))
                nc.gpsimd.tensor_tensor(base[k][:, :], resid[k][:, :], K.b_proj[:, :], ALU.add).then_inc(c["base"], 1)
                for i, (mean, var, r, o) in enumerate((("mean", "var", "rstd", "xt"), ("mean2", "var2", "rstd2", "tok"))):
                    pool.wait_ge(c[mean], n + 1)
                    if old(n):
                        pool.wait_ge(c[o], n - 1)
                    nc.gpsimd.tensor_tensor(rstd[k][:, i:i + 1], mv[k][:, i, 1:2], K.eps[:, :], ALU.add).then_inc(c[var], 1)
                    pool.wait_ge(c[var], n + 1)
                    nc.gpsimd.tensor_tensor(rstd[k][:, i:i + 1], rstd[k][:, i:i + 1], K.minus_half[:, 0:1],
                                            ALU.pow).then_inc(c[r], 1)
            steps(pool, NT, 2, 2, body)

        @block.tensor
        def _(pe):
            t = nc.tensor

            def body(n, k):
                pe.wait_ge(c["mid"], n + 1)
                if old(n):
                    pe.wait_ge(c["midT"], n - 1)
                for g in range(4):
                    x = t.transpose(ps_m[k][:, g * P:(g + 1) * P], mid[k][:, g * P:(g + 1) * P], K.ident[:, :])
                x.then_inc(c["midT_ps"], 1)
                pe.wait_ge(q_in[k], per(n, k))
                if old(n):
                    pe.wait_ge(c["attnT"], n - 1)
                for h in range(2):
                    t.matmul(ps_a[k][:, h * P:(h + 1) * P], K.ctx_bd[:, h, :], qT[k][:, h * P:(h + 1) * P],
                             start=True, stop=True)
                    x = t.matmul(ps_a[k][:, D + h * P:D + (h + 1) * P], K.ksum_bd[:, h, :], qT[k][:, h * P:(h + 1) * P],
                                 start=True, stop=True)
                x.then_inc(c["attn"], 1)
                pe.wait_ge(c["midT"], n + 1)
                if old(n):
                    pe.wait_ge(c["x2"], n - 1)
                for g in range(4):
                    t.matmul(ps_o[k][:, g * MUL:(g + 1) * MUL], midT[k][:, g * P:(g + 1) * P],
                             (K.w_lo0 if g == 0 else K.w_lo1)[:, :], start=True, stop=True)
                pe.wait_ge(c["attnT"], n + 1)
                for h in range(2):
                    x = t.matmul(ps_o[k][:, D:2 * D], attnT[k][:, h * P:(h + 1) * P], K.w_projT[:, h, :],
                                 start=h == 0, stop=h == 1)
                x.then_inc(c["out"], 1)
                pe.wait_ge(c["xt"], n + 1)
                if old(n):
                    pe.wait_ge(c["lg"], n - 1)
                for h in range(2):
                    x = t.transpose(ps_x[k][:, h * P:(h + 1) * P], xt[k][:, h * P:(h + 1) * P], K.ident[:, :])
                x.then_inc(c["xtT_ps"], 1)
                pe.wait_ge(c["xtT"], n + 1)
                for h in range(2):
                    x = t.matmul(ps_x[k][:, D:D + E], xtT[k][:, h * P:(h + 1) * P], K.w_r[:, h, :],
                                 start=h == 0, stop=h == 1)
                x.then_inc(c["logits"], 1)
            steps(pe, NT, 2, 2, body)

        @block.scalar
        def _(act):
            def body(n, k):
                act.wait_ge(c["midT_ps"], n + 1)
                if old(n):
                    act.wait_ge(c["out"], n - 1)
                nc.scalar.copy(midT[k][:, :], ps_m[k][:, :]).then_inc(c["midT"], 1)
                act.wait_ge(c["xtT_ps"], n + 1)
                if old(n):
                    act.wait_ge(c["logits"], n - 1)
                nc.scalar.copy(xtT[k][:, :], ps_x[k][:, 0:D]).then_inc(c["xtT"], 1)
                act.wait_ge(c["negmax"], n + 1)
                if old(n):
                    act.wait_ge(c["idx"], n - 1)
                nc.scalar.activation(ex[k][:, :], lg[k][:, :], ACT.Exp, bias=low[k][:, 0:1]).then_inc(c["exp"], 1)
                act.wait_ge(c["x2"], n + 1)
                act.dma_start(one(K.x2_d, n), x2[k][:, :]).then_inc(x2_out[k], 16)
                act.wait_ge(c["tok"], n + 1)
                act.dma_start(one(K.tok_d, n), tok[k][:, :]).then_inc(tok_out[k], 16)
            steps(act, NT, 2, 2, body)
            for k in range(2):
                for o in (x2_out, tok_out):
                    act.wait_ge(o[k], 16 * ((NT + 1 - k) // 2))

        @block.vector
        def _(dve):
            v = nc.vector

            def norm(n, k, i, x, o, names):
                st, mean, r, done = (c[z] for z in names)
                v.bn_stats(stats[k][:, i, :], x).then_inc(st, 1)
                wait_apart(dve, c["passed"], (st, n + 1))
                v.bn_aggr(mv[k][:, i, :], stats[k][:, i, :]).then_inc(mean, 1)
                dve.wait_ge(r, n + 1)
                v.tensor_scalar(o, x, mv[k][:, i, 0:1], rstd[k][:, i:i + 1], ALU.subtract, ALU.mult).then_inc(done, 1)

            def body(n, k):
                dve.wait_ge(c["attn"], n + 1)
                if old(n):
                    dve.wait_ge(c["out"], n - 1)
                v.tensor_scalar(den[k][:, :], ps_a[k][:, D:2 * D], 1e-6, None, ALU.max).then_inc(c["den"], 1)
                dve.wait_ge(c["den"], n + 1)
                v.reciprocal(rec[k][:, :], den[k][:, :]).then_inc(c["rec"], 1)
                dve.wait_ge(c["rec"], n + 1)
                v.tensor_tensor(attnT[k][:, :], ps_a[k][:, 0:D], rec[k][:, :], ALU.mult).then_inc(c["attnT"], 1)
                dve.wait_ge(c["base"], n + 1)
                dve.wait_ge(c["out"], n + 1)
                v.scalar_tensor_tensor(part[k][:, :], ps_o[k][:, 0:D], K.sc_o[:, bass.ds(n, 1)], base[k][:, :],
                                       ALU.mult, ALU.add).then_inc(c["part"], 1)
                dve.wait_ge(c["part"], n + 1)
                if old(n):
                    dve.wait_ge(x2_out[k], per(n, k) - 16)
                v.tensor_tensor(x2[k][:, :], ps_o[k][:, D:2 * D], part[k][:, :], ALU.add).then_inc(c["x2"], 1)
                dve.wait_ge(c["x2"], n + 1)
                if old(n):
                    dve.wait_ge(c["tok"], n - 1)
                norm(n, k, 0, x2[k][:, :], xt[k][:, :], ("stats", "mean", "rstd", "xt"))
                dve.wait_ge(c["xt"], n + 1)
                if old(n):
                    dve.wait_ge(tok_out[k], per(n, k) - 16)
                norm(n, k, 1, xt[k][:, :], tok[k][:, :], ("stats2", "mean2", "rstd2", "tok"))
                dve.wait_ge(c["logits"], n + 1)
                v.tensor_tensor(lg[k][:, :], ps_x[k][:, D:D + E], K.b_r[:, :], ALU.add).then_inc(c["lg"], 1)
                wait_apart(dve, c["passed"], (c["lg"], n + 1))
                v.max(top[k][:, 0, :], lg[k][:, :]).then_inc(c["lgmax"], 1)
                dve.wait_ge(c["lgmax"], n + 1)
                v.tensor_scalar(low[k][:, 0:1], top[k][:, 0, 0:1], -1.0, None, ALU.mult).then_inc(c["negmax"], 1)
                wait_apart(dve, c["passed"], (c["exp"], n + 1))
                v.max(top[k][:, 1, :], ex[k][:, :]).then_inc(c["top"], 1)
                wait_apart(dve, c["passed"], (c["top"], n + 1))
                v.max_index(idx[k][:, :], top[k][:, 1, :], ex[k][:, :]).then_inc(c["idx"], 1)
                dve.wait_ge(c["idx"], n + 1)
                v.tensor_copy(idxf[k][:, :], idx[k][:, 0:TOP]).then_inc(c["idxf"], 1)
                v.tensor_tensor(low[k][:, 1:2], top[k][:, 1, 0:1], top[k][:, 1, 1:2], ALU.add).then_inc(c["sum"], 1)
                dve.wait_ge(c["sum"], n + 1)
                v.reciprocal(low[k][:, 2:3], low[k][:, 1:2]).then_inc(c["inv"], 1)
                dve.wait_ge(c["inv"], n + 1)
                v.tensor_scalar(K.weight[:, bass.ds(n, 1), :].rearrange("p a t -> p (a t)"), top[k][:, 1, 0:TOP],
                                low[k][:, 2:3], None, ALU.mult).then_inc(c["weight"], 1)
                v.tensor_tensor(K.onehot[:, bass.ds(n, 1), :, :].rearrange("p a t e -> p (a t) e"),
                                K.iota_f[:, 0:E].unsqueeze(1).to_broadcast([P, TOP, E]),
                                idxf[k][:, :].unsqueeze(2).to_broadcast([P, TOP, E]), ALU.is_equal).then_inc(c["onehot"], 1)
            steps(dve, NT, 2, 2, body)


def dispatch(nc, A, K):
    G = NT * TOP
    with ExitStack() as ctx:
        m = Mem(nc, ctx, "dispatch")
        tot, incl, place = (m.sb(x, [P, G, E]) for x in ("tot", "incl", "place"))
        nb_i = m.sb("nb_i", [P, E], i32)
        nb, b_end, first = (m.sb(x, [P, E]) for x in ("nb", "b_end", "first"))
        pos = m.sb("pos", [P, G])
        gone, which = m.sb("gone", [1, NSB, E]), m.sb("which", [1, NSB])
        tok = [m.sb(f"tok{k}", [P, D]) for k in range(2)]
        idx = [m.sb(f"idx{k}", [P, TOP], i32) for k in range(2)]
        ps_w, ps_t = m.ps("within", 2), m.ps("total", 2)
        d, summed, copied, passed = (m.sem(x) for x in ("vector_steps", "summed", "copied", "passed"))
        tok_in, sent = ([m.sem(f"{x}{k}") for k in range(2)] for x in ("tok_in", "sent"))
        half = G // 2
        done_at = {}
        block = ctx.enter_context(nc.Block())
        old = lambda n: not (isinstance(n, int) and n < 2)

        @block.tensor
        def _(pe):
            for w, ps in ((K.before, ps_w), (K.ones, ps_t)):
                for h in range(2):
                    rhs = K.onehot[:, :, :, :].rearrange("p n t e -> p (n t e)")[:, h * half * E:(h + 1) * half * E]
                    x = nc.tensor.matmul(ps[:, h * 512:h * 512 + half * E], w[:, :], rhs, start=True, stop=True)
            x.then_inc(summed, 1)

        @block.vector
        def _(dve):
            v, n = nc.vector, [0]

            def done(ins):
                n[0] += 1
                ins.then_inc(d, 1)
                dve.wait_ge(d, n[0])

            halves = lambda ps: ps[:, :].rearrange("p (h n) -> p h n", h=2)[:, :, 0:half * E]
            dve.wait_ge(summed, 1)
            done(v.tensor_copy(tot[:, :, :].rearrange("p (h g) e -> p h (g e)", h=2), halves(ps_t)))
            for e in range(E):
                done(v.tensor_tensor_scan(incl[:, :, e], K.ones[:, 0:G], tot[:, :, e], 0.0, ALU.mult, ALU.add))
            done(v.tensor_tensor(place[:, :, :], incl[:, :, :], tot[:, :, :], ALU.subtract))
            done(v.tensor_tensor(place[:, :, :].rearrange("p (h g) e -> p h (g e)", h=2),
                                 place[:, :, :].rearrange("p (h g) e -> p h (g e)", h=2), halves(ps_w), ALU.add))
            done(v.tensor_scalar(nb[:, :], incl[:, G - 1, :], float(SB - 1), None, ALU.add))
            done(v.tensor_copy(nb_i[:, :], nb[:, :]))
            done(v.tensor_scalar(nb_i[:, :], nb_i[:, :], SB.bit_length() - 1, None, ALU.arith_shift_right))
            done(v.tensor_copy(nb[:, :], nb_i[:, :]))
            done(v.tensor_tensor_scan(b_end[:, :], K.ones[:, 0:E], nb[:, :], 0.0, ALU.mult, ALU.add))
            done(v.tensor_tensor(first[:, :], b_end[:, :], nb[:, :], ALU.subtract))
            done(v.tensor_scalar(first[:, :], first[:, :], float(SB), None, ALU.mult))
            done(v.tensor_tensor(place[:, :, :], place[:, :, :], first[:, :].unsqueeze(1).to_broadcast([P, G, E]), ALU.add))
            done(v.tensor_tensor(place[:, :, :], place[:, :, :], K.onehot[:, :, :, :].rearrange("p n t e -> p (n t) e"),
                                 ALU.mult))
            done(v.tensor_reduce(pos[:, :], place[:, :, :], AX.X, ALU.add))
            done(v.tensor_copy(K.pos_i[:, :, :].rearrange("p n t -> p (n t)"), pos[:, :]))
            done_at["pos"] = n[0]
            done(v.tensor_tensor(gone[:, :, :], K.iota_f[0:1, 0:NSB].unsqueeze(2).to_broadcast([1, NSB, E]),
                                 b_end[0:1, :].unsqueeze(1).to_broadcast([1, NSB, E]), ALU.is_ge))
            done(v.tensor_reduce(which[:, :], gone[:, :, :], AX.X, ALU.add))
            done(v.tensor_scalar(which[:, :], which[:, :], float(E - 1), None, ALU.min))
            done(v.tensor_copy(K.block_expert[:, :], which[:, :]))

        @block.sync
        def _(sp):
            def body(n, k):
                if old(n):
                    sp.wait_ge(sent[k], 2 * (per(n, k) - 16))
                sp.dma_start(tok[k][:, :], K.tok_d[bass.ds(n, 1), :, :].rearrange("a p d -> (a p) d")).then_inc(tok_in[k], 16)
            steps(sp, NT, 2, 2, body)

        @block.gpsimd
        def _(pool):
            pool.wait_ge(d, done_at["pos"])

            def body(n, k):
                wait_apart(pool, passed, *([(sent[k], 2 * (per(n, k) - 16))] if old(n) else []), (tok_in[k], per(n, k)))
                nc.gpsimd.tensor_copy(idx[k][:, :], K.pos_i[:, bass.ds(n, 1), :].rearrange("p a t -> p (a t)")
                                      ).then_inc(copied, 1)
                wait_apart(pool, passed, (copied, n + 1))
                for t in range(TOP):
                    nc.gpsimd.indirect_dma_start(
                        out=K.slot_d, out_offset=bass.IndirectOffsetOnAxis(ap=idx[k][:, t:t + 1], axis=0),
                        in_=tok[k][:, :], in_offset=None, bounds_check=NSLOT - 1, oob_is_err=False).then_inc(sent[k], 16)
            steps(pool, NT, 2, 2, body)
            for k in range(2):
                pool.wait_ge(sent[k], 32 * ((NT + 1 - k) // 2))


def experts(nc, A, K):
    NH = H // P
    with ExitStack() as ctx:
        m = Mem(nc, ctx, "experts")
        two = lambda name, shape, dt=f32: [m.sb(f"{name}{k}", shape, dt) for k in range(2)]
        w1, w2 = two("w1", [P, 2, H]), two("w2", [P, NH, D])
        ec, b2 = two("constants", [P, 2 + 2 + NH]), two("b2", [P, D])
        xb, xT, hT, yb = two("x", [P, 2, D]), two("xT", [P, 2, SB]), two("hT", [P, NH, SB]), two("y", [P, 2, D])
        ps_x = [m.ps(f"x{k}") for k in range(2)]
        ps_h = [m.ps(f"h{k}") for k in range(4)]
        ps_y = [m.ps(f"y{k}") for k in range(2)]
        loaded, stored = ([m.sem(f"{x}{k}") for k in range(2)] for x in ("loaded", "stored"))
        c = {x: m.sem(x) for x in ("turned", "xT", "first", "gelu", "second", "y")}
        block = ctx.enter_context(nc.Block())
        old = lambda n: not (isinstance(n, int) and n < 2)
        rows = lambda d, n: d.rearrange("(b h p) d -> p b h d", h=2, p=P)[:, bass.ds(n, 1), :, :].rearrange(
            "p b h d -> p (b h) d")
        LD = 16 * 5

        @block.sync
        def _(sp):
            def body(n, k):
                if old(n):
                    sp.wait_ge(c["y"], n - 1)
                e = sp.value_load(K.block_expert[0:1, bass.ds(n, 1)], min_val=0, max_val=E - 1)
                one = lambda a: a[bass.ds(e, 1), :, :].rearrange("a p n -> (a p) n")
                sp.dma_start(xb[k][:, :, :], rows(K.slot_d, n)).then_inc(loaded[k], 16)
                sp.dma_start(ec[k][:, :], one(A["e_const"])).then_inc(loaded[k], 16)
                sp.dma_start(w1[k][:, :, :].rearrange("p c n -> p (c n)"), one(A["w1"])).then_inc(loaded[k], 16)
                sp.dma_start(b2[k][:, :], one(A["b2"]).to_broadcast([P, D])).then_inc(loaded[k], 16)
                sp.dma_start(w2[k][:, :, :].rearrange("p c n -> p (c n)"), one(A["w2"])).then_inc(loaded[k], 16)
            steps(sp, NSB, 2, 2, body)

        @block.tensor
        def _(pe):
            t = nc.tensor

            def turn(n, k):
                pe.wait_ge(loaded[k], per(n, k, LD))
                if old(n):
                    pe.wait_ge(c["xT"], n - 1)
                for h in range(2):
                    for s in range(2):
                        x = t.transpose(ps_x[k][:, h * SB + s * P:h * SB + (s + 1) * P], xb[k][:, s, h * P:(h + 1) * P],
                                        K.ident[:, :])
                x.then_inc(c["turned"], 1)

            def layers(n, k, more):
                pe.wait_ge(c["xT"], n + 1)
                for j in range(NH):
                    if not (isinstance(n, int) and n == 0 and j < 4):
                        pe.wait_ge(c["gelu"], n * NH + (j - 3))
                    for h in range(2):
                        x = t.matmul(ps_h[j % 4][:, 0:SB], w1[k][:, h, j * P:(j + 1) * P], xT[k][:, h, :],
                                     start=h == 0, stop=h == 1)
                    x.then_inc(c["first"], 1)
                if more:
                    turn(n + 1, 1 - k)
                if not (isinstance(n, int) and n == 0):
                    pe.wait_ge(c["y"], n)
                for j in range(NH):
                    pe.wait_ge(c["gelu"], n * NH + (j + 1))
                    for s in range(2):
                        x = t.matmul(ps_y[s][:, 0:D], hT[k][:, j, s * P:(s + 1) * P], w2[k][:, j, :],
                                     start=j == 0, stop=j == NH - 1)
                x.then_inc(c["second"], 1)

            turn(0, 0)
            steps(pe, NSB - 2, 2, 2, lambda n, k: layers(n, k, True))
            layers(NSB - 2, 0, True)
            layers(NSB - 1, 1, False)

        @block.scalar
        def _(act):
            def shift(n, k):
                act.wait_ge(c["turned"], n + 1)
                if old(n):
                    act.wait_ge(c["first"], (n - 1) * NH)
                for h in range(2):
                    x = nc.scalar.activation(xT[k][:, h, :], ps_x[k][:, h * SB:(h + 1) * SB], ACT.Identity,
                                             scale=ec[k][:, h:h + 1], bias=ec[k][:, 2 + h:3 + h])
                x.then_inc(c["xT"], 1)

            def gelu(n, k, more):
                if old(n):
                    act.wait_ge(c["second"], n - 1)
                for j in range(NH):
                    act.wait_ge(c["first"], n * NH + (j + 1))
                    nc.scalar.activation(hT[k][:, j, :], ps_h[j % 4][:, 0:SB], ACT.Gelu,
                                         bias=ec[k][:, 4 + j:5 + j]).then_inc(c["gelu"], 1)
                if more:
                    shift(n + 1, 1 - k)
                act.wait_ge(c["y"], n + 1)
                act.dma_start(rows(K.y_d, n), yb[k][:, :, :]).then_inc(stored[k], 16)

            shift(0, 0)
            steps(act, NSB - 2, 2, 2, lambda n, k: gelu(n, k, True))
            gelu(NSB - 2, 0, True)
            gelu(NSB - 1, 1, False)
            for k in range(2):
                act.wait_ge(stored[k], 16 * NSB // 2)

        @block.vector
        def _(dve):
            def body(n, k):
                dve.wait_ge(c["second"], n + 1)
                if old(n):
                    dve.wait_ge(stored[k], per(n, k) - 16)
                for s in range(2):
                    x = nc.vector.tensor_tensor(yb[k][:, s, :], ps_y[s][:, 0:D], b2[k][:, :], ALU.add)
                x.then_inc(c["y"], 1)
            steps(dve, NSB, 2, 2, body)


def combine(nc, A, K, out):
    with ExitStack() as ctx:
        m = Mem(nc, ctx, "combine")
        two = lambda name, shape, dt=f32: [m.sb(f"{name}{k}", shape, dt) for k in range(2)]
        idx, x2, part, res = two("idx", [P, TOP], i32), two("x2", [P, D]), two("part", [P, D]), two("res", [P, D])
        rows = [two(f"rows{t}_", [P, D]) for t in range(TOP)]
        x2_in, fetched, stored = ([m.sem(f"{x}{k}") for k in range(2)] for x in ("x2_in", "fetched", "stored"))
        copied, part_ready, ready, passed = (m.sem(x) for x in ("copied", "part", "ready", "passed"))
        block = ctx.enter_context(nc.Block())
        old = lambda n: not (isinstance(n, int) and n < 2)
        one = lambda d, n: d[bass.ds(n, 1), :, :].rearrange("a p d -> (a p) d")

        @block.sync
        def _(sp):
            def body(n, k):
                if old(n):
                    sp.wait_ge(ready, n - 1)
                sp.dma_start(x2[k][:, :], one(K.x2_d, n)).then_inc(x2_in[k], 16)
            steps(sp, NT, 2, 2, body)

        @block.gpsimd
        def _(pool):

            def body(n, k):
                if old(n):
                    wait_apart(pool, passed, (ready, n - 1))
                nc.gpsimd.tensor_copy(idx[k][:, :], K.pos_i[:, bass.ds(n, 1), :].rearrange("p a t -> p (a t)")
                                      ).then_inc(copied, 1)
                wait_apart(pool, passed, (copied, n + 1))
                for t in range(TOP):
                    nc.gpsimd.indirect_dma_start(
                        out=rows[t][k][:, :], out_offset=None, in_=K.y_d,
                        in_offset=bass.IndirectOffsetOnAxis(ap=idx[k][:, t:t + 1], axis=0),
                        bounds_check=NSLOT - 1, oob_is_err=False).then_inc(fetched[k], 16)
            steps(pool, NT, 2, 2, body)

        @block.vector
        def _(dve):
            def body(n, k):
                dve.wait_ge(x2_in[k], per(n, k))
                dve.wait_ge(fetched[k], 2 * per(n, k))
                w = lambda t: K.weight[:, bass.ds(n, 1), t:t + 1].rearrange("p a t -> p (a t)")
                v = nc.vector
                v.scalar_tensor_tensor(part[k][:, :], rows[0][k][:, :], w(0), x2[k][:, :], ALU.mult,
                                       ALU.add).then_inc(part_ready, 1)
                dve.wait_ge(part_ready, n + 1)
                if old(n):
                    dve.wait_ge(stored[k], per(n, k) - 16)
                v.scalar_tensor_tensor(res[k][:, :], rows[1][k][:, :], w(1), part[k][:, :], ALU.mult,
                                       ALU.add).then_inc(ready, 1)
            steps(dve, NT, 2, 2, body)

        @block.scalar
        def _(act):
            def body(n, k):
                act.wait_ge(ready, n + 1)
                act.dma_start(one(out, n), res[k][:, :]).then_inc(stored[k], 16)
            steps(act, NT, 2, 2, body)
            for k in range(2):
                act.wait_ge(stored[k], 16 * ((NT + 1 - k) // 2))


class Shared:
    pass


def program(nc, A, out):
    with ExitStack() as ctx:
        K = Shared()
        sb = Mem(nc, ctx, "k").sb
        dram = lambda name, shape: nc.dram_tensor(name, shape, f32, kind="Internal").ap()
        K.table_d, K.resid_d = dram("gather_table", (NT, P, D)), dram("residual", (NT, P, D))
        K.qT_d, K.x2_d, K.tok_d = (dram(x, (NT, P, D)) for x in ("queries_T", "x_mid", "expert_rows"))
        K.slot_d, K.y_d = dram("slot_rows", (NSLOT, D)), dram("slot_results", (NSLOT, D))
        K.ident, K.ones, K.iota_f, K.before, K.upto, K.head_mask = (
            sb(x, [P, P]) for x in ("ident", "ones", "iota_f", "before", "upto", "head_mask"))
        K.iota_b = sb("iota_b", [P, P], bf16)
        K.minus_half, K.eps = sb("minus_half", [P, NT]), sb("eps", [P, 1])
        K.zeros = sb("zeros", [P, 512])
        K.valid_row, K.attr, K.dis, K.sc_f, K.sc_m, K.sc_o = (
            sb(x, [P, NT]) for x in ("valid_row", "attr", "dis", "sc_f", "sc_m", "sc_o"))
        K.w_nodeA, K.w_nodeB = sb("w_nodeA", [P, 256]), sb("w_nodeB", [P, 256])
        K.w_kvT, K.w_qT, K.w_projT = sb("w_kvT", [P, 2, 512]), sb("w_qT", [P, 2, 256]), sb("w_projT", [P, 2, 256])
        K.w_e1, K.w_e2 = sb("w_e1", [BAS, HID]), sb("w_e2", [HID, 256])
        K.w_lo0, K.w_lo1 = sb("w_lo0", [P, MUL]), sb("w_lo1", [P, MUL])
        K.w_r, K.b_r, K.b_proj = sb("w_r", [P, 2, E]), sb("b_r", [P, E]), sb("b_proj", [P, D])
        K.item_group, K.item_block = sb("item_group", [1, NI], i32), sb("item_block", [1, NI], i32)
        K.item_base = sb("item_base", [P, NI])
        K.ctx_bd, K.ksum_bd = sb("ctx_bd", [P, 2, P]), sb("ksum_bd", [P, 2, P])
        K.weight, K.onehot = sb("weight", [P, NT, TOP]), sb("onehot", [P, NT, TOP, E])
        K.pos_i, K.block_expert = sb("pos_i", [P, NT, TOP], i32), sb("block_expert", [1, NSB], i32)
        setup(nc, A, K)
        degrees(nc, A, K)
        items(nc, A, K)
        nodes(nc, A, K)
        with ExitStack() as sums:
            acc = sums.enter_context(nc.sbuf_tensor("accumulators", [P, NB + 1, 512], f32))
            edges(nc, A, K, acc)
            update(nc, A, K, acc)
        dispatch(nc, A, K)
        experts(nc, A, K)
        combine(nc, A, K, out)


def kernel(x, src, dst, edge_attr_10, edge_attr_4, node_vec1, L0_gnn_W_li0, L0_gnn_W_li1, L0_gnn_W_lm0, L0_gnn_W_lm1,
           L0_gnn_W_mlp1, L0_gnn_W_mlp2, L0_gnn_W_lo0, L0_gnn_W_lo1, L0_mix_Wq, L0_mix_Wkv, L0_mix_Wproj, L0_mix_bproj,
           L0_ffn_Wr, L0_ffn_br, L0_ffn_ln_g, L0_ffn_ln_b, L0_ffn_W1, L0_ffn_b1, L0_ffn_W2, L0_ffn_b2):
    import numpy as np
    import concourse.bacc as bacc
    from concourse.bass_utils import run_bass_kernel_spmd

    perm = np.concatenate([np.arange(MUL)] + [MUL + 3 * np.arange(MUL) + i for i in range(3)])

    def rows(a, n, fill=0):
        a = np.asarray(a)
        pad = np.full((n - a.shape[0],) + a.shape[1:], fill, a.dtype)
        return np.concatenate([a, pad])

    def diag(a, b):
        z = np.zeros((MUL, MUL), np.asarray(a).dtype)
        return np.block([[np.asarray(a), z], [z, np.asarray(b)]])

    ne = NG * GE
    by_group = lambda a: a.reshape(NG, GC, P, -1).transpose(0, 2, 1, 3).reshape(NG, P, -1)
    dst_p = rows(dst, NGP * GE, N_PAD - 1)
    y = np.asarray(edge_attr_4)
    chunks = lambda w: np.asarray(w).reshape(2, P, -1)
    W_2 = np.asarray(L0_gnn_W_mlp2).reshape(HID, 4, MUL)[:, [1, 0, 3, 2]].reshape(HID, 256)
    swap = lambda w: np.asarray(w).reshape(2, MUL, MUL)[::-1].reshape(P, MUL)
    per_chunk = lambda a: np.asarray(a).reshape(E, -1, P).transpose(0, 2, 1)
    arrays = {
        "x": rows(np.asarray(x)[:, perm], N_PAD).reshape(NT, P, D),
        "attr": rows(node_vec1, N_PAD).reshape(NT, P).T,
        "src": by_group(rows(src, ne)),
        "dst": by_group(dst_p[:ne]),
        "dst_cols": dst_p[:ne].reshape(NG * GC, P).T,
        "dst_rows": dst_p.reshape(NGP, GE),
        "y": by_group(rows(y, ne)),
        "el": rows(edge_attr_10, ne).reshape(NG, GE, BAS).transpose(0, 2, 1),
        "w_e1": np.asarray(L0_gnn_W_mlp1), "w_e2": W_2,
        "w_nodeA": np.concatenate([diag(L0_gnn_W_li0, L0_gnn_W_li1), diag(L0_gnn_W_lm0, L0_gnn_W_lm1)], 1),
        "w_nodeB": np.concatenate([diag(L0_gnn_W_li1, L0_gnn_W_li1), diag(L0_gnn_W_lm1, L0_gnn_W_lm1)], 1),
        "w_lo0": swap(L0_gnn_W_lo0), "w_lo1": swap(L0_gnn_W_lo1),
        "w_kvT": chunks(np.asarray(L0_mix_Wkv)[:, perm].T), "w_qT": chunks(np.asarray(L0_mix_Wq)[:, perm].T),
        "w_projT": chunks(np.asarray(L0_mix_Wproj)[perm].T), "b_proj": np.asarray(L0_mix_bproj)[perm][None],
        "w_r": chunks(np.asarray(L0_ffn_Wr)[perm]), "b_r": np.asarray(L0_ffn_br)[None],
        "w1": np.asarray(L0_ffn_W1)[:, perm].reshape(E, 2, P, H).transpose(0, 2, 1, 3).reshape(E, P, 2 * H),
        "w2": np.asarray(L0_ffn_W2)[:, :, perm].reshape(E, H // P, P, D).transpose(0, 2, 1, 3).reshape(E, P, -1),
        "e_const": np.concatenate([per_chunk(np.asarray(L0_ffn_ln_g)[:, perm]), per_chunk(np.asarray(L0_ffn_ln_b)[:, perm]),
                                   per_chunk(L0_ffn_b1)], 2),
        "b2": np.asarray(L0_ffn_b2)[:, perm][:, None],
    }
    arrays = {f"in_{k}": np.ascontiguousarray(a) for k, a in arrays.items()}
    nc = bacc.Bacc("TRN2", target_bir_lowering=False, num_devices=1)
    A = {k[3:]: nc.dram_tensor(k, a.shape, mybir.dt.from_np(a.dtype), kind="ExternalInput").ap()
         for k, a in arrays.items()}
    out = nc.dram_tensor("out", (NT, P, D), f32, kind="ExternalOutput").ap()
    program(nc, A, out)
    got = run_bass_kernel_spmd(nc, [arrays], core_ids=[0]).results[0]["out"]
    result = np.empty((N_NODES, D), got.dtype)
    result[:, perm] = got.reshape(N_PAD, D)[:N_NODES]
    return result
```

```python
from contextlib import ExitStack
import math

import concourse.bass as bass
from concourse import mybir

P = 128
N_NODES, D, MUL = 6250, 256, 64
NT = -(-N_NODES // P)
N_PAD = NT * P
N_EDGES = 200000
GE, GC = 512, 4
NG = -(-N_EDGES // GE)
UC = 32
NC = NT * UC
NEL = 46
TC = 7
EC = NG * 10 * GE // P // NEL
NGP = 4 * P
NB = NT
NI = NG + NB
HID, BAS = 100, 10
HEADS, HD = 8, 32
E, H, TOP = 8, 1024, 2
SB = 256
NSB = (TOP * N_PAD + E * (SB - 1)) // SB
NSLOT = NSB * SB
EPS = 1e-5
C_S, C_X = math.sin(math.pi / 8), math.cos(math.pi / 8)

f32, f32r, bf16, i32 = mybir.dt.float32, mybir.dt.float32r, mybir.dt.bfloat16, mybir.dt.int32
ALU, ACT, AX = mybir.AluOpType, mybir.ActivationFunctionType, mybir.AxisListType


def steps(eng, count, unroll, head, body):
    loops = (count - head) // unroll
    for n in range(head):
        body(n, n % unroll)
    if loops:
        with eng.Fori(0, loops) as i:
            for j in range(unroll):
                body(i * unroll + (head + j), (head + j) % unroll)
    for n in range(head + loops * unroll, count):
        body(n, n % unroll)


def steps_from(eng, first, end, unroll, body):
    loops = (end - first) // unroll
    with eng.Fori(0, loops) as i:
        for j in range(unroll):
            body(i * unroll + (first + j), (first + j) % unroll)
    for n in range(first + loops * unroll, end):
        body(n, n % unroll)


def per(n, k, each=16, slots=2):
    if isinstance(n, int):
        return (n // slots + 1) * each
    if each % slots == 0:
        return (n - k + slots) * (each // slots)
    raise ValueError(each)


def wait_apart(eng, passed, *waits):
    for sem, v in waits:
        eng.wait_ge(sem, v)
    eng.sem_inc(passed, 1)


class Mem:

    def __init__(self, nc, ctx, prefix):
        self.nc, self.ctx, self.prefix = nc, ctx, prefix

    def sb(self, name, shape, dt=f32):
        return self.ctx.enter_context(self.nc.sbuf_tensor(f"{self.prefix}_{name}", shape, dt))

    def ps(self, name, banks=1):
        return self.ctx.enter_context(self.nc.psum_tensor(f"{self.prefix}_ps_{name}", [P, 512 * banks], f32))

    def sem(self, name):
        return self.nc.alloc_semaphore(f"{self.prefix}_{name}")


def setup(nc, A, K):
    with ExitStack() as ctx:
        m = Mem(nc, ctx, "setup")
        loaded, made, scaled = m.sem("loaded"), m.sem("made"), m.sem("scaled")
        w_hi, low_row, w_part = m.sb("w_hi", [3 * BAS, HID], f32r), m.sb("low_row", [3 * BAS, 1]), m.sb("w_part", [3 * BAS, HID])
        block = ctx.enter_context(nc.Block())
        loads = [(K.w_nodeA[:, :], A["w_nodeA"]), (K.w_nodeB[:, :], A["w_nodeB"]),
                 (K.w_kvT[:, :, :], A["w_kvT"].rearrange("c p n -> p c n")),
                 (K.w_qT[:, :, :], A["w_qT"].rearrange("c p n -> p c n")),
                 (K.w_projT[:, :, :], A["w_projT"].rearrange("c p n -> p c n")),
                 (K.w_e1[:, :], A["w_e1"]), (K.w_e2[:, :], A["w_e2"]),
                 (K.w_lo0[:, :], A["w_lo0"]), (K.w_lo1[:, :], A["w_lo1"]),
                 (K.w_r[:, :, :], A["w_r"].rearrange("c p n -> p c n")),
                 (K.b_r[:, :], A["b_r"].to_broadcast([P, E])),
                 (K.b_proj[:, :], A["b_proj"].to_broadcast([P, D])),
                 (K.attr[:, :], A["attr"])]

        @block.sync
        def _(sp):
            for dst, src in loads:
                sp.dma_start(dst, src).then_inc(loaded, 16)
            sp.wait_ge(loaded, 16 * len(loads))

        @block.gpsimd
        def _(pool):
            g = nc.gpsimd
            g.memset(K.ones[:, :], 1.0).then_inc(made, 1)
            g.memset(K.zeros[:, :], 0.0).then_inc(made, 1)
            g.memset(K.minus_half[:, :], -0.5)
            g.memset(K.eps[:, :], EPS)
            pool.wait_ge(made, 2)
            g.affine_select(out=K.ident[:, :], in_=K.ones[:, :], compare_op=ALU.is_equal, fill=0.0, base=0,
                            pattern=[[-1, P]], channel_multiplier=1)
            g.affine_select(out=K.before[:, :], in_=K.ones[:, :], compare_op=ALU.is_gt, fill=0.0, base=0,
                            pattern=[[1, P]], channel_multiplier=-1)
            g.affine_select(out=K.upto[:, :], in_=K.ones[:, :], compare_op=ALU.is_ge, fill=0.0, base=0,
                            pattern=[[1, P]], channel_multiplier=-1)
            g.affine_select(out=K.valid_row[:, :], in_=K.ones[:, 0:NT], compare_op=ALU.is_ge, fill=0.0,
                            base=N_NODES - 1, pattern=[[-P, NT]], channel_multiplier=-1)
            g.affine_select(out=low_row[:, :], in_=K.zeros[0:3 * BAS, 0:1], compare_op=ALU.is_gt, fill=-1.0,
                            base=2 * BAS, pattern=[[0, 1]], channel_multiplier=-1)
            g.affine_select(out=K.head_mask[:, :], in_=K.ones[:, :], compare_op=ALU.is_ge, fill=0.0, base=0,
                            pattern=[[-HD, P // HD], [0, HD]], channel_multiplier=1).then_inc(made, 1)
            pool.wait_ge(made, 3)
            g.affine_select(out=K.head_mask[:, :], in_=K.head_mask[:, :], compare_op=ALU.is_ge, fill=0.0,
                            base=HD - 1, pattern=[[HD, P // HD], [0, HD]], channel_multiplier=-1)
            g.iota(K.iota_f[:, :], [[1, P]], base=0, channel_multiplier=0, allow_small_or_imprecise_dtypes=True)

        @block.vector
        def _(dve):
            dve.wait_ge(loaded, 16 * len(loads))
            nc.vector.tensor_scalar(K.w_lo0[MUL:P, :], K.w_lo0[MUL:P, :], 1 / math.sqrt(3.0), None,
                                    ALU.mult).then_inc(scaled, 1)
            nc.vector.tensor_copy(w_hi[:, :], K.w_e1[:, :]).then_inc(scaled, 1)
            dve.wait_ge(scaled, 2)
            dve.wait_ge(made, 3)
            nc.vector.scalar_tensor_tensor(w_part[:, :], w_hi[:, :].bitcast(f32), low_row[:, :], K.w_e1[:, :], ALU.mult,
                                           ALU.add).then_inc(scaled, 1)
            dve.wait_ge(scaled, 3)
            nc.vector.tensor_copy(K.w_e1s[:, :], w_part[:, :]).then_inc(scaled, 1)


def items(nc, A, K):
    with ExitStack() as ctx:
        m = Mem(nc, ctx, "items")
        dst = m.sb("dst", [P, 4, GE], i32)
        ends = m.sb("ends", [P, 2, 4], i32); endf = m.sb("endf", [P, 2, 4])
        count = m.sb("count", [P, 4]); start = m.sb("start", [P, 4]); end = m.sb("end", [P, 4])
        shift = m.sb("shift", [P, 4]); prefix = m.sb("prefix", [P, 4])
        group_id = m.sb("group_id", [P, 4]); real = m.sb("real", [P, 4])
        item = m.sb("item", [P, NI])
        begun = m.sb("begun", [P, 4, NI]); mine = m.sb("mine", [P, 4, NI])
        w_id = m.sb("w_id", [P, 4, P]); w_shift = m.sb("w_shift", [P, 4, P]); w_real = m.sb("w_real", [P, 4, P])
        row_b = m.sb("row_b", [P, NI])
        totals, p_id, p_shift, p_real = (m.ps(x) for x in ("totals", "id", "shift", "real"))
        loaded, iotas, d, summed = (m.sem(x) for x in ("loaded", "iotas", "vector_steps", "summed"))
        ready_at = {}
        block = ctx.enter_context(nc.Block())

        @block.sync
        def _(sp):
            sp.dma_start(dst[:, :, :], A["dst_rows"].rearrange("(g p) e -> p g e", p=P)).then_inc(loaded, 16)

        @block.gpsimd
        def _(pool):
            g = nc.gpsimd
            g.iota(group_id[:, :], [[P, 4]], base=0, channel_multiplier=1, allow_small_or_imprecise_dtypes=True)
            g.iota(item[:, :], [[1, NI]], base=0, channel_multiplier=0,
                   allow_small_or_imprecise_dtypes=True).then_inc(iotas, 1)

        @block.vector
        def _(dve):
            v, n = nc.vector, [0]

            def done(ins):
                n[0] += 1
                ins.then_inc(d, 1)
                dve.wait_ge(d, n[0])

            dve.wait_ge(loaded, 16)
            dve.wait_ge(iotas, 1)
            done(v.tensor_reduce(ends[:, 0, :], dst[:, :, :], AX.X, ALU.min))
            done(v.tensor_reduce(ends[:, 1, :], dst[:, :, :], AX.X, ALU.max))
            done(v.tensor_scalar(ends[:, :, :], ends[:, :, :], 7, None, ALU.arith_shift_right))
            done(v.tensor_copy(endf[:, :, :], ends[:, :, :]))
            done(v.scalar_tensor_tensor(count[:, :], endf[:, 1, :], 1.0, endf[:, 0, :], ALU.add, ALU.subtract))
            dve.wait_ge(summed, 1)
            done(v.tensor_copy(end[:, :], totals[:, 0:4]))
            done(v.tensor_copy(prefix[:, :], totals[:, 4:8]))
            for g in range(1, 4):
                for h in range(g):
                    done(v.tensor_tensor(end[:, g:g + 1], end[:, g:g + 1], prefix[:, h:h + 1], ALU.add))
            done(v.tensor_tensor(start[:, :], end[:, :], count[:, :], ALU.subtract))
            done(v.tensor_tensor(shift[:, :], endf[:, 0, :], start[:, :], ALU.subtract))
            done(v.tensor_scalar(real[:, :], group_id[:, :], float(NG), None, ALU.is_lt))
            for g in range(4):
                done(v.tensor_scalar(begun[:, g, :], item[:, :], start[:, g:g + 1], None, ALU.is_ge))
                done(v.tensor_scalar(mine[:, g, :], item[:, :], end[:, g:g + 1], None, ALU.is_lt))
                done(v.tensor_tensor(mine[:, g, :], mine[:, g, :], begun[:, g, :], ALU.mult))
                done(v.tensor_scalar(mine[:, g, :], mine[:, g, :], real[:, g:g + 1], None, ALU.mult))
                done(v.tensor_scalar(w_id[:, g, :], K.ones[:, :], group_id[:, g:g + 1], None, ALU.mult))
                done(v.tensor_scalar(w_shift[:, g, :], K.ones[:, :], shift[:, g:g + 1], None, ALU.mult))
                done(v.tensor_scalar(w_real[:, g, :], K.ones[:, :], real[:, g:g + 1], None, ALU.mult))
            ready_at["look-up"] = n[0]
            dve.wait_ge(summed, 2)
            done(v.tensor_copy(K.item_group[:, :], p_id[0:1, 0:NI]))
            done(v.scalar_tensor_tensor(row_b[:, :], p_shift[:, 0:NI], -float(NB), item[:, :], ALU.add, ALU.add))
            done(v.tensor_tensor(row_b[:, :], row_b[:, :], p_real[:, 0:NI], ALU.mult))
            done(v.tensor_scalar(row_b[:, :], row_b[:, :], float(NB), None, ALU.add))
            done(v.tensor_copy(K.item_block[:, :], row_b[0:1, :]))
            done(v.tensor_scalar(K.item_base[:, :], row_b[:, :], float(P), None, ALU.mult))

        @block.tensor
        def _(pe):
            pe.wait_ge(d, 5)
            nc.tensor.matmul(totals[:, 0:4], K.upto[:, :], count[:, :], start=True, stop=True)
            nc.tensor.matmul(totals[:, 4:8], K.ones[:, :], count[:, :], start=True, stop=True).then_inc(summed, 1)
            pe.wait_ge(d, ready_at["look-up"])
            for ps, w in ((p_id, w_id), (p_shift, w_shift), (p_real, w_real)):
                for g in range(4):
                    x = nc.tensor.matmul(ps[:, 0:NI], w[:, g, :], mine[:, g, :], start=g == 0, stop=g == 3)
            x.then_inc(summed, 1)


def moments(dve, v, stepped, stats, mean, var, diff):
    (m0, s0), (m1, s1) = ((stats[:, :, 3 * h + 1], stats[:, :, 3 * h + 2]) for h in range(2))
    v.tensor_tensor(diff, m0, m1, ALU.subtract).then_inc(stepped, 1)
    v.tensor_tensor(mean, m0, m1, ALU.add).then_inc(stepped, 1)
    v.tensor_tensor(var, s0, s1, ALU.add).then_inc(stepped, 1)
    dve.wait_ge(stepped, 3)
    v.tensor_scalar(mean, mean, 0.5, None, ALU.mult).then_inc(stepped, 1)
    v.scalar_tensor_tensor(diff, diff, 0.25, diff, ALU.mult, ALU.mult).then_inc(stepped, 1)
    dve.wait_ge(stepped, 5)
    v.scalar_tensor_tensor(var, var, 1.0 / D, diff, ALU.mult, ALU.add).then_inc(stepped, 1)
    dve.wait_ge(stepped, MOMENT_STEPS)


MOMENT_STEPS = 6


def nodes(nc, A, K):
    with ExitStack() as ctx:
        m = Mem(nc, ctx, "nodes")
        two = lambda name, shape, dt=f32: [m.sb(f"{name}{k}", shape, dt) for k in range(2)]
        dst = m.sb("dst", [P, NC], i32)
        lo, hi = m.sb("lo", [P, NC], bf16), m.sb("hi", [P, NC], bf16)
        iota_r = m.sb("iota_r", [P, P, UC], bf16)
        hot_lo, hot_hi = two("hot_lo", [P, P, UC], bf16), two("hot_hi", [P, NB, UC], bf16)
        part = hot_lo[0][:, :, :].rearrange("p j c -> p (j c)").bitcast(i32)[:, 0:NC]
        x, f = K.x2, m.sb("f", [P, NT, D])
        stats, mean, var, diff = m.sb("stats", [P, NT, 6]), m.sb("mean", [P, NT]), m.sb("var", [P, NT]), m.sb("diff", [P, NT])
        rstd, shift = m.sb("rstd", [P, NT]), m.sb("shift", [P, NT])
        el, el_hi, el_lo = (two(z, [P, EC], t) for z, t in (("el", f32), ("el_hi", f32r), ("el_lo", f32r)))
        xn, xnT, res, k_t, q_t = (two(z, [P, D]) for z in ("xn", "xnT", "res", "k", "q"))
        k_low, k_high, q_low, q_high = (two(z, [P, D]) for z in ("k_low", "k_high", "q_low", "q_high"))
        m_t, v_t = two("m", [P, D]), two("v", [P, 2, P + 1])
        ps_q, sums = m.ps("q"), m.ps("sums")
        ps_c, deg = sums[:, 0:2 * (P + 1)], sums[:, 2 * (P + 1):2 * (P + 1) + NT]
        ps_T, ps_f, ps_kv = ([m.ps(f"{z}{k}") for k in range(2)] for z in ("T", "f", "kv"))
        c = {z: m.sem(z) for z in (
            "x_in", "dst_in", "split", "hot", "counted", "clamped", "dis", "scales", "stats", "moments", "b", "rstd",
            "shift", "var", "iota", "xn", "turned", "xnT", "fm", "kv", "queries", "fm_used", "k_parts", "q_parts",
            "exps", "v", "k", "q", "res", "context", "f_scaled", "f_out", "built", "el_hi", "el_lo")}
        el_in, el_out = ([m.sem(f"{z}{k}") for k in range(2)] for z in ("el_in", "el_out"))
        el_cols = lambda d, n: d.rearrange("g b e -> (g b e)").rearrange("(p n) -> p n", p=P)[:, bass.ds(n * EC, EC)]
        res_out, q_out = ([m.sem(f"{z}{k}") for k in range(2)] for z in ("res_out", "q_out"))
        block = ctx.enter_context(nc.Block())
        old = lambda n: not (isinstance(n, int) and n < 2)
        one = lambda d, n: d[bass.ds(n, 1), :, :].rearrange("a p d -> (a p) d")
        tile = lambda a, n: a[:, bass.ds(n, 1), :].rearrange("p a d -> p (a d)")

        @block.sync
        def _(sp):
            sp.dma_start(x[:, :, :], A["x"].rearrange("t p d -> p t d")).then_inc(c["x_in"], 16)
            sp.dma_start(dst[:, :], A["dst_cols"]).then_inc(c["dst_in"], 16)

            lengths_in = lambda n, k: sp.dma_start(el[k][:, :], el_cols(A["el"], n)).then_inc(el_in[k], 16)

            def body(n, k, split=True, more=True):
                sp.wait_ge(c["res"], n + 1)
                sp.dma_start(one(K.resid_d, n), res[k][:, :]).then_inc(res_out[k], 16)
                sp.wait_ge(c["q"], n + 1)
                sp.dma_start(one(K.qT_d, n), q_t[k][:, :]).then_inc(q_out[k], 16)
                if split:
                    sp.wait_ge(c["el_lo"], n + 1)
                    sp.dma_start(el_cols(K.el_hi_d, n), el_hi[k][:, :].bitcast(f32)).then_inc(el_out[k], 16)
                    sp.dma_start(el_cols(K.el_lo_d, n), el_lo[k][:, :].bitcast(f32)).then_inc(el_out[k], 16)
                if more:
                    lengths_in(n + 2, k)

            lengths_in(0, 0)
            lengths_in(1, 1)
            steps(sp, NEL - 2, 2, 2, body)
            for n in range(NEL - 2, NT):
                body(n, n % 2, n < NEL, False)
            for t in range(0, NT, TC):
                sp.wait_ge(c["f_scaled"], t // TC + 1)
                sp.dma_start(K.table_d[t:t + TC].rearrange("t p d -> p t d"), f[:, t:t + TC, :]).then_inc(c["f_out"], 16)
            sp.wait_ge(c["f_out"], 16 * (NT // TC))
            for k in range(2):
                for out in (res_out, q_out):
                    sp.wait_ge(out[k], 16 * ((NT + 1 - k) // 2))
                sp.wait_ge(el_out[k], 32 * ((NEL + 1 - k) // 2))

        @block.gpsimd
        def _(pool):
            g = nc.gpsimd
            g.iota(iota_r[:, :, :], [[1, P], [0, UC]], base=0, channel_multiplier=0,
                   allow_small_or_imprecise_dtypes=True).then_inc(c["iota"], 1)
            pool.wait_ge(c["moments"], MOMENT_STEPS)
            g.tensor_tensor(rstd[:, :], var[:, :], K.eps[:, :].to_broadcast([P, NT]), ALU.add).then_inc(c["var"], 1)
            pool.wait_ge(c["var"], 1)
            g.tensor_tensor(rstd[:, :], rstd[:, :], K.minus_half[:, :], ALU.pow).then_inc(c["rstd"], 1)

            def body(n, k):
                pool.wait_ge(c["fm_used"], n + 1)
                if old(n):
                    pool.wait_ge(res_out[k], per(n, k) - 16)
                g.tensor_tensor(res[k][:, :], m_t[k][:, :], tile(x, n), ALU.add).then_inc(c["b"], 1)
                pool.wait_ge(c["b"], n + 1)
                g.tensor_tensor(res[k][:, :], res[k][:, :], K.b_proj[:, :], ALU.add).then_inc(c["res"], 1)
                pool.wait_ge(c["exps"], n + 1)
                if old(n):
                    pool.wait_ge(c["context"], n - 1)
                g.tensor_tensor(k_t[k][:, :], k_high[k][:, :], k_low[k][:, :], ALU.add).then_inc(c["k"], 1)
                if old(n):
                    pool.wait_ge(q_out[k], per(n, k) - 16)
                g.tensor_tensor(q_t[k][:, :], q_high[k][:, :], q_low[k][:, :], ALU.add).then_inc(c["q"], 1)
            steps(pool, NT, 2, 2, body)
            pool.wait_ge(c["clamped"], 1)
            g.tensor_tensor(K.dis[:, :], K.dis[:, :], K.minus_half[:, :], ALU.pow).then_inc(c["dis"], 1)

        @block.vector
        def _(dve):
            v = nc.vector
            v.tensor_scalar(K.sc_m[:, :], K.attr[:, :], C_S / 8.0, None, ALU.mult).then_inc(c["scales"], 1)
            dve.wait_ge(c["x_in"], 16)

            def norms(n, k):
                v.bn_stats(tile(stats, n), tile(x, n)).then_inc(c["stats"], 1)
            steps(dve, NT, 7, 0, norms)
            dve.wait_ge(c["stats"], NT)
            moments(dve, v, c["moments"], stats, mean[:, :], var[:, :], diff[:, :])
            dve.wait_ge(c["rstd"], 1)
            v.scalar_tensor_tensor(shift[:, :], mean[:, :], -1.0, rstd[:, :], ALU.mult, ALU.mult).then_inc(c["shift"], 1)
            dve.wait_ge(c["dst_in"], 16)
            v.tensor_scalar(part, dst[:, :], P - 1, None, ALU.bitwise_and).then_inc(c["split"], 1)
            dve.wait_ge(c["split"], 1)
            v.tensor_copy(lo[:, :], part).then_inc(c["split"], 1)
            dve.wait_ge(c["split"], 2)
            v.tensor_scalar(part, dst[:, :], 7, None, ALU.arith_shift_right).then_inc(c["split"], 1)
            dve.wait_ge(c["split"], 3)
            v.tensor_copy(hi[:, :], part).then_inc(c["split"], 1)
            dve.wait_ge(c["iota"], 1)
            dve.wait_ge(c["split"], 4)

            def hots(n, k):
                if old(n):
                    dve.wait_ge(c["counted"], n - 1)
                cols = lambda a, w: a[:, bass.ds(n * UC, UC)].unsqueeze(1).to_broadcast([P, w, UC])
                v.tensor_tensor(hot_lo[k][:, :, :], iota_r[:, :, :], cols(lo, P), ALU.is_equal)
                v.tensor_tensor(hot_hi[k][:, :, :], iota_r[:, 0:NB, :], cols(hi, NB), ALU.is_equal).then_inc(c["hot"], 1)
            def lengths(n, k):
                dve.wait_ge(el_in[k], per(n, k))
                if old(n):
                    dve.wait_ge(el_out[k], 2 * (per(n, k) - 16))
                v.tensor_copy(el_hi[k][:, :], el[k][:, :]).then_inc(c["el_hi"], 1)
                dve.wait_ge(c["el_hi"], n + 1)
                v.tensor_tensor(el_lo[k][:, :], el[k][:, :], el_hi[k][:, :].bitcast(f32), ALU.subtract).then_inc(c["el_lo"], 1)

            def both(n, k):
                hots(n, k)
                lengths(n, k)
            steps(dve, NEL, 2, 2, both)
            for n in range(NEL, NT):
                hots(n, n % 2)
            dve.wait_ge(c["context"], NT)
            v.tensor_scalar(K.dis[:, :], deg, 1.0, None, ALU.max).then_inc(c["clamped"], 1)
            dve.wait_ge(c["dis"], 1)
            v.scalar_tensor_tensor(K.sc_f[:, :], K.dis[:, :], 1 / 80.0, K.attr[:, :], ALU.mult, ALU.mult)
            v.scalar_tensor_tensor(K.sc_o[:, :], K.dis[:, :], C_X / math.sqrt(128.0), K.attr[:, :],
                                   ALU.mult, ALU.mult).then_inc(c["scales"], 1)
            dve.wait_ge(c["scales"], 2)
            dve.wait_ge(c["fm_used"], NT)

            for t in range(0, NT, TC):
                v.tensor_tensor(f[:, t:t + TC, :], f[:, t:t + TC, :],
                                K.sc_f[:, t:t + TC].unsqueeze(2).to_broadcast([P, TC, D]), ALU.mult).then_inc(c["f_scaled"], 1)
            pc = ps_c.rearrange("p (c n) -> p c n", c=2)
            heads = K.head_mask[:, :].unsqueeze(1).to_broadcast([P, 2, P])
            v.tensor_tensor(K.ctx_bd[:, :, :], pc[:, :, 0:P], heads, ALU.mult)
            v.tensor_tensor(K.ksum_bd[:, :, :], pc[:, :, P:P + 1].to_broadcast([P, 2, P]), heads, ALU.mult).then_inc(c["built"], 1)

        @block.scalar
        def _(act):
            a = nc.scalar

            def normed(n, k):
                if old(n):
                    act.wait_ge(c["turned"], n - 1)
                a.activation(xn[k][:, :], tile(x, n), ACT.Identity, scale=rstd[:, bass.ds(n, 1)],
                             bias=shift[:, bass.ds(n, 1)]).then_inc(c["xn"], 1)

            def turned(n, k):
                act.wait_ge(c["turned"], n + 1)
                if old(n):
                    act.wait_ge(c["queries"], n - 1)
                a.copy(xnT[k][:, :], ps_T[k][:, 0:D]).then_inc(c["xnT"], 1)

            def emptied(n, k):
                act.wait_ge(c["fm"], n + 1)
                pf = ps_f[k][:, :].rearrange("p (c h n) -> p c h n", c=2, h=2)
                a.copy(tile(f, n).rearrange("p (c n) -> p c n", c=2), pf[:, :, 0, :])
                if old(n):
                    act.wait_ge(c["res"], n - 1)
                a.activation(m_t[k][:, :].rearrange("p (c n) -> p c n", c=2), pf[:, :, 1, :], ACT.Identity,
                             scale=K.sc_m[:, bass.ds(n, 1)]).then_inc(c["fm_used"], 1)
                act.wait_ge(c["kv"], n + 1)
                if old(n):
                    act.wait_ge(c["q"], n - 1)
                    act.wait_ge(c["context"], n - 1)
                a.activation(k_low[k][:, :], ps_kv[k][:, 0:D], ACT.Relu, scale=-1.0).then_inc(c["k_parts"], 1)
                a.activation(k_high[k][:, :], ps_kv[k][:, 0:D], ACT.Relu)
                a.copy(v_t[k][:, :, 0:P], ps_kv[k][:, D:2 * D].rearrange("p (c n) -> p c n", c=2))
                a.copy(v_t[k][:, :, P:P + 1],
                       K.valid_row[:, bass.ds(n, 1)].unsqueeze(1).to_broadcast([P, 2, 1])).then_inc(c["v"], 1)
                act.wait_ge(c["queries"], n + 1)
                a.activation(q_low[k][:, :], ps_q[:, 0:D], ACT.Relu, scale=-1.0)
                a.activation(q_high[k][:, :], ps_q[:, 0:D], ACT.Relu).then_inc(c["q_parts"], 1)
                act.wait_ge(c["k_parts"], n + 1)
                a.activation(k_low[k][:, :], k_low[k][:, :], ACT.Exp, scale=-1.0)
                act.wait_ge(c["q_parts"], n + 1)
                a.activation(q_low[k][:, :], q_low[k][:, :], ACT.Exp, scale=-1.0).then_inc(c["exps"], 1)

            def body(n, k):
                turned(n + 1, 1 - k)
                normed(n + 2, k)
                emptied(n, k)

            act.wait_ge(c["shift"], 1)
            act.wait_ge(c["scales"], 1)
            normed(0, 0)
            normed(1, 1)
            turned(0, 0)
            steps(act, NT - 2, 2, 2, body)
            turned(NT - 1, (NT - 1) % 2)
            emptied(NT - 2, NT % 2)
            emptied(NT - 1, (NT - 1) % 2)

        @block.tensor
        def _(pe):
            t = nc.tensor

            def turn(n, k):
                pe.wait_ge(c["xn"], n + 1)
                if old(n):
                    pe.wait_ge(c["xnT"], n - 1)
                for h in range(2):
                    z = t.transpose(ps_T[k][:, h * P:(h + 1) * P], xn[k][:, h * P:(h + 1) * P], K.ident[:, :])
                z.then_inc(c["turned"], 1)

            def project(n, k):
                pe.wait_ge(c["xnT"], n + 1)
                if old(n):
                    pe.wait_ge(c["exps"], n - 1)
                xa, xb = xnT[k][:, 0:P], xnT[k][:, P:D]
                t.matmul(ps_f[k][:, 0:256], xa, K.w_nodeA[:, :], start=True, stop=True)
                t.matmul(ps_f[k][:, 256:512], xb, K.w_nodeB[:, :], start=True, stop=True).then_inc(c["fm"], 1)
                t.matmul(ps_kv[k][:, :], xa, K.w_kvT[:, 0, :], start=True, stop=False)
                t.matmul(ps_kv[k][:, :], xb, K.w_kvT[:, 1, :], start=False, stop=True).then_inc(c["kv"], 1)
                if not (isinstance(n, int) and n == 0):
                    pe.wait_ge(c["q_parts"], n)
                for o in range(2):
                    for h, xh in enumerate((xa, xb)):
                        z = t.matmul(ps_q[:, o * P:(o + 1) * P], K.w_qT[:, h, o * P:(o + 1) * P], xh,
                                     start=h == 0, stop=h == 1)
                z.then_inc(c["queries"], 1)

            def context(n, k):
                pe.wait_ge(c["k"], n + 1)
                pe.wait_ge(c["v"], n + 1)
                last = isinstance(n, int) and n == NT - 1
                for h in range(2):
                    z = t.matmul(ps_c[:, h * (P + 1):(h + 1) * (P + 1)], k_t[k][:, h * P:(h + 1) * P],
                                 v_t[k][:, h, :], start=False, stop=last, skip_group_check=True)
                z.then_inc(c["context"], 1)

            def count(n, k):
                pe.wait_ge(c["hot"], n + 1)
                first, last = (isinstance(n, int) and n == e for e in (0, NT - 1))
                for j in range(UC):
                    z = t.matmul(deg, hot_lo[k][:, :, j], hot_hi[k][:, :, j], start=first and j == 0,
                                 stop=last and j == UC - 1, skip_group_check=True)
                z.then_inc(c["counted"], 1)

            def body(n, k):
                turn(n + 1, 1 - k)
                project(n, k)
                context(n - 1, 1 - k)
                count(n, k)

            turn(0, 0)
            turn(1, 1)
            project(0, 0)
            count(0, 0)
            body(1, 1)
            steps_from(pe, 2, NT - 1, 2, body)
            project(NT - 1, (NT - 1) % 2)
            context(NT - 2, NT % 2)
            count(NT - 1, (NT - 1) % 2)
            context(NT - 1, (NT - 1) % 2)


def edges(nc, A, K, acc):
    FREE = 4
    with ExitStack() as ctx:
        m = Mem(nc, ctx, "edges")
        four = lambda name, shape, dt=f32: [m.sb(f"{name}{k}", shape, dt) for k in range(4)]
        two = lambda name, shape, dt=f32: [m.sb(f"{name}{k}", shape, dt) for k in range(2)]
        el, src, dst = four("el", [3 * BAS, GE], f32r), four("src", [P, GC], i32), four("dst", [P, GC], i32)
        y = four("y", [P, GC, 4])
        rel, hT = two("rel", [P, GC]), two("hT", [HID, GE])
        hot, hot_y = two("hot", [P, GC, P]), two("hot_y", [P, GC, P])
        warm = m.sb("warm", [P, 1])
        room = K.x2[:, :, :].rearrange("p t d -> p (t d)")
        cut = lambda at, n: room[:, at * GC * D:(at + n) * GC * D].rearrange("p (c n) -> p c n", c=GC)
        rows, Z, msg = [cut(k, 1) for k in range(4)], [cut(4 + k, 1) for k in range(2)], [cut(6 + 2 * k, 2) for k in range(2)]
        dot3 = [cut(10 + k, 1)[:, :, 0:3 * MUL].rearrange("p c (i u) -> p c i u", i=3) for k in range(2)]
        dot2 = [cut(10 + k, 1)[:, :, 3 * MUL:] for k in range(2)]
        ps_e = [m.ps(f"edge{k}", 2) for k in range(2)]
        ps_h, ps_s = ([m.ps(f"{x}{k}") for k in range(2)] for x in ("hidden", "sum"))
        loaded, gathered = ([m.sem(f"{x}{k}") for k in range(4)] for x in ("loaded", "gathered"))
        c = {x: m.sem(x) for x in ("cleared", "messages", "flushed", "hidden", "act", "weights", "factors", "rel", "hot_y",
                                   "dot3", "dot2", "dot", "hot", "summed", "zeroed", "passed")}
        block = ctx.enter_context(nc.Block())
        LD = 16 * 6

        @block.sync
        def _(sp):
            def body(n, k):
                sp.wait_ge(c["messages"], n + 1)
                sp.wait_ge(c["hot_y"], n + 1)
                t = sp.value_load(K.item_group[0:1, bass.ds(n, 1)], min_val=0, max_val=NG - 1)
                one = lambda a: a[bass.ds(t, 1), :, :].rearrange("a p n -> (a p) n")
                sp.dma_start(src[k][:, :], one(A["src"])).then_inc(loaded[k], 16)
                sp.dma_start(dst[k][:, :], one(A["dst"])).then_inc(loaded[k], 16)
                sp.dma_start(y[k][:, :, :].rearrange("p c n -> p (c n)"), one(A["y"])).then_inc(loaded[k], 16)
                for i, part in enumerate((K.el_hi_d, K.el_lo_d, K.el_hi_d)):
                    sp.dma_start(el[k][i * BAS:(i + 1) * BAS, :].bitcast(f32), one(part)).then_inc(loaded[k], 16)
            steps(sp, NI, 4, 0, body)

        @block.gpsimd
        def _(pool):
            def body(n, k):
                wait_apart(pool, c["passed"], (c["messages"], n + 1), (loaded[k], per(n, k, LD, 4)))
                for j in range(GC):
                    nc.gpsimd.indirect_dma_start(
                        out=rows[k][:, j, :], out_offset=None, in_=K.table_d.rearrange("t p d -> (t p) d"),
                        in_offset=bass.IndirectOffsetOnAxis(ap=src[k][:, j:j + 1], axis=0),
                        bounds_check=N_PAD - 1, oob_is_err=False).then_inc(gathered[k], 16)
            steps(pool, NI, 4, 0, body)

        @block.scalar
        def _(act):
            def body(n, k):
                act.wait_ge(c["hidden"], n + 1)
                nc.scalar.activation(hT[k % 2][:, :], ps_h[k % 2][0:HID, :], ACT.Silu,
                                     scale=1 / math.sqrt(BAS)).then_inc(c["act"], 1)
                act.wait_ge(gathered[k], per(n, k, 64, 4))
                act.wait_ge(c["messages"], n + 3)
                for j in range(GC):
                    for i in range(3):
                        x = nc.scalar.activation(Z[k % 2][:, j, MUL * (i + 1):MUL * (i + 2)], rows[k][:, j, 0:MUL],
                                                 ACT.Identity, scale=y[k][:, j, 1 + i:2 + i])
                x.then_inc(c["factors"], 1)
                act.wait_ge(c["hot"], n + 1)
                act.wait_ge(c["flushed"], n + 1)
                for j in range(GC):
                    x = nc.scalar.activation(hot_y[k % 2][:, j, :], hot[k % 2][:, j, :], ACT.Identity, scale=y[k][:, j, 0:1])
                x.then_inc(c["hot_y"], 1)
            act.dma_start(K.slot_d.rearrange("(p a) d -> p (a d)", p=P).rearrange("p (a n) -> p a n", n=512),
                          K.zeros[:, :].unsqueeze(1).to_broadcast([P, NSLOT * D // P // 512, 512])).then_inc(c["zeroed"], 16)
            act.sem_inc(c["hot_y"], FREE)
            nc.scalar.activation(warm[:, :], K.eps[:, :], ACT.Silu)
            steps(act, NI, 4, 0, body)
            act.wait_ge(c["zeroed"], 16)

        @block.vector
        def _(dve):
            v = nc.vector
            v.memset(acc[:, 0:(NB + 1) // 2, :], 0.0)
            v.memset(acc[:, (NB + 1) // 2:, :], 0.0).then_inc(c["cleared"], 1)
            dve.wait_ge(c["cleared"], 1)
            dve.sem_inc(c["messages"], FREE)
            dve.sem_inc(c["flushed"], 2)

            def flush(n, k):
                b = dve.value_load(K.item_block[0:1, bass.ds(n, 1)], min_val=0, max_val=NB)
                dve.wait_ge(c["flushed"], n + 2)
                dve.wait_ge(c["summed"], n + 1)
                a = acc[:, bass.ds(b, 1), :].rearrange("p a n -> p (a n)")
                v.tensor_tensor(a, a, ps_s[k % 2][:, :], ALU.add).then_inc(c["flushed"], 1)

            def body(n, k):
                h = k % 2
                dve.wait_ge(loaded[k], per(n, k, LD, 4))
                dve.wait_ge(c["hot"], n)
                v.tensor_scalar(rel[h][:, :], dst[k][:, :], K.item_base[:, bass.ds(n, 1)], None,
                                ALU.subtract).then_inc(c["rel"], 1)
                dve.wait_ge(gathered[k], per(n, k, 64, 4))
                dve.wait_ge(c["dot"], n)
                v.tensor_tensor(dot3[h][:, :, :, :], rows[k][:, :, MUL:D].rearrange("p c (i u) -> p c i u", i=3),
                                y[k][:, :, 1:4].unsqueeze(3).to_broadcast([P, GC, 3, MUL]),
                                ALU.mult).then_inc(c["dot3"], 1)
                dve.wait_ge(c["rel"], n + 1)
                dve.wait_ge(c["flushed"], n + 1)
                v.tensor_tensor(hot[h][:, :, :], K.iota_f[:, :].unsqueeze(1).to_broadcast([P, GC, P]),
                                rel[h][:, :].unsqueeze(2).to_broadcast([P, GC, P]), ALU.is_equal).then_inc(c["hot"], 1)
                dve.wait_ge(c["dot3"], n + 1)
                v.tensor_tensor(dot2[h][:, :, :], dot3[h][:, :, 0, :], dot3[h][:, :, 1, :],
                                ALU.add).then_inc(c["dot2"], 1)
                dve.wait_ge(c["weights"], n + 1)
                w = ps_e[h][:, :].rearrange("p (c n) -> p c n", c=GC)
                three = lambda a: a.rearrange("p c (i u) -> p c i u", i=3)
                spread = lambda a: a.unsqueeze(2).to_broadcast([P, GC, 3, MUL])

                def scalars(o, factor):
                    return v.tensor_tensor(msg[h][:, :, o * D:o * D + MUL], factor[:, :, 0:MUL],
                                           w[:, :, o * P:o * P + MUL], ALU.mult)

                def vectors(o, factor):
                    return v.tensor_tensor(three(msg[h][:, :, o * D + MUL:(o + 1) * D]), three(factor[:, :, MUL:D]),
                                           spread(w[:, :, o * P + MUL:(o + 1) * P]), ALU.mult)
                scalars(0, rows[k])
                dve.wait_ge(c["dot2"], n + 1)
                dve.wait_ge(c["messages"], n + 3)
                v.tensor_tensor(Z[h][:, :, 0:MUL], dot2[h][:, :, :], dot3[h][:, :, 2, :], ALU.add).then_inc(c["dot"], 1)
                vectors(0, rows[k])
                dve.wait_ge(c["factors"], n + 1)
                vectors(1, Z[h])
                dve.wait_ge(c["dot"], n + 1)
                scalars(1, Z[h]).then_inc(c["messages"], 1)

            def both(n, k):
                body(n, k)
                flush(n - 1, (k - 1) % 4)

            body(0, 0)
            steps_from(dve, 1, NI, 4, both)
            flush(NI - 1, (NI - 1) % 4)

        @block.tensor
        def _(pe):
            t = nc.tensor

            def hidden(n, k):
                pe.wait_ge(loaded[k], per(n, k, LD, 4))
                t.matmul(ps_h[k % 2][0:HID, :], K.w_e1s[:, :], el[k][:, :], start=True, stop=True).then_inc(c["hidden"], 1)

            def weights(n, k):
                pe.wait_ge(c["messages"], n + 3)
                pe.wait_ge(c["act"], n + 1)
                for j in range(GC):
                    x = t.matmul(ps_e[k % 2][:, j * 256:(j + 1) * 256], hT[k % 2][:, j * P:(j + 1) * P],
                                 K.w_e2[:, :], start=True, stop=True)
                x.then_inc(c["weights"], 1)

            def sums(n, k):
                pe.wait_ge(c["flushed"], n + 1)
                pe.wait_ge(c["messages"], n + 1 + FREE)
                pe.wait_ge(c["hot_y"], n + 1 + FREE)
                into = ps_s[k % 2][:, :].rearrange("p (g o u) -> p g o u", g=4, o=2)
                for j in range(GC):
                    for o, rows_hot in ((0, hot_y), (1, hot)):
                        x = t.matmul(into[:, :, o, :], rows_hot[k % 2][:, j, :], msg[k % 2][:, j, o * D:(o + 1) * D],
                                     start=j == 0 and o == 0, stop=j == GC - 1, skip_group_check=True)
                x.then_inc(c["summed"], 1)

            def body(n, k):
                weights(n, k)
                hidden(n + 1, (k + 1) % 4)
                sums(n - 1, (k - 1) % 4)

            hidden(0, 0)
            weights(0, 0)
            hidden(1, 1)
            steps_from(pe, 1, NI - 1, 4, body)
            weights(NI - 1, (NI - 1) % 4)
            sums(NI - 2, (NI - 2) % 4)
            sums(NI - 1, (NI - 1) % 4)


def update(nc, A, K, acc):
    with ExitStack() as ctx:
        m = Mem(nc, ctx, "update")
        two = lambda name, shape, dt=f32: [m.sb(f"{name}{k}", shape, dt) for k in range(2)]
        mid, midT = two("mid", [P, 512]), two("midT", [P, 512])
        resid = [m.sb(f"resid{k}", [P, D]) for k in range(2)] + [K.w_nodeA, K.w_nodeB]
        qT = [m.sb(f"qT{k}", [P, D]) for k in range(4)]
        den, attnT, xt, xtT = (two(z, [P, D]) for z in ("den", "attnT", "xt", "xtT"))
        stats, mean, mean2 = m.sb("stats", [P, NT, 6]), m.sb("mean", [P, NT]), m.sb("mean2", [P, NT])
        var, diff = m.sb("var", [P, NT]), m.sb("diff", [P, NT])
        rstd, shift, rstd2 = (m.sb(z, [P, NT]) for z in ("rstd", "shift", "rstd2"))
        eq = m.sb("eq", [P, NT, E])
        lg = K.w_qT[:, :, :].rearrange("p c n -> p (c n)")[:, 0:NT * E].rearrange("p (t e) -> p t e", e=E)
        room = K.w_kvT[:, :, :].rearrange("p c n -> p (c n)")
        left, ramp = (room[:, k * NT * E:(k + 1) * NT * E].rearrange("p (t e) -> p t e", e=E) for k in range(2))
        rank, total = (room[:, (2 * E + k) * NT:(2 * E + k + 1) * NT] for k in range(2))
        top = m.sb("top", [P, TOP, NT])
        ps_m, ps_a, ps_o = ([m.ps(f"{z}{k}") for k in range(2)] for z in ("mid", "attn", "out"))
        ps_x, ps_l = ps_m, m.ps("logits")
        resid_in, q_in = ([m.sem(f"{z}{k}") for k in range(4)] for z in ("resid_in", "q_in"))
        c = {z: m.sem(z) for z in (
            "mid", "turned", "midT", "attn", "den", "inverse", "attnT", "out", "part", "x2", "stats", "moments", "passed",
            "var", "rstd", "shift", "xt", "stats2", "moments2", "var2", "rstd2", "xt_turned", "xtT", "logits", "ramp",
            "shifted", "exp")}
        r = m.sem("router_steps")
        block = ctx.enter_context(nc.Block())
        old = lambda n: not (isinstance(n, int) and n < 2)
        one = lambda d, n: d[bass.ds(n, 1), :, :].rearrange("a p d -> (a p) d")
        tile = lambda a, n: a[:, bass.ds(n, 1), :].rearrange("p a d -> p (a d)")

        @block.sync
        def _(sp):
            def body(n, k):
                reused = not (isinstance(n, int) and n < 4)
                if reused:
                    sp.wait_ge(c["part"], n - 3)
                sp.dma_start(resid[k][:, :], one(K.resid_d, n)).then_inc(resid_in[k], 16)
                if reused:
                    sp.wait_ge(c["attn"], n - 3)
                sp.dma_start(qT[k][:, :], one(K.qT_d, n)).then_inc(q_in[k], 16)
            steps(sp, NT, 4, 4, body)

        @block.gpsimd
        def _(pool):
            g = nc.gpsimd
            g.iota(ramp[:, :, :], [[0, NT], [-1, E]], base=E, channel_multiplier=0,
                   allow_small_or_imprecise_dtypes=True).then_inc(c["ramp"], 1)

            def body(n, k):
                if old(n):
                    wait_apart(pool, c["passed"], (c["turned"], n - 1))
                g.tensor_copy(mid[k][:, :], tile(acc, n)).then_inc(c["mid"], 1)
            steps(pool, NT, 2, 2, body)
            for known, added, o, done in (("moments", "var", rstd, "rstd"), ("moments2", "var2", rstd2, "rstd2")):
                pool.wait_ge(c[known], MOMENT_STEPS)
                g.tensor_tensor(o[:, :], var[:, :], K.eps[:, :].to_broadcast([P, NT]), ALU.add).then_inc(c[added], 1)
                pool.wait_ge(c[added], 1)
                g.tensor_tensor(o[:, :], o[:, :], K.minus_half[:, :], ALU.pow).then_inc(c[done], 1)

        @block.tensor
        def _(pe):
            t = nc.tensor

            def first(n, slot):
                k = slot % 2
                pe.wait_ge(c["mid"], n + 1)
                if old(n):
                    pe.wait_ge(c["midT"], n - 1)
                for g in range(4):
                    z = t.transpose(ps_m[k][:, g * P:(g + 1) * P], mid[k][:, g * P:(g + 1) * P], K.ident[:, :])
                z.then_inc(c["turned"], 1)
                pe.wait_ge(q_in[slot], per(n, slot, 16, 4))
                if old(n):
                    pe.wait_ge(c["attnT"], n - 1)
                for h in range(2):
                    t.matmul(ps_a[k][:, h * P:(h + 1) * P], K.ctx_bd[:, h, :], qT[slot][:, h * P:(h + 1) * P],
                             start=True, stop=True)
                    z = t.matmul(ps_a[k][:, D + h * P:D + (h + 1) * P], K.ksum_bd[:, h, :], qT[slot][:, h * P:(h + 1) * P],
                                 start=True, stop=True)
                z.then_inc(c["attn"], 1)

            def second(n, k):
                pe.wait_ge(c["midT"], n + 1)
                if old(n):
                    pe.wait_ge(c["x2"], n - 1)
                for g in range(4):
                    t.matmul(ps_o[k][:, g * MUL:(g + 1) * MUL], midT[k][:, g * P:(g + 1) * P],
                             (K.w_lo0 if g == 0 else K.w_lo1)[:, :], start=True, stop=True)
                pe.wait_ge(c["attnT"], n + 1)
                for h in range(2):
                    z = t.matmul(ps_o[k][:, D:2 * D], attnT[k][:, h * P:(h + 1) * P], K.w_projT[:, h, :],
                                 start=h == 0, stop=h == 1)
                z.then_inc(c["out"], 1)

            def body(n, k):
                first(n + 1, (k + 1) % 4)
                second(n, k % 2)

            first(0, 0)
            steps(pe, NT - 1, 4, 4, body)
            second(NT - 1, (NT - 1) % 2)

            def turn(n, k):
                pe.wait_ge(c["xt"], n + 1)
                if old(n):
                    pe.wait_ge(c["xtT"], n - 1)
                for h in range(2):
                    z = t.transpose(ps_x[k][:, h * P:(h + 1) * P], xt[k][:, h * P:(h + 1) * P], K.ident[:, :])
                z.then_inc(c["xt_turned"], 1)

            def logits(n, k):
                pe.wait_ge(c["xtT"], n + 1)
                for h in range(2):
                    z = t.matmul(ps_l[:, bass.ds(n * E, E)], xtT[k][:, h * P:(h + 1) * P], K.w_r[:, h, :],
                                 start=h == 0, stop=h == 1)
                z.then_inc(c["logits"], 1)

            def route(n, k):
                turn(n + 1, 1 - k)
                logits(n, k)

            turn(0, 0)
            steps(pe, NT - 1, 2, 2, route)
            logits(NT - 1, (NT - 1) % 2)

        @block.scalar
        def _(act):
            a = nc.scalar

            def body(n, k):
                act.wait_ge(c["turned"], n + 1)
                if old(n):
                    act.wait_ge(c["out"], n - 1)
                a.copy(midT[k][:, :], ps_m[k][:, :]).then_inc(c["midT"], 1)
            steps(act, NT, 2, 2, body)
            act.wait_ge(c["shift"], 1)

            def normed(n, k):
                if old(n):
                    act.wait_ge(c["xt_turned"], n - 1)
                    act.wait_ge(c["stats2"], n - 1)
                a.activation(xt[k][:, :], tile(K.x2, n), ACT.Identity, scale=rstd[:, bass.ds(n, 1)],
                             bias=shift[:, bass.ds(n, 1)]).then_inc(c["xt"], 1)

            def turned(n, k):
                act.wait_ge(c["xt_turned"], n + 1)
                if old(n):
                    act.wait_ge(c["logits"], n - 1)
                a.copy(xtT[k][:, :], ps_x[k][:, 0:D]).then_inc(c["xtT"], 1)

            def route(n, k):
                normed(n + 1, 1 - k)
                turned(n, k)

            normed(0, 0)
            steps(act, NT - 1, 2, 2, route)
            turned(NT - 1, (NT - 1) % 2)
            act.wait_ge(c["shifted"], 1)
            a.activation(left[:, :, :], lg[:, :, :], ACT.Exp).then_inc(c["exp"], 1)

        @block.vector
        def _(dve):
            v = nc.vector

            def attention(n, k):
                dve.wait_ge(c["attn"], n + 1)
                if old(n):
                    dve.wait_ge(c["out"], n - 1)
                v.tensor_scalar(den[k][:, :], ps_a[k][:, D:2 * D], 1e-6, None, ALU.max).then_inc(c["den"], 1)
                dve.wait_ge(c["den"], n + 1)
                v.reciprocal(den[k][:, :], den[k][:, :]).then_inc(c["inverse"], 1)
                dve.wait_ge(c["inverse"], n + 1)
                v.tensor_tensor(attnT[k][:, :], ps_a[k][:, 0:D], den[k][:, :], ALU.mult).then_inc(c["attnT"], 1)

            def residual(n, slot):
                k = slot % 2
                dve.wait_ge(resid_in[slot], per(n, slot, 16, 4))
                dve.wait_ge(c["out"], n + 1)
                v.scalar_tensor_tensor(tile(K.x2, n), ps_o[k][:, 0:D], K.sc_o[:, bass.ds(n, 1)], resid[slot][:, :],
                                       ALU.mult, ALU.add).then_inc(c["part"], 1)
                dve.wait_ge(c["part"], n + 1)
                v.tensor_tensor(tile(K.x2, n), ps_o[k][:, D:2 * D], tile(K.x2, n), ALU.add).then_inc(c["x2"], 1)
                wait_apart(dve, c["passed"], (c["x2"], n + 1))
                v.bn_stats(tile(stats, n), tile(K.x2, n)).then_inc(c["stats"], 1)

            def body(n, k):
                attention(n + 1, (k + 1) % 2)
                residual(n, k)

            attention(0, 0)
            steps(dve, NT - 1, 4, 4, body)
            residual(NT - 1, (NT - 1) % 4)
            dve.wait_ge(c["stats"], NT)
            moments(dve, v, c["moments"], stats, mean[:, :], var[:, :], diff[:, :])
            dve.wait_ge(c["rstd"], 1)
            v.scalar_tensor_tensor(shift[:, :], mean[:, :], -1.0, rstd[:, :], ALU.mult, ALU.mult).then_inc(c["shift"], 1)

            def norms(n, k):
                wait_apart(dve, c["passed"], (c["xt"], n + 1))
                v.bn_stats(tile(stats, n), xt[k][:, :]).then_inc(c["stats2"], 1)
            steps(dve, NT, 2, 2, norms)
            dve.wait_ge(c["stats2"], NT)
            moments(dve, v, c["moments2"], stats, mean2[:, :], var[:, :], diff[:, :])

            n_done = [0]

            def done(ins):
                n_done[0] += 1
                ins.then_inc(r, 1)
                dve.wait_ge(r, n_done[0])

            wide = lambda a: a.unsqueeze(2).to_broadcast([P, NT, E])
            dve.wait_ge(c["shift"], 1)
            dve.wait_ge(c["rstd2"], 1)
            done(v.tensor_tensor(K.tok_scale[:, :], rstd[:, :], rstd2[:, :], ALU.mult))
            done(v.tensor_tensor(K.tok_shift[:, :], shift[:, :], mean2[:, :], ALU.subtract))
            done(v.tensor_tensor(K.tok_shift[:, :], K.tok_shift[:, :], rstd2[:, :], ALU.mult))
            dve.wait_ge(c["logits"], NT)
            done(v.tensor_tensor(lg[:, :, :], ps_l[:, 0:NT * E].rearrange("p (t e) -> p t e", e=E),
                                 K.b_r[:, :].unsqueeze(1).to_broadcast([P, NT, E]), ALU.add))
            done(v.tensor_reduce(rank, lg[:, :, :], AX.X, ALU.max))
            done(v.tensor_tensor(lg[:, :, :], lg[:, :, :], wide(rank), ALU.subtract))
            dve.sem_inc(c["shifted"], 1)
            dve.wait_ge(c["exp"], 1)
            dve.wait_ge(c["ramp"], 1)
            for i in range(TOP):
                done(v.tensor_reduce(top[:, i, :], left[:, :, :], AX.X, ALU.max))
                done(v.tensor_tensor(eq[:, :, :], left[:, :, :], wide(top[:, i, :]), ALU.is_equal))
                done(v.tensor_tensor(eq[:, :, :], eq[:, :, :], ramp[:, :, :], ALU.mult))
                done(v.tensor_reduce(rank, eq[:, :, :], AX.X, ALU.max))
                done(v.tensor_tensor(K.onehot[:, :, i, :], eq[:, :, :], wide(rank), ALU.is_equal))
                if i + 1 < TOP:
                    done(v.scalar_tensor_tensor(left[:, :, :], K.onehot[:, :, i, :], -2.0, left[:, :, :], ALU.mult, ALU.add))
            done(v.tensor_tensor(total, top[:, 0, :], top[:, 1, :], ALU.add))
            done(v.reciprocal(total, total))
            for i in range(TOP):
                done(v.tensor_tensor(K.weight[:, :, i], top[:, i, :], total, ALU.mult))


def dispatch(nc, A, K):
    G = NT * TOP
    with ExitStack() as ctx:
        m = Mem(nc, ctx, "dispatch")
        tot, incl, place = (m.sb(x, [P, G, E]) for x in ("tot", "incl", "place"))
        nb_i = m.sb("nb_i", [P, E], i32)
        nb, b_end, first = (m.sb(x, [P, E]) for x in ("nb", "b_end", "first"))
        pos = m.sb("pos", [P, G])
        gone, which = m.sb("gone", [1, NSB, E]), m.sb("which", [1, NSB])
        tok = [m.sb(f"tok{k}", [P, D]) for k in range(4)]
        idx = [m.sb(f"idx{k}", [P, TOP], i32) for k in range(4)]
        ps_w, ps_t = m.ps("within", 2), m.ps("total", 2)
        d, summed, copied, passed = (m.sem(x) for x in ("vector_steps", "summed", "copied", "passed"))
        normed = m.sem("normed")
        sent = [m.sem(f"sent{k}") for k in range(4)]
        half = G // 2
        done_at = {}
        block = ctx.enter_context(nc.Block())
        old = lambda n: not (isinstance(n, int) and n < 4)

        @block.tensor
        def _(pe):
            for w, ps in ((K.before, ps_w), (K.ones, ps_t)):
                for h in range(2):
                    rhs = K.onehot[:, :, :, :].rearrange("p n t e -> p (n t e)")[:, h * half * E:(h + 1) * half * E]
                    x = nc.tensor.matmul(ps[:, h * 512:h * 512 + half * E], w[:, :], rhs, start=True, stop=True)
            x.then_inc(summed, 1)

        @block.vector
        def _(dve):
            v, n = nc.vector, [0]

            def done(ins):
                n[0] += 1
                ins.then_inc(d, 1)
                dve.wait_ge(d, n[0])

            halves = lambda ps: ps[:, :].rearrange("p (h n) -> p h n", h=2)[:, :, 0:half * E]
            dve.wait_ge(summed, 1)
            done(v.tensor_copy(tot[:, :, :].rearrange("p (h g) e -> p h (g e)", h=2), halves(ps_t)))
            for e in range(E):
                done(v.tensor_tensor_scan(incl[:, :, e], K.ones[:, 0:G], tot[:, :, e], 0.0, ALU.mult, ALU.add))
            done(v.tensor_tensor(place[:, :, :], incl[:, :, :], tot[:, :, :], ALU.subtract))
            done(v.tensor_tensor(place[:, :, :].rearrange("p (h g) e -> p h (g e)", h=2),
                                 place[:, :, :].rearrange("p (h g) e -> p h (g e)", h=2), halves(ps_w), ALU.add))
            done(v.tensor_scalar(nb[:, :], incl[:, G - 1, :], float(SB - 1), None, ALU.add))
            done(v.tensor_copy(nb_i[:, :], nb[:, :]))
            done(v.tensor_scalar(nb_i[:, :], nb_i[:, :], SB.bit_length() - 1, None, ALU.arith_shift_right))
            done(v.tensor_copy(nb[:, :], nb_i[:, :]))
            done(v.tensor_tensor_scan(b_end[:, :], K.ones[:, 0:E], nb[:, :], 0.0, ALU.mult, ALU.add))
            done(v.tensor_tensor(first[:, :], b_end[:, :], nb[:, :], ALU.subtract))
            done(v.tensor_scalar(first[:, :], first[:, :], float(SB), None, ALU.mult))
            done(v.tensor_tensor(place[:, :, :], place[:, :, :], first[:, :].unsqueeze(1).to_broadcast([P, G, E]), ALU.add))
            done(v.tensor_tensor(place[:, :, :], place[:, :, :], K.onehot[:, :, :, :].rearrange("p n t e -> p (n t) e"),
                                 ALU.mult))
            done(v.tensor_reduce(pos[:, :], place[:, :, :], AX.X, ALU.add))
            done(v.tensor_copy(K.pos_i[:, :, :].rearrange("p n t -> p (n t)"), pos[:, :]))
            done_at["pos"] = n[0]
            done(v.tensor_tensor(gone[:, :, :], K.iota_f[0:1, 0:NSB].unsqueeze(2).to_broadcast([1, NSB, E]),
                                 b_end[0:1, :].unsqueeze(1).to_broadcast([1, NSB, E]), ALU.is_ge))
            done(v.tensor_reduce(which[:, :], gone[:, :, :], AX.X, ALU.add))
            done(v.tensor_scalar(which[:, :], which[:, :], float(E - 1), None, ALU.min))
            done(v.tensor_copy(K.block_expert[:, :], which[:, :]))

        @block.scalar
        def _(act):
            def body(n, k):
                if old(n):
                    act.wait_ge(sent[k], per(n, k, 32, 4) - 32)
                nc.scalar.activation(tok[k][:, :], K.x2[:, bass.ds(n, 1), :].rearrange("p a d -> p (a d)"), ACT.Identity,
                                     scale=K.tok_scale[:, bass.ds(n, 1)],
                                     bias=K.tok_shift[:, bass.ds(n, 1)]).then_inc(normed, 1)
            steps(act, NT, 4, 4, body)

        @block.gpsimd
        def _(pool):
            pool.wait_ge(d, done_at["pos"])

            def body(n, k):
                wait_apart(pool, passed, *([(sent[k], per(n, k, 32, 4) - 32)] if old(n) else []), (normed, n + 1))
                nc.gpsimd.tensor_copy(idx[k][:, :], K.pos_i[:, bass.ds(n, 1), :].rearrange("p a t -> p (a t)")
                                      ).then_inc(copied, 1)
                wait_apart(pool, passed, (copied, n + 1))
                for t in range(TOP):
                    nc.gpsimd.indirect_dma_start(
                        out=K.slot_d, out_offset=bass.IndirectOffsetOnAxis(ap=idx[k][:, t:t + 1], axis=0),
                        in_=tok[k][:, :], in_offset=None, bounds_check=NSLOT - 1, oob_is_err=False).then_inc(sent[k], 16)
            steps(pool, NT, 4, 4, body)
            for k in range(4):
                pool.wait_ge(sent[k], 32 * ((NT + 3 - k) // 4))


def experts(nc, A, K):
    NH = H // P
    with ExitStack() as ctx:
        m = Mem(nc, ctx, "experts")
        two = lambda name, shape, dt=f32: [m.sb(f"{name}{k}", shape, dt) for k in range(2)]
        w1, w2 = two("w1", [P, 2, H]), two("w2", [P, NH, D])
        ec, b2 = two("constants", [P, 2 + 2 + NH]), two("b2", [P, D])
        xb, xT, hT, yb = two("x", [P, 2, D]), two("xT", [P, 2, SB]), two("hT", [P, NH, SB]), two("y", [P, 2, D])
        ps_x = [m.ps(f"x{k}") for k in range(2)]
        ps_h = [m.ps(f"h{k}") for k in range(4)]
        ps_y = [m.ps(f"y{k}") for k in range(2)]
        rows_in, loaded, stored = ([m.sem(f"{x}{k}") for k in range(2)] for x in ("rows_in", "loaded", "stored"))
        c = {x: m.sem(x) for x in ("turned", "xT", "first", "gelu", "second", "y")}
        block = ctx.enter_context(nc.Block())
        old = lambda n: not (isinstance(n, int) and n < 2)
        rows = lambda d, n: d.rearrange("(b h p) d -> p b h d", h=2, p=P)[:, bass.ds(n, 1), :, :].rearrange(
            "p b h d -> p (b h) d")
        LD = 16 * 4

        @block.sync
        def _(sp):
            def body(n, k):
                if old(n):
                    sp.wait_ge(c["turned"], n - 1)
                sp.dma_start(xb[k][:, :, :], rows(K.slot_d, n)).then_inc(rows_in[k], 16)
                if old(n):
                    sp.wait_ge(c["y"], n - 1)
                e = sp.value_load(K.block_expert[0:1, bass.ds(n, 1)], min_val=0, max_val=E - 1)
                one = lambda a: a[bass.ds(e, 1), :, :].rearrange("a p n -> (a p) n")
                sp.dma_start(ec[k][:, :], one(A["e_const"])).then_inc(loaded[k], 16)
                sp.dma_start(w1[k][:, :, :].rearrange("p c n -> p (c n)"), one(A["w1"])).then_inc(loaded[k], 16)
                sp.dma_start(b2[k][:, :], one(A["b2"]).to_broadcast([P, D])).then_inc(loaded[k], 16)
                sp.dma_start(w2[k][:, :, :].rearrange("p c n -> p (c n)"), one(A["w2"])).then_inc(loaded[k], 16)
            steps(sp, NSB, 2, 2, body)

        @block.tensor
        def _(pe):
            t = nc.tensor

            def turn(n, k):
                pe.wait_ge(rows_in[k], per(n, k))
                if old(n):
                    pe.wait_ge(c["xT"], n - 1)
                for h in range(2):
                    for s in range(2):
                        x = t.transpose(ps_x[k][:, h * SB + s * P:h * SB + (s + 1) * P], xb[k][:, s, h * P:(h + 1) * P],
                                        K.ident[:, :])
                x.then_inc(c["turned"], 1)

            def layers(n, k, more):
                pe.wait_ge(c["xT"], n + 1)
                pe.wait_ge(loaded[k], per(n, k, LD))
                for j in range(NH):
                    if not (isinstance(n, int) and n == 0 and j < 4):
                        pe.wait_ge(c["gelu"], n * NH + (j - 3))
                    for h in range(2):
                        x = t.matmul(ps_h[j % 4][:, 0:SB], w1[k][:, h, j * P:(j + 1) * P], xT[k][:, h, :],
                                     start=h == 0, stop=h == 1)
                    x.then_inc(c["first"], 1)
                if more:
                    turn(n + 1, 1 - k)
                if not (isinstance(n, int) and n == 0):
                    pe.wait_ge(c["y"], n)
                for j in range(NH):
                    pe.wait_ge(c["gelu"], n * NH + (j + 1))
                    for s in range(2):
                        x = t.matmul(ps_y[s][:, 0:D], hT[k][:, j, s * P:(s + 1) * P], w2[k][:, j, :],
                                     start=j == 0, stop=j == NH - 1)
                x.then_inc(c["second"], 1)

            turn(0, 0)
            steps(pe, NSB - 2, 2, 2, lambda n, k: layers(n, k, True))
            layers(NSB - 2, 0, True)
            layers(NSB - 1, 1, False)

        @block.scalar
        def _(act):
            def shift(n, k):
                act.wait_ge(c["turned"], n + 1)
                act.wait_ge(loaded[k], per(n, k, LD))
                if old(n):
                    act.wait_ge(c["first"], (n - 1) * NH)
                for h in range(2):
                    x = nc.scalar.activation(xT[k][:, h, :], ps_x[k][:, h * SB:(h + 1) * SB], ACT.Identity,
                                             scale=ec[k][:, h:h + 1], bias=ec[k][:, 2 + h:3 + h])
                x.then_inc(c["xT"], 1)

            def gelu(n, k, more):
                if old(n):
                    act.wait_ge(c["second"], n - 1)
                for j in range(NH):
                    act.wait_ge(c["first"], n * NH + (j + 1))
                    nc.scalar.activation(hT[k][:, j, :], ps_h[j % 4][:, 0:SB], ACT.Gelu,
                                         bias=ec[k][:, 4 + j:5 + j]).then_inc(c["gelu"], 1)
                if more:
                    shift(n + 1, 1 - k)
                act.wait_ge(c["y"], n + 1)
                act.dma_start(rows(K.y_d, n), yb[k][:, :, :]).then_inc(stored[k], 16)

            shift(0, 0)
            steps(act, NSB - 2, 2, 2, lambda n, k: gelu(n, k, True))
            gelu(NSB - 2, 0, True)
            gelu(NSB - 1, 1, False)
            for k in range(2):
                act.wait_ge(stored[k], 16 * NSB // 2)

        @block.vector
        def _(dve):
            def body(n, k):
                dve.wait_ge(c["second"], n + 1)
                if old(n):
                    dve.wait_ge(stored[k], per(n, k) - 16)
                for s in range(2):
                    x = nc.vector.tensor_tensor(yb[k][:, s, :], ps_y[s][:, 0:D], b2[k][:, :], ALU.add)
                x.then_inc(c["y"], 1)
            steps(dve, NSB, 2, 2, body)


def combine(nc, A, K, out):
    with ExitStack() as ctx:
        m = Mem(nc, ctx, "combine")
        four = lambda name, shape, dt=f32: [m.sb(f"{name}{k}", shape, dt) for k in range(4)]
        idx, part, res = four("idx", [P, TOP], i32), four("part", [P, D]), four("res", [P, D])
        rows = [four(f"rows{t}_", [P, D]) for t in range(TOP)]
        fetched, stored = ([m.sem(f"{x}{k}") for k in range(4)] for x in ("fetched", "stored"))
        copied, part_ready, ready, passed = (m.sem(x) for x in ("copied", "part", "ready", "passed"))
        block = ctx.enter_context(nc.Block())
        old = lambda n: not (isinstance(n, int) and n < 4)

        @block.gpsimd
        def _(pool):
            def body(n, k):
                if old(n):
                    wait_apart(pool, passed, (ready, n - 3))
                nc.gpsimd.tensor_copy(idx[k][:, :], K.pos_i[:, bass.ds(n, 1), :].rearrange("p a t -> p (a t)")
                                      ).then_inc(copied, 1)
                wait_apart(pool, passed, (copied, n + 1))
                for t in range(TOP):
                    nc.gpsimd.indirect_dma_start(
                        out=rows[t][k][:, :], out_offset=None, in_=K.y_d,
                        in_offset=bass.IndirectOffsetOnAxis(ap=idx[k][:, t:t + 1], axis=0),
                        bounds_check=NSLOT - 1, oob_is_err=False).then_inc(fetched[k], 16)
            steps(pool, NT, 4, 4, body)

        @block.vector
        def _(dve):
            def body(n, k):
                dve.wait_ge(fetched[k], per(n, k, 32, 4))
                w = lambda t: K.weight[:, bass.ds(n, 1), t:t + 1].rearrange("p a t -> p (a t)")
                v = nc.vector
                if old(n):
                    dve.wait_ge(ready, n - 3)
                v.scalar_tensor_tensor(part[k][:, :], rows[0][k][:, :], w(0),
                                       K.x2[:, bass.ds(n, 1), :].rearrange("p a d -> p (a d)"), ALU.mult,
                                       ALU.add).then_inc(part_ready, 1)
                dve.wait_ge(part_ready, n + 1)
                if old(n):
                    dve.wait_ge(stored[k], per(n, k, 16, 4) - 16)
                v.scalar_tensor_tensor(res[k][:, :], rows[1][k][:, :], w(1), part[k][:, :], ALU.mult,
                                       ALU.add).then_inc(ready, 1)
            steps(dve, NT, 4, 4, body)

        @block.sync
        def _(sp):
            def body(n, k):
                sp.wait_ge(ready, n + 1)
                sp.dma_start(out[bass.ds(n, 1), :, :].rearrange("a p d -> (a p) d"), res[k][:, :]).then_inc(stored[k], 16)
            steps(sp, NT, 4, 4, body)
            for k in range(4):
                sp.wait_ge(stored[k], 16 * ((NT + 3 - k) // 4))


class Shared:
    pass


def program(nc, A, out):
    with ExitStack() as ctx:
        K = Shared()
        sb = Mem(nc, ctx, "k").sb
        dram = lambda name, shape: nc.dram_tensor(name, shape, f32, kind="Internal").ap()
        K.table_d, K.resid_d = dram("gather_table", (NT, P, D)), dram("residual", (NT, P, D))
        K.qT_d = dram("queries_T", (NT, P, D))
        K.el_hi_d, K.el_lo_d = dram("el_hi", (NG, BAS, GE)), dram("el_lo", (NG, BAS, GE))
        K.slot_d, K.y_d = dram("slot_rows", (NSLOT, D)), dram("slot_results", (NSLOT, D))
        K.ident, K.ones, K.iota_f, K.before, K.upto, K.head_mask = (
            sb(x, [P, P]) for x in ("ident", "ones", "iota_f", "before", "upto", "head_mask"))
        K.minus_half, K.eps = sb("minus_half", [P, NT]), sb("eps", [P, 1])
        K.zeros = sb("zeros", [P, 512])
        K.x2 = sb("x2", [P, NT, D])
        K.tok_scale, K.tok_shift = sb("tok_scale", [P, NT]), sb("tok_shift", [P, NT])
        K.valid_row, K.attr, K.dis, K.sc_f, K.sc_m, K.sc_o = (
            sb(x, [P, NT]) for x in ("valid_row", "attr", "dis", "sc_f", "sc_m", "sc_o"))
        K.w_nodeA, K.w_nodeB = sb("w_nodeA", [P, 256]), sb("w_nodeB", [P, 256])
        K.w_kvT, K.w_qT, K.w_projT = sb("w_kvT", [P, 2, 512]), sb("w_qT", [P, 2, 256]), sb("w_projT", [P, 2, 256])
        K.w_e1, K.w_e2 = sb("w_e1", [3 * BAS, HID]), sb("w_e2", [HID, 256])
        K.w_e1s = sb("w_e1s", [3 * BAS, HID], f32r)
        K.w_lo0, K.w_lo1 = sb("w_lo0", [P, MUL]), sb("w_lo1", [P, MUL])
        K.w_r, K.b_r, K.b_proj = sb("w_r", [P, 2, E]), sb("b_r", [P, E]), sb("b_proj", [P, D])
        K.item_group, K.item_block = sb("item_group", [1, NI], i32), sb("item_block", [1, NI], i32)
        K.item_base = sb("item_base", [P, NI])
        K.ctx_bd, K.ksum_bd = sb("ctx_bd", [P, 2, P]), sb("ksum_bd", [P, 2, P])
        K.weight, K.onehot = sb("weight", [P, NT, TOP]), sb("onehot", [P, NT, TOP, E])
        K.pos_i, K.block_expert = sb("pos_i", [P, NT, TOP], i32), sb("block_expert", [1, NSB], i32)
        setup(nc, A, K)
        items(nc, A, K)
        nodes(nc, A, K)
        with ExitStack() as sums:
            acc = sums.enter_context(nc.sbuf_tensor("accumulators", [P, NB + 1, 512], f32))
            edges(nc, A, K, acc)
            update(nc, A, K, acc)
        dispatch(nc, A, K)
        experts(nc, A, K)
        combine(nc, A, K, out)


def kernel(x, src, dst, edge_attr_10, edge_attr_4, node_vec1, L0_gnn_W_li0, L0_gnn_W_li1, L0_gnn_W_lm0, L0_gnn_W_lm1,
           L0_gnn_W_mlp1, L0_gnn_W_mlp2, L0_gnn_W_lo0, L0_gnn_W_lo1, L0_mix_Wq, L0_mix_Wkv, L0_mix_Wproj, L0_mix_bproj,
           L0_ffn_Wr, L0_ffn_br, L0_ffn_ln_g, L0_ffn_ln_b, L0_ffn_W1, L0_ffn_b1, L0_ffn_W2, L0_ffn_b2):
    import numpy as np
    import concourse.bacc as bacc
    from concourse.bass_utils import run_bass_kernel_spmd

    perm = np.concatenate([np.arange(MUL)] + [MUL + 3 * np.arange(MUL) + i for i in range(3)])

    def rows(a, n, fill=0):
        a = np.asarray(a)
        pad = np.full((n - a.shape[0],) + a.shape[1:], fill, a.dtype)
        return np.concatenate([a, pad])

    def diag(a, b):
        z = np.zeros((MUL, MUL), np.asarray(a).dtype)
        return np.block([[np.asarray(a), z], [z, np.asarray(b)]])

    ne = NG * GE
    by_group = lambda a: a.reshape(NG, GC, P, -1).transpose(0, 2, 1, 3).reshape(NG, P, -1)
    dst_p = rows(dst, NGP * GE, N_PAD - 1)
    y = np.asarray(edge_attr_4)
    chunks = lambda w: np.asarray(w).reshape(2, P, -1)
    W_2 = np.asarray(L0_gnn_W_mlp2).reshape(HID, 4, MUL)[:, [0, 3, 1, 2]].reshape(HID, 256)
    swap = lambda w: np.asarray(w).reshape(2, MUL, MUL)[::-1].reshape(P, MUL)
    per_chunk = lambda a: np.asarray(a).reshape(E, -1, P).transpose(0, 2, 1)
    arrays = {
        "x": rows(np.asarray(x)[:, perm], N_PAD).reshape(NT, P, D),
        "attr": rows(node_vec1, N_PAD).reshape(NT, P).T,
        "src": by_group(rows(src, ne)),
        "dst": by_group(dst_p[:ne]),
        "dst_cols": dst_p[:NC * P].reshape(NC, P).T,
        "dst_rows": dst_p.reshape(NGP, GE),
        "y": by_group(rows(y, ne)),
        "el": rows(edge_attr_10, ne).reshape(NG, GE, BAS).transpose(0, 2, 1),
        "w_e1": np.concatenate([np.asarray(L0_gnn_W_mlp1)] * 3), "w_e2": W_2,
        "w_nodeA": np.concatenate([diag(L0_gnn_W_li0, L0_gnn_W_li1), diag(L0_gnn_W_lm0, L0_gnn_W_lm1)], 1),
        "w_nodeB": np.concatenate([diag(L0_gnn_W_li1, L0_gnn_W_li1), diag(L0_gnn_W_lm1, L0_gnn_W_lm1)], 1),
        "w_lo0": np.asarray(L0_gnn_W_lo0), "w_lo1": swap(L0_gnn_W_lo1),
        "w_kvT": chunks(np.asarray(L0_mix_Wkv)[:, perm].T), "w_qT": chunks(np.asarray(L0_mix_Wq)[:, perm].T),
        "w_projT": chunks(np.asarray(L0_mix_Wproj)[perm].T), "b_proj": np.asarray(L0_mix_bproj)[perm][None],
        "w_r": chunks(np.asarray(L0_ffn_Wr)[perm]), "b_r": np.asarray(L0_ffn_br)[None],
        "w1": np.asarray(L0_ffn_W1)[:, perm].reshape(E, 2, P, H).transpose(0, 2, 1, 3).reshape(E, P, 2 * H),
        "w2": np.asarray(L0_ffn_W2)[:, :, perm].reshape(E, H // P, P, D).transpose(0, 2, 1, 3).reshape(E, P, -1),
        "e_const": np.concatenate([per_chunk(np.asarray(L0_ffn_ln_g)[:, perm]), per_chunk(np.asarray(L0_ffn_ln_b)[:, perm]),
                                   per_chunk(L0_ffn_b1)], 2),
        "b2": np.asarray(L0_ffn_b2)[:, perm][:, None],
    }
    arrays = {f"in_{k}": np.ascontiguousarray(a) for k, a in arrays.items()}
    nc = bacc.Bacc("TRN2", target_bir_lowering=False, num_devices=1)
    A = {k[3:]: nc.dram_tensor(k, a.shape, mybir.dt.from_np(a.dtype), kind="ExternalInput").ap()
         for k, a in arrays.items()}
    out = nc.dram_tensor("out", (NT, P, D), f32, kind="ExternalOutput").ap()
    program(nc, A, out)
    got = run_bass_kernel_spmd(nc, [arrays], core_ids=[0]).results[0]["out"]
    result = np.empty((N_NODES, D), got.dtype)
    result[:, perm] = got.reshape(N_PAD, D)[:N_NODES]
    return result
```

```python
from contextlib import ExitStack
import math

import concourse.bass as bass
from concourse import mybir

P = 128
N_NODES, D, MUL = 6250, 256, 64
NT = -(-N_NODES // P)
N_PAD = NT * P
N_EDGES = 200000
GE, GC = 512, 4
NG = -(-N_EDGES // GE)
UC = 32
NC = NT * UC
NEL = 46
TC = 7
EC = NG * 10 * GE // P // NEL
NGP = 4 * P
NB = NT
NI = NG + NB
HID, BAS = 100, 10
HEADS, HD = 8, 32
E, H, TOP = 8, 1024, 2
SB = 256
NSB = (TOP * N_PAD + E * (SB - 1)) // SB
NSLOT = NSB * SB
GP = 14
EPS = 1e-5
C_S, C_X = math.sin(math.pi / 8), math.cos(math.pi / 8)

f32, f32r, bf16, i32 = mybir.dt.float32, mybir.dt.float32r, mybir.dt.bfloat16, mybir.dt.int32
ALU, ACT, AX = mybir.AluOpType, mybir.ActivationFunctionType, mybir.AxisListType


def steps(eng, count, unroll, head, body):
    loops = (count - head) // unroll
    for n in range(head):
        body(n, n % unroll)
    if loops:
        with eng.Fori(0, loops) as i:
            for j in range(unroll):
                body(i * unroll + (head + j), (head + j) % unroll)
    for n in range(head + loops * unroll, count):
        body(n, n % unroll)


def steps_from(eng, first, end, unroll, body):
    loops = (end - first) // unroll
    with eng.Fori(0, loops) as i:
        for j in range(unroll):
            body(i * unroll + (first + j), (first + j) % unroll)
    for n in range(first + loops * unroll, end):
        body(n, n % unroll)


def per(n, k, each=16, slots=2):
    if isinstance(n, int):
        return (n // slots + 1) * each
    if each % slots == 0:
        return (n - k + slots) * (each // slots)
    raise ValueError(each)


def wait_apart(eng, passed, *waits):
    for sem, v in waits:
        eng.wait_ge(sem, v)
    eng.sem_inc(passed, 1)


class Mem:

    def __init__(self, nc, ctx, prefix):
        self.nc, self.ctx, self.prefix = nc, ctx, prefix

    def sb(self, name, shape, dt=f32):
        return self.ctx.enter_context(self.nc.sbuf_tensor(f"{self.prefix}_{name}", shape, dt))

    def ps(self, name, banks=1):
        return self.ctx.enter_context(self.nc.psum_tensor(f"{self.prefix}_ps_{name}", [P, 512 * banks], f32))

    def sem(self, name):
        return self.nc.alloc_semaphore(f"{self.prefix}_{name}")


def setup(nc, A, K):
    with ExitStack() as ctx:
        m = Mem(nc, ctx, "setup")
        loaded, made, scaled = m.sem("loaded"), m.sem("made"), m.sem("scaled")
        w_hi, w_part = m.sb("w_hi", [3 * BAS, HID], f32r), m.sb("w_part", [3 * BAS, HID])
        low_row = m.sb("low_row", [3 * BAS, 1])
        block = ctx.enter_context(nc.Block())
        loads = [(K.w_nodeA[:, :], A["w_nodeA"]), (K.w_nodeB[:, :], A["w_nodeB"]),
                 (K.w_kvT[:, :, :], A["w_kvT"].rearrange("c p n -> p c n")),
                 (K.w_qT[:, :, :], A["w_qT"].rearrange("c p n -> p c n")),
                 (K.w_projT[:, :, :], A["w_projT"].rearrange("c p n -> p c n")),
                 (K.w_e1[:, :], A["w_e1"]), (K.w_e2[:, :], A["w_e2"]),
                 (K.w_lo0[:, :], A["w_lo0"]), (K.w_lo1[:, :], A["w_lo1"]),
                 (K.w_r[:, :, :], A["w_r"].rearrange("c p n -> p c n")),
                 (K.b_r[:, :], A["b_r"].to_broadcast([P, E])),
                 (K.b_proj[:, :], A["b_proj"].to_broadcast([P, D])),
                 (K.attr[:, :], A["attr"])]

        @block.sync
        def _(sp):
            for dst, src in loads:
                sp.dma_start(dst, src).then_inc(loaded, 16)
            sp.wait_ge(loaded, 16 * len(loads))

        @block.gpsimd
        def _(pool):
            g = nc.gpsimd
            g.memset(K.ones[:, :], 1.0).then_inc(made, 1)
            g.memset(K.zeros[:, :], 0.0).then_inc(made, 1)
            g.memset(K.minus_half[:, :], -0.5)
            g.memset(K.eps[:, :], EPS)
            pool.wait_ge(made, 2)
            g.affine_select(out=K.ident[:, :], in_=K.ones[:, :], compare_op=ALU.is_equal, fill=0.0, base=0,
                            pattern=[[-1, P]], channel_multiplier=1)
            g.affine_select(out=K.before[:, :], in_=K.ones[:, :], compare_op=ALU.is_gt, fill=0.0, base=0,
                            pattern=[[1, P]], channel_multiplier=-1)
            g.affine_select(out=K.upto[:, :], in_=K.ones[:, :], compare_op=ALU.is_ge, fill=0.0, base=0,
                            pattern=[[1, P]], channel_multiplier=-1)
            g.affine_select(out=K.valid_row[:, :], in_=K.ones[:, 0:NT], compare_op=ALU.is_ge, fill=0.0,
                            base=N_NODES - 1, pattern=[[-P, NT]], channel_multiplier=-1)
            g.affine_select(out=low_row[:, :], in_=K.zeros[0:3 * BAS, 0:1], compare_op=ALU.is_gt, fill=-1.0,
                            base=2 * BAS, pattern=[[0, 1]], channel_multiplier=-1)
            g.affine_select(out=K.head_mask[:, :], in_=K.ones[:, :], compare_op=ALU.is_ge, fill=0.0, base=0,
                            pattern=[[-HD, P // HD], [0, HD]], channel_multiplier=1).then_inc(made, 1)
            pool.wait_ge(made, 3)
            g.affine_select(out=K.head_mask[:, :], in_=K.head_mask[:, :], compare_op=ALU.is_ge, fill=0.0,
                            base=HD - 1, pattern=[[HD, P // HD], [0, HD]], channel_multiplier=-1)
            g.iota(K.iota_f[:, :], [[1, P]], base=0, channel_multiplier=0, allow_small_or_imprecise_dtypes=True)

        @block.vector
        def _(dve):
            dve.wait_ge(loaded, 16 * len(loads))
            nc.vector.tensor_scalar(K.w_lo0[MUL:P, :], K.w_lo0[MUL:P, :], 1 / math.sqrt(3.0), None,
                                    ALU.mult).then_inc(scaled, 1)
            nc.vector.tensor_copy(w_hi[:, :], K.w_e1[:, :]).then_inc(scaled, 1)
            dve.wait_ge(scaled, 2)
            dve.wait_ge(made, 3)
            nc.vector.scalar_tensor_tensor(w_part[:, :], w_hi[:, :].bitcast(f32), low_row[:, :], K.w_e1[:, :], ALU.mult,
                                           ALU.add).then_inc(scaled, 1)
            dve.wait_ge(scaled, 3)
            nc.vector.tensor_copy(K.w_e1s[:, :], w_part[:, :]).then_inc(scaled, 1)


def items(nc, A, K):
    with ExitStack() as ctx:
        m = Mem(nc, ctx, "items")
        dst = m.sb("dst", [P, 4, GE], i32)
        ends = m.sb("ends", [P, 2, 4], i32); endf = m.sb("endf", [P, 2, 4])
        count = m.sb("count", [P, 4]); start = m.sb("start", [P, 4]); end = m.sb("end", [P, 4])
        shift = m.sb("shift", [P, 4]); prefix = m.sb("prefix", [P, 4])
        group_id = m.sb("group_id", [P, 4]); real = m.sb("real", [P, 4])
        item = m.sb("item", [P, NI])
        begun = m.sb("begun", [P, 4, NI]); mine = m.sb("mine", [P, 4, NI])
        w_id = m.sb("w_id", [P, 4, P]); w_shift = m.sb("w_shift", [P, 4, P]); w_real = m.sb("w_real", [P, 4, P])
        row_b = m.sb("row_b", [P, NI])
        totals, p_id, p_shift, p_real = (m.ps(x) for x in ("totals", "id", "shift", "real"))
        loaded, x_in, iotas, d, summed = (m.sem(x) for x in ("loaded", "x_in", "iotas", "vector_steps", "summed"))
        ready_at = {}
        block = ctx.enter_context(nc.Block())

        @block.sync
        def _(sp):
            sp.dma_start(dst[:, :, :], A["dst_rows"].rearrange("(g p) e -> p g e", p=P)).then_inc(loaded, 16)
            sp.dma_start(K.x2[:, :, :], A["x"].rearrange("t p d -> p t d")).then_inc(x_in, 16)
            sp.wait_ge(x_in, 16)

        @block.gpsimd
        def _(pool):
            g = nc.gpsimd
            g.iota(group_id[:, :], [[P, 4]], base=0, channel_multiplier=1, allow_small_or_imprecise_dtypes=True)
            g.iota(item[:, :], [[1, NI]], base=0, channel_multiplier=0,
                   allow_small_or_imprecise_dtypes=True).then_inc(iotas, 1)

        @block.vector
        def _(dve):
            v, n = nc.vector, [0]

            def done(ins):
                n[0] += 1
                ins.then_inc(d, 1)
                dve.wait_ge(d, n[0])

            dve.wait_ge(loaded, 16)
            dve.wait_ge(iotas, 1)
            done(v.tensor_reduce(ends[:, 0, :], dst[:, :, :], AX.X, ALU.min))
            done(v.tensor_reduce(ends[:, 1, :], dst[:, :, :], AX.X, ALU.max))
            done(v.tensor_scalar(ends[:, :, :], ends[:, :, :], 7, None, ALU.arith_shift_right))
            done(v.tensor_copy(endf[:, :, :], ends[:, :, :]))
            done(v.tensor_scalar(real[:, :], group_id[:, :], float(NG), None, ALU.is_lt))
            done(v.scalar_tensor_tensor(count[:, :], endf[:, 1, :], 1.0, endf[:, 0, :], ALU.add, ALU.subtract))
            done(v.tensor_tensor(count[:, :], count[:, :], real[:, :], ALU.mult))
            ready_at["counts"] = n[0]
            dve.wait_ge(summed, 1)
            done(v.tensor_copy(end[:, :], totals[:, 0:4]))
            done(v.tensor_copy(prefix[:, :], totals[:, 4:8]))
            for g in range(1, 4):
                for h in range(g):
                    done(v.tensor_tensor(end[:, g:g + 1], end[:, g:g + 1], prefix[:, h:h + 1], ALU.add))
            done(v.tensor_tensor(start[:, :], end[:, :], count[:, :], ALU.subtract))
            done(v.tensor_tensor(shift[:, :], endf[:, 0, :], start[:, :], ALU.subtract))
            for g in range(4):
                done(v.tensor_scalar(begun[:, g, :], item[:, :], start[:, g:g + 1], None, ALU.is_ge))
                done(v.scalar_tensor_tensor(mine[:, g, :], item[:, :], end[:, g:g + 1], begun[:, g, :], ALU.is_lt, ALU.mult))
                for w, value in ((w_id, group_id), (w_shift, shift), (w_real, real)):
                    x = v.tensor_scalar(w[:, g, :], K.ones[:, :], value[:, g:g + 1], None, ALU.mult)
            done(x)
            ready_at["look-up"] = n[0]
            dve.wait_ge(summed, 2)
            done(v.tensor_copy(K.item_group[:, :], p_id[0:1, 0:NI]))
            done(v.scalar_tensor_tensor(row_b[:, :], p_shift[:, 0:NI], -float(NB), item[:, :], ALU.add, ALU.add))
            done(v.tensor_tensor(row_b[:, :], row_b[:, :], p_real[:, 0:NI], ALU.mult))
            done(v.tensor_scalar(row_b[:, :], row_b[:, :], float(NB), None, ALU.add))
            done(v.tensor_copy(K.item_block[:, :], row_b[0:1, :]))
            done(v.tensor_scalar(K.item_base[:, :], row_b[:, :], float(P), None, ALU.mult))

        @block.tensor
        def _(pe):
            pe.wait_ge(d, ready_at["counts"])
            nc.tensor.matmul(totals[:, 0:4], K.upto[:, :], count[:, :], start=True, stop=True)
            nc.tensor.matmul(totals[:, 4:8], K.ones[:, :], count[:, :], start=True, stop=True).then_inc(summed, 1)
            pe.wait_ge(d, ready_at["look-up"])
            for ps, w in ((p_id, w_id), (p_shift, w_shift), (p_real, w_real)):
                for g in range(4):
                    x = nc.tensor.matmul(ps[:, 0:NI], w[:, g, :], mine[:, g, :], start=g == 0, stop=g == 3)
            x.then_inc(summed, 1)


def moments(dve, v, stepped, stats, mean, var, diff):
    (m0, s0), (m1, s1) = ((stats[:, :, 3 * h + 1], stats[:, :, 3 * h + 2]) for h in range(2))
    v.tensor_tensor(diff, m0, m1, ALU.subtract).then_inc(stepped, 1)
    v.tensor_tensor(mean, m0, m1, ALU.add).then_inc(stepped, 1)
    v.tensor_tensor(var, s0, s1, ALU.add).then_inc(stepped, 1)
    dve.wait_ge(stepped, 3)
    v.tensor_scalar(mean, mean, 0.5, None, ALU.mult).then_inc(stepped, 1)
    v.scalar_tensor_tensor(diff, diff, 0.25, diff, ALU.mult, ALU.mult).then_inc(stepped, 1)
    dve.wait_ge(stepped, 5)
    v.scalar_tensor_tensor(var, var, 1.0 / D, diff, ALU.mult, ALU.add).then_inc(stepped, 1)
    dve.wait_ge(stepped, MOMENT_STEPS)


MOMENT_STEPS = 6


def nodes(nc, A, K):
    with ExitStack() as ctx:
        m = Mem(nc, ctx, "nodes")
        two = lambda name, shape, dt=f32: [m.sb(f"{name}{k}", shape, dt) for k in range(2)]
        dst = m.sb("dst", [P, NC], i32)
        lo, hi = m.sb("lo", [P, NC], bf16), m.sb("hi", [P, NC], bf16)
        iota_r = m.sb("iota_r", [P, P, UC], bf16)
        hot_lo, hot_hi = two("hot_lo", [P, P, UC], bf16), two("hot_hi", [P, NB, UC], bf16)
        part = hot_lo[0][:, :, :].rearrange("p j c -> p (j c)").bitcast(i32)[:, 0:NC]
        x, f = K.x2, m.sb("f", [P, NT, D])
        stats = m.sb("stats", [P, NT, 6])
        mean, var, diff = (m.sb(z, [P, NT]) for z in ("mean", "var", "diff"))
        rstd, shift = m.sb("rstd", [P, NT]), m.sb("shift", [P, NT])
        el, el_hi, el_lo = (two(z, [P, EC], t) for z, t in (("el", f32), ("el_hi", f32r), ("el_lo", f32r)))
        xn, xnT, res, k_t, q_t = (two(z, [P, D]) for z in ("xn", "xnT", "res", "k", "q"))
        k_low, k_high, q_low, q_high = (two(z, [P, D]) for z in ("k_low", "k_high", "q_low", "q_high"))
        m_t, v_t = two("m", [P, D]), two("v", [P, 2, P + 1])
        ps_q, sums = m.ps("q"), m.ps("sums")
        ps_c, deg = sums[:, 0:2 * (P + 1)], sums[:, 2 * (P + 1):2 * (P + 1) + NT]
        ps_T, ps_f, ps_kv = ([m.ps(f"{z}{k}") for k in range(2)] for z in ("T", "f", "kv"))
        c = {z: m.sem(z) for z in (
            "dst_in", "split", "hot", "counted", "clamped", "dis", "scales", "stats", "moments", "b", "rstd",
            "shift", "var", "iota", "xn", "turned", "xnT", "fm", "kv", "queries", "fm_used", "k_parts", "q_parts",
            "exps", "v", "k", "q", "res", "context", "f_scaled", "f_out", "el_hi", "el_lo")}
        el_in, el_out = ([m.sem(f"{z}{k}") for k in range(2)] for z in ("el_in", "el_out"))
        el_cols = lambda d, n: d.rearrange("g b e -> (g b e)").rearrange("(p n) -> p n", p=P)[:, bass.ds(n * EC, EC)]
        res_out, q_out = ([m.sem(f"{z}{k}") for k in range(2)] for z in ("res_out", "q_out"))
        block = ctx.enter_context(nc.Block())
        old = lambda n: not (isinstance(n, int) and n < 2)
        one = lambda d, n: d[bass.ds(n, 1), :, :].rearrange("a p d -> (a p) d")
        tile = lambda a, n: a[:, bass.ds(n, 1), :].rearrange("p a d -> p (a d)")

        @block.sync
        def _(sp):
            sp.dma_start(dst[:, :], A["dst_cols"]).then_inc(c["dst_in"], 16)

            lengths_in = lambda n, k: sp.dma_start(el[k][:, :], el_cols(A["el"], n)).then_inc(el_in[k], 16)

            def body(n, k, split=True, more=True):
                sp.wait_ge(c["res"], n + 1)
                sp.dma_start(one(K.resid_d, n), res[k][:, :]).then_inc(res_out[k], 16)
                sp.wait_ge(c["q"], n + 1)
                sp.dma_start(one(K.qT_d, n), q_t[k][:, :]).then_inc(q_out[k], 16)
                if split:
                    sp.wait_ge(c["el_lo"], n + 1)
                    sp.dma_start(el_cols(K.el_hi_d, n), el_hi[k][:, :].bitcast(f32)).then_inc(el_out[k], 16)
                    sp.dma_start(el_cols(K.el_lo_d, n), el_lo[k][:, :].bitcast(f32)).then_inc(el_out[k], 16)
                if more:
                    lengths_in(n + 2, k)

            lengths_in(0, 0)
            lengths_in(1, 1)
            steps(sp, NEL - 2, 2, 2, body)
            for n in range(NEL - 2, NT):
                body(n, n % 2, n < NEL, False)
            for t in range(0, NT, TC):
                sp.wait_ge(c["f_scaled"], t // TC + 1)
                sp.dma_start(K.table_d[t:t + TC].rearrange("t p d -> p t d"), f[:, t:t + TC, :]).then_inc(c["f_out"], 16)
            sp.wait_ge(c["f_out"], 16 * (NT // TC))
            for k in range(2):
                for out in (res_out, q_out):
                    sp.wait_ge(out[k], 16 * ((NT + 1 - k) // 2))
                sp.wait_ge(el_out[k], 32 * ((NEL + 1 - k) // 2))

        @block.gpsimd
        def _(pool):
            g = nc.gpsimd
            g.iota(iota_r[:, :, :], [[1, P], [0, UC]], base=0, channel_multiplier=0,
                   allow_small_or_imprecise_dtypes=True).then_inc(c["iota"], 1)
            pool.wait_ge(c["moments"], MOMENT_STEPS)
            g.tensor_tensor(rstd[:, :], var[:, :], K.eps[:, :].to_broadcast([P, NT]), ALU.add).then_inc(c["var"], 1)
            pool.wait_ge(c["var"], 1)
            for at in (slice(0, 4), slice(4, NT)):
                g.tensor_tensor(rstd[:, at], rstd[:, at], K.minus_half[:, at], ALU.pow).then_inc(c["rstd"], 1)

            def body(n, k):
                pool.wait_ge(c["fm_used"], n + 1)
                if old(n):
                    pool.wait_ge(res_out[k], per(n, k) - 16)
                g.tensor_tensor(res[k][:, :], m_t[k][:, :], tile(x, n), ALU.add).then_inc(c["b"], 1)
                pool.wait_ge(c["b"], n + 1)
                g.tensor_tensor(res[k][:, :], res[k][:, :], K.b_proj[:, :], ALU.add).then_inc(c["res"], 1)
                pool.wait_ge(c["exps"], n + 1)
                if old(n):
                    pool.wait_ge(c["context"], n - 1)
                g.tensor_tensor(k_t[k][:, :], k_high[k][:, :], k_low[k][:, :], ALU.add).then_inc(c["k"], 1)
                if old(n):
                    pool.wait_ge(q_out[k], per(n, k) - 16)
                g.tensor_tensor(q_t[k][:, :], q_high[k][:, :], q_low[k][:, :], ALU.add).then_inc(c["q"], 1)
            steps(pool, NT, 2, 2, body)
            pool.wait_ge(c["clamped"], 1)
            g.tensor_tensor(K.dis[:, :], K.dis[:, :], K.minus_half[:, :], ALU.pow).then_inc(c["dis"], 1)

        @block.vector
        def _(dve):
            v = nc.vector
            v.tensor_scalar(K.sc_m[:, :], K.attr[:, :], C_S / 8.0, None, ALU.mult).then_inc(c["scales"], 1)
            def norms(n, k):
                v.bn_stats(tile(stats, n), tile(x, n)).then_inc(c["stats"], 1)
            steps(dve, NT, 7, 0, norms)
            dve.wait_ge(c["stats"], NT)
            moments(dve, v, c["moments"], stats, mean[:, :], var[:, :], diff[:, :])

            def shifts(part, at):
                dve.wait_ge(c["rstd"], part)
                v.scalar_tensor_tensor(shift[:, at], mean[:, at], -1.0, rstd[:, at], ALU.mult, ALU.mult).then_inc(c["shift"], 1)
            shifts(1, slice(0, 4))
            dve.wait_ge(c["dst_in"], 16)
            v.tensor_scalar(part, dst[:, :], P - 1, None, ALU.bitwise_and).then_inc(c["split"], 1)
            dve.wait_ge(c["split"], 1)
            v.tensor_copy(lo[:, :], part).then_inc(c["split"], 1)
            dve.wait_ge(c["split"], 2)
            v.tensor_scalar(part, dst[:, :], 7, None, ALU.arith_shift_right).then_inc(c["split"], 1)
            dve.wait_ge(c["split"], 3)
            v.tensor_copy(hi[:, :], part).then_inc(c["split"], 1)
            shifts(2, slice(4, NT))
            dve.wait_ge(c["iota"], 1)
            dve.wait_ge(c["split"], 4)

            def hots(n, k):
                if old(n):
                    dve.wait_ge(c["counted"], n - 1)
                cols = lambda a, w: a[:, bass.ds(n * UC, UC)].unsqueeze(1).to_broadcast([P, w, UC])
                v.tensor_tensor(hot_lo[k][:, :, :], iota_r[:, :, :], cols(lo, P), ALU.is_equal)
                v.tensor_tensor(hot_hi[k][:, :, :], iota_r[:, 0:NB, :], cols(hi, NB), ALU.is_equal).then_inc(c["hot"], 1)
            def lengths(n, k):
                dve.wait_ge(el_in[k], per(n, k))
                if old(n):
                    dve.wait_ge(el_out[k], 2 * (per(n, k) - 16))
                v.tensor_copy(el_hi[k][:, :], el[k][:, :]).then_inc(c["el_hi"], 1)
                dve.wait_ge(c["el_hi"], n + 1)
                v.tensor_tensor(el_lo[k][:, :], el[k][:, :], el_hi[k][:, :].bitcast(f32),
                                ALU.subtract).then_inc(c["el_lo"], 1)

            def both(n, k):
                hots(n, k)
                lengths(n, k)
            steps(dve, NEL, 2, 2, both)
            for n in range(NEL, NT):
                hots(n, n % 2)
            dve.wait_ge(c["context"], NT)
            v.tensor_scalar(K.dis[:, :], deg, 1.0, None, ALU.max).then_inc(c["clamped"], 1)
            dve.wait_ge(c["dis"], 1)
            v.scalar_tensor_tensor(K.sc_f[:, :], K.dis[:, :], 1 / 80.0, K.attr[:, :], ALU.mult, ALU.mult)
            v.scalar_tensor_tensor(K.sc_o[:, :], K.dis[:, :], C_X / math.sqrt(128.0), K.attr[:, :],
                                   ALU.mult, ALU.mult).then_inc(c["scales"], 1)
            dve.wait_ge(c["scales"], 2)
            dve.wait_ge(c["fm_used"], NT)

            for t in range(0, NT, TC):
                v.tensor_tensor(f[:, t:t + TC, :], f[:, t:t + TC, :],
                                K.sc_f[:, t:t + TC].unsqueeze(2).to_broadcast([P, TC, D]), ALU.mult).then_inc(c["f_scaled"], 1)
            pc = ps_c.rearrange("p (c n) -> p c n", c=2)
            heads = K.head_mask[:, :].unsqueeze(1).to_broadcast([P, 2, P])
            v.tensor_tensor(K.ctx_bd[:, :, :], pc[:, :, 0:P], heads, ALU.mult)
            first_of_head = K.head_mask[:, :].rearrange("p (h u) -> p h u", u=HD)[:, :, 0].unsqueeze(1)
            v.tensor_tensor(K.ksum_bd[:, :, :], pc[:, :, P:P + 1].to_broadcast([P, 2, P // HD]),
                            first_of_head.to_broadcast([P, 2, P // HD]), ALU.mult)

        @block.scalar
        def _(act):
            a = nc.scalar

            def normed(n, k):
                if old(n):
                    act.wait_ge(c["turned"], n - 1)
                a.activation(xn[k][:, :], tile(x, n), ACT.Identity, scale=rstd[:, bass.ds(n, 1)],
                             bias=shift[:, bass.ds(n, 1)]).then_inc(c["xn"], 1)

            def turned(n, k):
                act.wait_ge(c["turned"], n + 1)
                if old(n):
                    act.wait_ge(c["queries"], n - 1)
                a.copy(xnT[k][:, :], ps_T[k][:, 0:D]).then_inc(c["xnT"], 1)

            def emptied(n, k):
                act.wait_ge(c["fm"], n + 1)
                pf = ps_f[k][:, :].rearrange("p (c h n) -> p c h n", c=2, h=2)
                a.copy(tile(f, n).rearrange("p (c n) -> p c n", c=2), pf[:, :, 0, :])
                if old(n):
                    act.wait_ge(c["res"], n - 1)
                a.activation(m_t[k][:, :].rearrange("p (c n) -> p c n", c=2), pf[:, :, 1, :], ACT.Identity,
                             scale=K.sc_m[:, bass.ds(n, 1)]).then_inc(c["fm_used"], 1)
                act.wait_ge(c["kv"], n + 1)
                if old(n):
                    act.wait_ge(c["q"], n - 1)
                    act.wait_ge(c["context"], n - 1)
                a.activation(k_low[k][:, :], ps_kv[k][:, 0:D], ACT.Relu, scale=-1.0).then_inc(c["k_parts"], 1)
                a.activation(k_high[k][:, :], ps_kv[k][:, 0:D], ACT.Relu)
                a.copy(v_t[k][:, :, 0:P], ps_kv[k][:, D:2 * D].rearrange("p (c n) -> p c n", c=2))
                a.copy(v_t[k][:, :, P:P + 1],
                       K.valid_row[:, bass.ds(n, 1)].unsqueeze(1).to_broadcast([P, 2, 1])).then_inc(c["v"], 1)
                act.wait_ge(c["queries"], n + 1)
                a.activation(q_low[k][:, :], ps_q[:, 0:D], ACT.Relu, scale=-1.0)
                a.activation(q_high[k][:, :], ps_q[:, 0:D], ACT.Relu).then_inc(c["q_parts"], 1)
                act.wait_ge(c["k_parts"], n + 1)
                a.activation(k_low[k][:, :], k_low[k][:, :], ACT.Exp, scale=-1.0)
                act.wait_ge(c["q_parts"], n + 1)
                a.activation(q_low[k][:, :], q_low[k][:, :], ACT.Exp, scale=-1.0).then_inc(c["exps"], 1)

            def body(n, k):
                turned(n + 1, 1 - k)
                normed(n + 2, k)
                emptied(n, k)

            act.wait_ge(c["shift"], 1)
            act.wait_ge(c["scales"], 1)
            normed(0, 0)
            normed(1, 1)
            turned(0, 0)
            body(0, 0)
            body(1, 1)
            act.wait_ge(c["shift"], 2)
            steps_from(act, 2, NT - 2, 2, body)
            turned(NT - 1, (NT - 1) % 2)
            emptied(NT - 2, NT % 2)
            emptied(NT - 1, (NT - 1) % 2)

        @block.tensor
        def _(pe):
            t = nc.tensor

            def turn(n, k):
                pe.wait_ge(c["xn"], n + 1)
                if old(n):
                    pe.wait_ge(c["xnT"], n - 1)
                for h in range(2):
                    z = t.transpose(ps_T[k][:, h * P:(h + 1) * P], xn[k][:, h * P:(h + 1) * P], K.ident[:, :])
                z.then_inc(c["turned"], 1)

            def project(n, k):
                pe.wait_ge(c["xnT"], n + 1)
                if old(n):
                    pe.wait_ge(c["exps"], n - 1)
                xa, xb = xnT[k][:, 0:P], xnT[k][:, P:D]
                t.matmul(ps_f[k][:, 0:256], xa, K.w_nodeA[:, :], start=True, stop=True)
                t.matmul(ps_f[k][:, 256:512], xb, K.w_nodeB[:, :], start=True, stop=True).then_inc(c["fm"], 1)
                t.matmul(ps_kv[k][:, :], xa, K.w_kvT[:, 0, :], start=True, stop=False)
                t.matmul(ps_kv[k][:, :], xb, K.w_kvT[:, 1, :], start=False, stop=True).then_inc(c["kv"], 1)
                if not (isinstance(n, int) and n == 0):
                    pe.wait_ge(c["q_parts"], n)
                for o in range(2):
                    for h, xh in enumerate((xa, xb)):
                        z = t.matmul(ps_q[:, o * P:(o + 1) * P], K.w_qT[:, h, o * P:(o + 1) * P], xh,
                                     start=h == 0, stop=h == 1)
                z.then_inc(c["queries"], 1)

            def context(n, k):
                pe.wait_ge(c["k"], n + 1)
                pe.wait_ge(c["v"], n + 1)
                last = isinstance(n, int) and n == NT - 1
                for h in range(2):
                    z = t.matmul(ps_c[:, h * (P + 1):(h + 1) * (P + 1)], k_t[k][:, h * P:(h + 1) * P],
                                 v_t[k][:, h, :], start=False, stop=last, skip_group_check=True)
                z.then_inc(c["context"], 1)

            def count(n, k):
                pe.wait_ge(c["hot"], n + 1)
                first, last = (isinstance(n, int) and n == e for e in (0, NT - 1))
                for j in range(UC):
                    z = t.matmul(deg, hot_lo[k][:, :, j], hot_hi[k][:, :, j], start=first and j == 0,
                                 stop=last and j == UC - 1, skip_group_check=True)
                z.then_inc(c["counted"], 1)

            def body(n, k):
                turn(n + 1, 1 - k)
                project(n, k)
                context(n - 1, 1 - k)
                count(n, k)

            turn(0, 0)
            turn(1, 1)
            project(0, 0)
            count(0, 0)
            body(1, 1)
            steps_from(pe, 2, NT - 1, 2, body)
            project(NT - 1, (NT - 1) % 2)
            context(NT - 2, NT % 2)
            count(NT - 1, (NT - 1) % 2)
            context(NT - 1, (NT - 1) % 2)


def edges(nc, A, K, acc):
    FREE = 4
    with ExitStack() as ctx:
        m = Mem(nc, ctx, "edges")
        four = lambda name, shape, dt=f32: [m.sb(f"{name}{k}", shape, dt) for k in range(4)]
        two = lambda name, shape, dt=f32: [m.sb(f"{name}{k}", shape, dt) for k in range(2)]
        el, ends = four("el", [3 * BAS, GE], f32r), four("ends", [P, 2, GC], i32)
        y = four("y", [P, GC, 4])
        rel, hT = two("rel", [P, GC]), two("hT", [HID, GE])
        hot, hot_y = two("hot", [P, GC, P]), two("hot_y", [P, GC, P])
        warm = m.sb("warm", [P, 1])
        room = K.x2[:, :, :].rearrange("p t d -> p (t d)")
        cut = lambda at, n: room[:, at * GC * D:(at + n) * GC * D].rearrange("p (c n) -> p c n", c=GC)
        rows, Z = [cut(k, 1) for k in range(4)], [cut(4 + k, 1) for k in range(2)]
        msg = [cut(6 + 2 * k, 2) for k in range(2)]
        dot3 = [cut(10 + k, 1)[:, :, 0:3 * MUL].rearrange("p c (i u) -> p c i u", i=3) for k in range(2)]
        dot2 = [cut(10 + k, 1)[:, :, 3 * MUL:] for k in range(2)]
        ps_e = [m.ps(f"edge{k}", 2) for k in range(2)]
        ps_h, ps_s = ([m.ps(f"{x}{k}") for k in range(2)] for x in ("hidden", "sum"))
        loaded, gathered = ([m.sem(f"{x}{k}") for k in range(4)] for x in ("loaded", "gathered"))
        c = {x: m.sem(x) for x in ("cleared", "messages", "flushed", "hidden", "act", "weights", "factors", "rel", "hot_y",
                                   "dot3", "dot2", "dot", "hot", "summed", "passed")}
        block = ctx.enter_context(nc.Block())
        LD = 16 * 5

        @block.sync
        def _(sp):
            def body(n, k):
                sp.wait_ge(c["messages"], n + 1)
                sp.wait_ge(c["hot_y"], n + 1)
                t = sp.value_load(K.item_group[0:1, bass.ds(n, 1)], min_val=0, max_val=NG - 1)
                one = lambda a: a[bass.ds(t, 1), :, :].rearrange("a p n -> (a p) n")
                sp.dma_start(ends[k][:, :, :].rearrange("p s c -> p (s c)"), one(A["ends"])).then_inc(loaded[k], 16)
                sp.dma_start(y[k][:, :, :].rearrange("p c n -> p (c n)"), one(A["y"])).then_inc(loaded[k], 16)
                for i, part in enumerate((K.el_hi_d, K.el_lo_d, K.el_hi_d)):
                    sp.dma_start(el[k][i * BAS:(i + 1) * BAS, :].bitcast(f32), one(part)).then_inc(loaded[k], 16)
            steps(sp, NI, 4, 0, body)

        @block.gpsimd
        def _(pool):
            def body(n, k):
                wait_apart(pool, c["passed"], (c["messages"], n + 1), (loaded[k], per(n, k, LD, 4)))
                for j in range(GC):
                    nc.gpsimd.indirect_dma_start(
                        out=rows[k][:, j, :], out_offset=None, in_=K.table_d.rearrange("t p d -> (t p) d"),
                        in_offset=bass.IndirectOffsetOnAxis(ap=ends[k][:, 0, j:j + 1], axis=0),
                        bounds_check=N_PAD - 1, oob_is_err=False).then_inc(gathered[k], 16)
            steps(pool, NI, 4, 0, body)

        @block.scalar
        def _(act):
            def body(n, k):
                act.wait_ge(c["hidden"], n + 1)
                nc.scalar.activation(hT[k % 2][:, :], ps_h[k % 2][0:HID, :], ACT.Silu,
                                     scale=1 / math.sqrt(BAS)).then_inc(c["act"], 1)
                act.wait_ge(gathered[k], per(n, k, 64, 4))
                act.wait_ge(c["messages"], n + 3)
                for j in range(GC):
                    for i in range(3):
                        x = nc.scalar.activation(Z[k % 2][:, j, MUL * (i + 1):MUL * (i + 2)], rows[k][:, j, 0:MUL],
                                                 ACT.Identity, scale=y[k][:, j, 1 + i:2 + i])
                x.then_inc(c["factors"], 1)
                act.wait_ge(c["hot"], n + 1)
                act.wait_ge(c["flushed"], n + 1)
                for j in range(GC):
                    x = nc.scalar.activation(hot_y[k % 2][:, j, :], hot[k % 2][:, j, :], ACT.Identity, scale=y[k][:, j, 0:1])
                x.then_inc(c["hot_y"], 1)
            act.sem_inc(c["hot_y"], FREE)
            nc.scalar.activation(acc[:, (NB + 1) // 2:, :], K.zeros[:, :].unsqueeze(1).to_broadcast([P, (NB + 1) // 2, 512]),
                                 ACT.Identity).then_inc(c["cleared"], 1)
            nc.scalar.activation(warm[:, :], K.eps[:, :], ACT.Silu)
            steps(act, NI, 4, 0, body)

        @block.vector
        def _(dve):
            v = nc.vector
            dve.sem_inc(c["messages"], FREE)
            dve.sem_inc(c["flushed"], 2)
            v.memset(acc[:, 0:(NB + 1) // 2, :], 0.0).then_inc(c["cleared"], 1)
            dve.wait_ge(c["cleared"], 2)

            def flush(n, k):
                b = dve.value_load(K.item_block[0:1, bass.ds(n, 1)], min_val=0, max_val=NB)
                dve.wait_ge(c["flushed"], n + 2)
                dve.wait_ge(c["summed"], n + 1)
                a = acc[:, bass.ds(b, 1), :].rearrange("p a n -> p (a n)")
                v.tensor_tensor(a, a, ps_s[k % 2][:, :], ALU.add).then_inc(c["flushed"], 1)

            def body(n, k):
                h = k % 2
                dve.wait_ge(loaded[k], per(n, k, LD, 4))
                dve.wait_ge(c["hot"], n)
                v.tensor_scalar(rel[h][:, :], ends[k][:, 1, :], K.item_base[:, bass.ds(n, 1)], None,
                                ALU.subtract).then_inc(c["rel"], 1)
                dve.wait_ge(gathered[k], per(n, k, 64, 4))
                dve.wait_ge(c["dot"], n)
                v.tensor_tensor(dot3[h][:, :, :, :], rows[k][:, :, MUL:D].rearrange("p c (i u) -> p c i u", i=3),
                                y[k][:, :, 1:4].unsqueeze(3).to_broadcast([P, GC, 3, MUL]),
                                ALU.mult).then_inc(c["dot3"], 1)
                dve.wait_ge(c["rel"], n + 1)
                dve.wait_ge(c["flushed"], n + 1)
                v.tensor_tensor(hot[h][:, :, :], K.iota_f[:, :].unsqueeze(1).to_broadcast([P, GC, P]),
                                rel[h][:, :].unsqueeze(2).to_broadcast([P, GC, P]), ALU.is_equal).then_inc(c["hot"], 1)
                dve.wait_ge(c["dot3"], n + 1)
                v.tensor_tensor(dot2[h][:, :, :], dot3[h][:, :, 0, :], dot3[h][:, :, 1, :],
                                ALU.add).then_inc(c["dot2"], 1)
                dve.wait_ge(c["weights"], n + 1)
                w = ps_e[h][:, :].rearrange("p (c n) -> p c n", c=GC)
                three = lambda a: a.rearrange("p c (i u) -> p c i u", i=3)
                spread = lambda a: a.unsqueeze(2).to_broadcast([P, GC, 3, MUL])

                def scalars(o, factor):
                    return v.tensor_tensor(msg[h][:, :, o * D:o * D + MUL], factor[:, :, 0:MUL],
                                           w[:, :, o * P:o * P + MUL], ALU.mult)

                def vectors(o, factor):
                    return v.tensor_tensor(three(msg[h][:, :, o * D + MUL:(o + 1) * D]), three(factor[:, :, MUL:D]),
                                           spread(w[:, :, o * P + MUL:(o + 1) * P]), ALU.mult)
                scalars(0, rows[k])
                dve.wait_ge(c["dot2"], n + 1)
                dve.wait_ge(c["messages"], n + 3)
                v.tensor_tensor(Z[h][:, :, 0:MUL], dot2[h][:, :, :], dot3[h][:, :, 2, :], ALU.add).then_inc(c["dot"], 1)
                vectors(0, rows[k])
                dve.wait_ge(c["factors"], n + 1)
                vectors(1, Z[h])
                dve.wait_ge(c["dot"], n + 1)
                scalars(1, Z[h]).then_inc(c["messages"], 1)

            def both(n, k):
                body(n, k)
                flush(n - 1, (k - 1) % 4)

            body(0, 0)
            steps_from(dve, 1, NI, 4, both)
            flush(NI - 1, (NI - 1) % 4)

        @block.tensor
        def _(pe):
            t = nc.tensor

            def hidden(n, k):
                pe.wait_ge(loaded[k], per(n, k, LD, 4))
                t.matmul(ps_h[k % 2][0:HID, :], K.w_e1s[:, :], el[k][:, :], start=True, stop=True).then_inc(c["hidden"], 1)

            def weights(n, k):
                pe.wait_ge(c["messages"], n + 3)
                pe.wait_ge(c["act"], n + 1)
                for j in range(GC):
                    x = t.matmul(ps_e[k % 2][:, j * 256:(j + 1) * 256], hT[k % 2][:, j * P:(j + 1) * P],
                                 K.w_e2[:, :], start=True, stop=True)
                x.then_inc(c["weights"], 1)

            def sums(n, k):
                pe.wait_ge(c["flushed"], n + 1)
                pe.wait_ge(c["messages"], n + 1 + FREE)
                pe.wait_ge(c["hot_y"], n + 1 + FREE)
                into = ps_s[k % 2][:, :].rearrange("p (g o u) -> p g o u", g=4, o=2)
                for j in range(GC):
                    for o, rows_hot in ((0, hot_y), (1, hot)):
                        x = t.matmul(into[:, :, o, :], rows_hot[k % 2][:, j, :], msg[k % 2][:, j, o * D:(o + 1) * D],
                                     start=j == 0 and o == 0, stop=j == GC - 1, skip_group_check=True)
                x.then_inc(c["summed"], 1)

            def body(n, k):
                weights(n, k)
                hidden(n + 1, (k + 1) % 4)
                sums(n - 1, (k - 1) % 4)

            hidden(0, 0)
            weights(0, 0)
            hidden(1, 1)
            steps_from(pe, 1, NI - 1, 4, body)
            weights(NI - 1, (NI - 1) % 4)
            sums(NI - 2, (NI - 2) % 4)
            sums(NI - 1, (NI - 1) % 4)


def update(nc, A, K, acc, out):
    with ExitStack() as ctx:
        m = Mem(nc, ctx, "update")
        two = lambda name, shape, dt=f32: [m.sb(f"{name}{k}", shape, dt) for k in range(2)]
        mid, midT = two("mid", [P, 512]), two("midT", [P, 512])
        resid = [m.sb(f"resid{k}", [P, D]) for k in range(2)] + [K.w_nodeA, K.w_nodeB]
        qT = [m.sb(f"qT{k}", [P, D]) for k in range(4)]
        den = two("den", [P, HEADS])
        attn, attnT, xt, xtT = (two(z, [P, D]) for z in ("attn", "attnT", "xt", "xtT"))
        stats, mean, mean2 = m.sb("stats", [P, NT, 6]), m.sb("mean", [P, NT]), m.sb("mean2", [P, NT])
        var, diff = m.sb("var", [P, NT]), m.sb("diff", [P, NT])
        rstd, shift, rstd2 = (m.sb(z, [P, NT]) for z in ("rstd", "shift", "rstd2"))
        eq = m.sb("eq", [P, NT, E])
        lg = K.w_qT[:, :, :].rearrange("p c n -> p (c n)")[:, 0:NT * E].rearrange("p (t e) -> p t e", e=E)
        room = K.w_kvT[:, :, :].rearrange("p c n -> p (c n)")
        left, ramp = (room[:, k * NT * E:(k + 1) * NT * E].rearrange("p (t e) -> p t e", e=E) for k in range(2))
        rank, total = (room[:, (2 * E + k) * NT:(2 * E + k + 1) * NT] for k in range(2))
        top = m.sb("top", [P, TOP, NT])
        ps_m, ps_a, ps_o = ([m.ps(f"{z}{k}") for k in range(2)] for z in ("mid", "attn", "out"))
        ps_x, ps_l = ps_m, m.ps("logits")
        resid_in, q_in = ([m.sem(f"{z}{k}") for k in range(4)] for z in ("resid_in", "q_in"))
        c = {z: m.sem(z) for z in (
            "mid", "turned", "midT", "attn", "den", "inverse", "divided", "attn_turned", "attnT", "out", "part", "x2",
            "stats", "moments", "passed", "var", "rstd", "shift", "xt", "stats2", "moments2", "var2", "rstd2", "xt_turned",
            "xtT", "logits", "ramp", "begun", "shifted", "exp")}
        r = m.sem("router_steps")
        block = ctx.enter_context(nc.Block())
        old = lambda n: not (isinstance(n, int) and n < 2)
        one = lambda d, n: d[bass.ds(n, 1), :, :].rearrange("a p d -> (a p) d")
        tile = lambda a, n: a[:, bass.ds(n, 1), :].rearrange("p a d -> p (a d)")

        @block.sync
        def _(sp):
            def body(n, k):
                reused = not (isinstance(n, int) and n < 4)
                if reused:
                    sp.wait_ge(c["part"], n - 3)
                sp.dma_start(resid[k][:, :], one(K.resid_d, n)).then_inc(resid_in[k], 16)
                if reused:
                    sp.wait_ge(c["attn"], n - 3)
                sp.dma_start(qT[k][:, :], one(K.qT_d, n)).then_inc(q_in[k], 16)
            steps(sp, NT, 4, 4, body)
            sp.dma_start(out[NT], K.zeros[:, 0:D]).then_inc(c["begun"], 16)
            sp.dma_start(K.tok_d[NT], K.zeros[:, 0:D]).then_inc(c["begun"], 16)
            sp.wait_ge(c["x2"], NT)
            sp.dma_start(out[0:NT].rearrange("t p d -> p t d"), K.x2[:, :, :]).then_inc(c["begun"], 16)
            sp.wait_ge(c["begun"], 48)

        @block.gpsimd
        def _(pool):
            g = nc.gpsimd
            g.iota(ramp[:, :, :], [[0, NT], [-1, E]], base=E, channel_multiplier=0,
                   allow_small_or_imprecise_dtypes=True).then_inc(c["ramp"], 1)

            def body(n, k):
                if old(n):
                    wait_apart(pool, c["passed"], (c["turned"], n - 1))
                g.tensor_copy(mid[k][:, :], tile(acc, n)).then_inc(c["mid"], 1)
            steps(pool, NT, 2, 2, body)
            for known, added, o, done in (("moments", "var", rstd, "rstd"), ("moments2", "var2", rstd2, "rstd2")):
                pool.wait_ge(c[known], MOMENT_STEPS)
                g.tensor_tensor(o[:, :], var[:, :], K.eps[:, :].to_broadcast([P, NT]), ALU.add).then_inc(c[added], 1)
                pool.wait_ge(c[added], 1)
                g.tensor_tensor(o[:, :], o[:, :], K.minus_half[:, :], ALU.pow).then_inc(c[done], 1)

        @block.tensor
        def _(pe):
            t = nc.tensor

            def first(n, slot):
                k = slot % 2
                pe.wait_ge(c["mid"], n + 1)
                if old(n):
                    pe.wait_ge(c["midT"], n - 1)
                for g in range(4):
                    z = t.transpose(ps_m[k][:, g * P:(g + 1) * P], mid[k][:, g * P:(g + 1) * P], K.ident[:, :])
                z.then_inc(c["turned"], 1)
                pe.wait_ge(q_in[slot], per(n, slot, 16, 4))
                if old(n):
                    pe.wait_ge(c["attnT"], n - 1)
                for h in range(2):
                    q = qT[slot][:, h * P:(h + 1) * P]
                    t.matmul(ps_a[k][:, h * P:(h + 1) * P], q, K.ctx_bd[:, h, :], start=True, stop=True)
                    z = t.matmul(ps_a[k][:, D + h * HEADS // 2:D + (h + 1) * HEADS // 2], q, K.ksum_bd[:, h, :],
                                 start=True, stop=True)
                z.then_inc(c["attn"], 1)

            def turn_attention(n, k):
                pe.wait_ge(c["divided"], n + 1)
                for h in range(2):
                    z = t.transpose(ps_a[k][:, h * P:(h + 1) * P], attn[k][:, h * P:(h + 1) * P], K.ident[:, :])
                z.then_inc(c["attn_turned"], 1)

            def second(n, k):
                pe.wait_ge(c["midT"], n + 1)
                if old(n):
                    pe.wait_ge(c["x2"], n - 1)
                for g in range(4):
                    t.matmul(ps_o[k][:, g * MUL:(g + 1) * MUL], midT[k][:, g * P:(g + 1) * P],
                             (K.w_lo0 if g == 0 else K.w_lo1)[:, :], start=True, stop=True)
                pe.wait_ge(c["attnT"], n + 1)
                for h in range(2):
                    z = t.matmul(ps_o[k][:, D:2 * D], attnT[k][:, h * P:(h + 1) * P], K.w_projT[:, h, :],
                                 start=h == 0, stop=h == 1)
                z.then_inc(c["out"], 1)

            def body(n, slot):
                first(n + 1, (slot + 1) % 4)
                turn_attention(n, slot % 2)
                if not (isinstance(n, int) and n == 0):
                    second(n - 1, (slot + 1) % 2)

            first(0, 0)
            steps(pe, NT - 1, 4, 4, body)
            turn_attention(NT - 1, (NT - 1) % 2)
            second(NT - 2, NT % 2)
            second(NT - 1, (NT - 1) % 2)

            def turn(n, k):
                pe.wait_ge(c["xt"], n + 1)
                if old(n):
                    pe.wait_ge(c["xtT"], n - 1)
                for h in range(2):
                    z = t.transpose(ps_x[k][:, h * P:(h + 1) * P], xt[k][:, h * P:(h + 1) * P], K.ident[:, :])
                z.then_inc(c["xt_turned"], 1)

            def logits(n, k):
                pe.wait_ge(c["xtT"], n + 1)
                for h in range(2):
                    z = t.matmul(ps_l[:, bass.ds(n * E, E)], xtT[k][:, h * P:(h + 1) * P], K.w_r[:, h, :],
                                 start=h == 0, stop=h == 1)
                z.then_inc(c["logits"], 1)

            def route(n, k):
                turn(n + 1, 1 - k)
                logits(n, k)

            turn(0, 0)
            steps(pe, NT - 1, 2, 2, route)
            logits(NT - 1, (NT - 1) % 2)

        @block.scalar
        def _(act):
            a = nc.scalar

            def sums(n, k):
                act.wait_ge(c["turned"], n + 1)
                if old(n):
                    act.wait_ge(c["out"], n - 1)
                a.copy(midT[k][:, :], ps_m[k][:, :]).then_inc(c["midT"], 1)

            def attention(n, k):
                act.wait_ge(c["attn_turned"], n + 1)
                if old(n):
                    act.wait_ge(c["out"], n - 1)
                a.copy(attnT[k][:, :], ps_a[k][:, 0:D]).then_inc(c["attnT"], 1)

            def both(n, k):
                attention(n, k)
                sums(n + 1, 1 - k)

            sums(0, 0)
            steps(act, NT - 1, 2, 2, both)
            attention(NT - 1, (NT - 1) % 2)
            act.wait_ge(c["shift"], 1)

            def normed(n, k):
                if old(n):
                    act.wait_ge(c["xt_turned"], n - 1)
                    act.wait_ge(c["stats2"], n - 1)
                a.activation(xt[k][:, :], tile(K.x2, n), ACT.Identity, scale=rstd[:, bass.ds(n, 1)],
                             bias=shift[:, bass.ds(n, 1)]).then_inc(c["xt"], 1)

            steps(act, NT, 2, 2, normed)
            act.wait_ge(c["shifted"], 1)
            a.activation(left[:, :, :], lg[:, :, :], ACT.Exp).then_inc(c["exp"], 1)

        @block.vector
        def _(dve):
            v = nc.vector

            def guard(n, k):
                dve.wait_ge(c["attn"], n + 1)
                if old(n):
                    dve.wait_ge(c["divided"], n - 1)
                v.tensor_scalar(den[k][:, :], ps_a[k][:, D:D + HEADS], 1e-6, None, ALU.max).then_inc(c["den"], 1)

            def invert(n, k):
                dve.wait_ge(c["den"], n + 1)
                v.reciprocal(den[k][:, :], den[k][:, :]).then_inc(c["inverse"], 1)

            def divide(n, k):
                dve.wait_ge(c["inverse"], n + 1)
                if old(n):
                    dve.wait_ge(c["attn_turned"], n - 1)
                by_head = lambda a: a.rearrange("p (h u) -> p h u", h=HEADS)
                v.tensor_tensor(by_head(attn[k][:, :]), by_head(ps_a[k][:, 0:D]),
                                den[k][:, :].unsqueeze(2).to_broadcast([P, HEADS, HD]), ALU.mult).then_inc(c["divided"], 1)

            def onto_residual(n, slot):
                dve.wait_ge(resid_in[slot], per(n, slot, 16, 4))
                dve.wait_ge(c["out"], n + 1)
                v.scalar_tensor_tensor(tile(K.x2, n), ps_o[slot % 2][:, 0:D], K.sc_o[:, bass.ds(n, 1)], resid[slot][:, :],
                                       ALU.mult, ALU.add).then_inc(c["part"], 1)

            def onto_part(n, slot):
                dve.wait_ge(c["part"], n + 1)
                v.tensor_tensor(tile(K.x2, n), ps_o[slot % 2][:, D:2 * D], tile(K.x2, n), ALU.add).then_inc(c["x2"], 1)

            def statistics(n):
                wait_apart(dve, c["passed"], (c["x2"], n + 1))
                v.bn_stats(tile(stats, n), tile(K.x2, n)).then_inc(c["stats"], 1)

            def body(n, slot):
                k, before = (slot + 1) % 2, (slot - 1) % 4
                for step in (guard, invert, divide):
                    step(n + 1, k)
                if not (isinstance(n, int) and n == 0):
                    onto_residual(n - 1, before)
                    onto_part(n - 1, before)
                    statistics(n - 1)

            for step in (guard, invert, divide):
                step(0, 0)
            steps(dve, NT - 1, 4, 4, body)
            for n in (NT - 2, NT - 1):
                onto_residual(n, n % 4)
                onto_part(n, n % 4)
                statistics(n)
            dve.wait_ge(c["stats"], NT)
            moments(dve, v, c["moments"], stats, mean[:, :], var[:, :], diff[:, :])
            dve.wait_ge(c["rstd"], 1)
            v.scalar_tensor_tensor(shift[:, :], mean[:, :], -1.0, rstd[:, :], ALU.mult, ALU.mult).then_inc(c["shift"], 1)

            def norms(n, k):
                wait_apart(dve, c["passed"], (c["xt"], n + 1))
                v.bn_stats(tile(stats, n), xt[k][:, :]).then_inc(c["stats2"], 1)

            def turned(n, k):
                dve.wait_ge(c["xt_turned"], n + 1)
                if old(n):
                    dve.wait_ge(c["logits"], n - 1)
                v.tensor_copy(xtT[k][:, :], ps_x[k][:, 0:D]).then_inc(c["xtT"], 1)

            def rows(n, k):
                norms(n, k)
                turned(n, k)
            steps(dve, NT, 2, 2, rows)
            dve.wait_ge(c["stats2"], NT)
            moments(dve, v, c["moments2"], stats, mean2[:, :], var[:, :], diff[:, :])

            n_done = [0]

            def done(ins):
                n_done[0] += 1
                ins.then_inc(r, 1)
                dve.wait_ge(r, n_done[0])

            wide = lambda a: a.unsqueeze(2).to_broadcast([P, NT, E])
            dve.wait_ge(c["logits"], NT)
            done(v.tensor_tensor(lg[:, :, :], ps_l[:, 0:NT * E].rearrange("p (t e) -> p t e", e=E),
                                 K.b_r[:, :].unsqueeze(1).to_broadcast([P, NT, E]), ALU.add))
            done(v.tensor_reduce(rank, lg[:, :, :], AX.X, ALU.max))
            done(v.tensor_tensor(lg[:, :, :], lg[:, :, :], wide(rank), ALU.subtract))
            dve.sem_inc(c["shifted"], 1)
            dve.wait_ge(c["exp"], 1)
            dve.wait_ge(c["ramp"], 1)
            for i in range(TOP):
                done(v.tensor_reduce(top[:, i, :], left[:, :, :], AX.X, ALU.max))
                done(v.tensor_tensor(eq[:, :, :], left[:, :, :], wide(top[:, i, :]), ALU.is_equal))
                done(v.tensor_tensor(eq[:, :, :], eq[:, :, :], ramp[:, :, :], ALU.mult))
                done(v.tensor_reduce(rank, eq[:, :, :], AX.X, ALU.max))
                done(v.tensor_tensor(K.onehot[:, :, i, :], eq[:, :, :], wide(rank), ALU.is_equal))
                if i + 1 < TOP:
                    done(v.scalar_tensor_tensor(left[:, :, :], K.onehot[:, :, i, :], -2.0, left[:, :, :], ALU.mult, ALU.add))
            done(v.tensor_tensor(total, top[:, 0, :], top[:, 1, :], ALU.add))
            done(v.reciprocal(total, total))
            for i in range(TOP):
                done(v.tensor_tensor(K.weight[:, :, i], top[:, i, :], total, ALU.mult))
            dve.wait_ge(c["shift"], 1)
            dve.wait_ge(c["rstd2"], 1)
            done(v.tensor_tensor(K.tok_scale[:, :], rstd[:, :], rstd2[:, :], ALU.mult))
            done(v.tensor_tensor(K.tok_shift[:, :], shift[:, :], mean2[:, :], ALU.subtract))
            done(v.tensor_tensor(K.tok_shift[:, :], K.tok_shift[:, :], rstd2[:, :], ALU.mult))


def dispatch(nc, A, K):
    G = NT * TOP
    with ExitStack() as ctx:
        m = Mem(nc, ctx, "dispatch")
        tot, incl, place = (m.sb(x, [P, G, E]) for x in ("tot", "incl", "place"))
        nb_i = m.sb("nb_i", [P, E], i32)
        nb, b_end, first = (m.sb(x, [P, E]) for x in ("nb", "b_end", "first"))
        pos = m.sb("pos", [P, G])
        gone, which = m.sb("gone", [1, NSB, E]), m.sb("which", [1, NSB])
        tok = [m.sb(f"tok{k}", [P, D]) for k in range(4)]
        part, lo, hi, ids = m.sb("part", [P, G], i32), m.sb("lo", [P, G]), m.sb("hi", [P, G]), m.sb("ids", [P, G])
        C = NSLOT // P
        hot_lo, hot_hi, hot_id, hot_w = ([m.sb(f"{z}{k}", [P, GP, w]) for k in range(2)] for z, w in (
            ("hot_lo", P), ("hot_hi", C), ("hot_id", C), ("hot_w", C)))
        pos_i, spare, empty = m.sb("pos_i", [P, G], i32), m.sb("spare", [P, 1]), m.sb("empty", [P, C])
        ps_token, ps_weight = m.ps("token"), m.ps("weight")
        ps_w, ps_t = m.ps("within", 2), m.ps("total", 2)
        d, summed, normed, numbered, hot_one, hot, hot_weight, looked_up = (m.sem(x) for x in (
            "vector_steps", "summed", "normed", "numbered", "hot_one", "hot", "hot_weight", "looked_up"))
        sent = [m.sem(f"sent{k}") for k in range(4)]
        half = G // 2
        of_step = lambda a, n, w: a[:, bass.ds(n * GP, GP)].unsqueeze(2).to_broadcast([P, GP, w])
        block = ctx.enter_context(nc.Block())
        old = lambda n: not (isinstance(n, int) and n < 4)

        @block.tensor
        def _(pe):
            for w, ps in ((K.before, ps_w), (K.ones, ps_t)):
                for h in range(2):
                    rhs = K.onehot[:, :, :, :].rearrange("p n t e -> p (n t e)")[:, h * half * E:(h + 1) * half * E]
                    x = nc.tensor.matmul(ps[:, h * 512:h * 512 + half * E], w[:, :], rhs, start=True, stop=True)
            x.then_inc(summed, 1)

            def look_up(n, k):
                pe.wait_ge(hot, n + 1)
                pe.wait_ge(hot_weight, n + 1)
                first, last = (isinstance(n, int) and n == e for e in (0, G // GP - 1))
                for j in range(GP):
                    for ps, hot_x in ((ps_token, hot_id), (ps_weight, hot_w)):
                        x = nc.tensor.matmul(ps[:, 0:C], hot_lo[k][:, j, :], hot_x[k][:, j, :],
                                             start=first and j == 0, stop=last and j == GP - 1)
                x.then_inc(looked_up, 1)
            steps(pe, G // GP - 1, 2, 2, look_up)
            look_up(G // GP - 1, (G // GP - 1) % 2)

        @block.vector
        def _(dve):
            v, n = nc.vector, [0]

            def done(ins):
                n[0] += 1
                ins.then_inc(d, 1)
                dve.wait_ge(d, n[0])

            halves = lambda ps: ps[:, :].rearrange("p (h n) -> p h n", h=2)[:, :, 0:half * E]
            dve.wait_ge(summed, 1)
            done(v.tensor_copy(tot[:, :, :].rearrange("p (h g) e -> p h (g e)", h=2), halves(ps_t)))
            for e in range(E):
                done(v.tensor_tensor_scan(incl[:, :, e], K.ones[:, 0:G], tot[:, :, e], 0.0, ALU.mult, ALU.add))
            done(v.tensor_tensor(place[:, :, :], incl[:, :, :], tot[:, :, :], ALU.subtract))
            done(v.tensor_tensor(place[:, :, :].rearrange("p (h g) e -> p h (g e)", h=2),
                                 place[:, :, :].rearrange("p (h g) e -> p h (g e)", h=2), halves(ps_w), ALU.add))
            done(v.tensor_scalar(nb[:, :], incl[:, G - 1, :], float(SB - 1), None, ALU.add))
            done(v.tensor_copy(nb_i[:, :], nb[:, :]))
            done(v.tensor_scalar(nb_i[:, :], nb_i[:, :], SB.bit_length() - 1, None, ALU.arith_shift_right))
            done(v.tensor_copy(nb[:, :], nb_i[:, :]))
            done(v.tensor_tensor_scan(b_end[:, :], K.ones[:, 0:E], nb[:, :], 0.0, ALU.mult, ALU.add))
            done(v.tensor_tensor(first[:, :], b_end[:, :], nb[:, :], ALU.subtract))
            done(v.tensor_scalar(first[:, :], first[:, :], float(SB), None, ALU.mult))
            done(v.tensor_tensor(place[:, :, :], place[:, :, :], first[:, :].unsqueeze(1).to_broadcast([P, G, E]), ALU.add))
            done(v.tensor_tensor(place[:, :, :], place[:, :, :], K.onehot[:, :, :, :].rearrange("p n t e -> p (n t) e"),
                                 ALU.mult))
            done(v.tensor_reduce(pos[:, :], place[:, :, :], AX.X, ALU.add))
            done(v.tensor_copy(pos_i[:, :], pos[:, :]))
            done(v.tensor_scalar(part[:, :], pos_i[:, :], P - 1, None, ALU.bitwise_and))
            done(v.tensor_copy(lo[:, :], part[:, :]))
            done(v.tensor_scalar(part[:, :], pos_i[:, :], 7, None, ALU.arith_shift_right))
            done(v.tensor_copy(hi[:, :], part[:, :]))
            dve.wait_ge(numbered, 1)

            def hots(n, k):
                if not (isinstance(n, int) and n < 2):
                    dve.wait_ge(looked_up, n - 1)
                wide = lambda a, w: of_step(a, n, w)
                count = lambda w: K.iota_f[:, 0:w].unsqueeze(1).to_broadcast([P, GP, w])
                v.tensor_tensor(hot_hi[k][:, :, :], count(C), wide(hi, C), ALU.is_equal).then_inc(hot_one, 1)
                v.tensor_tensor(hot_lo[k][:, :, :], count(P), wide(lo, P), ALU.is_equal)
                dve.wait_ge(hot_one, n + 1)
                v.tensor_tensor(hot_id[k][:, :, :], hot_hi[k][:, :, :], wide(ids, C), ALU.mult).then_inc(hot, 1)
            steps(dve, G // GP, 2, 2, hots)
            done(v.tensor_tensor(gone[:, :, :], K.iota_f[0:1, 0:NSB].unsqueeze(2).to_broadcast([1, NSB, E]),
                                 b_end[0:1, :].unsqueeze(1).to_broadcast([1, NSB, E]), ALU.is_ge))
            done(v.tensor_reduce(which[:, :], gone[:, :, :], AX.X, ALU.add))
            done(v.tensor_scalar(which[:, :], which[:, :], float(E - 1), None, ALU.min))
            done(v.tensor_copy(K.block_expert[:, :], which[:, :]))
            dve.wait_ge(looked_up, G // GP)
            v.tensor_copy(K.slot_weight[:, :], ps_weight[:, 0:C])
            done(v.tensor_scalar(empty[:, :], ps_token[:, 0:C], 0.0, None, ALU.is_equal))
            done(v.tensor_scalar(empty[:, :], empty[:, :], spare[:, :], None, ALU.mult))
            done(v.scalar_tensor_tensor(empty[:, :], ps_token[:, 0:C], -1.0, empty[:, :], ALU.add, ALU.add))
            done(v.tensor_copy(K.slot_token[:, :], empty[:, :]))

        @block.scalar
        def _(act):
            def body(n, k):
                if old(n):
                    act.wait_ge(sent[k], per(n, k, 16, 4) - 16)
                nc.scalar.activation(tok[k][:, :], K.x2[:, bass.ds(n, 1), :].rearrange("p a d -> p (a d)"), ACT.Identity,
                                     scale=K.tok_scale[:, bass.ds(n, 1)],
                                     bias=K.tok_shift[:, bass.ds(n, 1)]).then_inc(normed, 1)
            steps(act, NT, 4, 4, body)

        @block.sync
        def _(sp):
            def body(n, k):
                sp.wait_ge(normed, n + 1)
                sp.dma_start(K.tok_d[bass.ds(n, 1), :, :].rearrange("a p d -> (a p) d"), tok[k][:, :]).then_inc(sent[k], 16)
            steps(sp, NT, 4, 4, body)
            for k in range(4):
                sp.wait_ge(sent[k], 16 * ((NT + 3 - k) // 4))

        @block.gpsimd
        def _(pool):
            nc.gpsimd.iota(spare[:, :], [[0, 1]], base=N_PAD + 1, channel_multiplier=1, allow_small_or_imprecise_dtypes=True)
            nc.gpsimd.iota(ids[:, :].rearrange("p (n t) -> p n t", t=TOP), [[P, NT], [0, TOP]], base=1, channel_multiplier=1,
                           allow_small_or_imprecise_dtypes=True).then_inc(numbered, 1)
            weights = K.weight[:, :, :].rearrange("p n t -> p (n t)")

            def weighted(n, k):
                pool.wait_ge(hot_one, n + 1)
                nc.gpsimd.tensor_tensor(hot_w[k][:, :, :], hot_hi[k][:, :, :], of_step(weights, n, C),
                                        ALU.mult).then_inc(hot_weight, 1)
            steps(pool, G // GP, 2, 2, weighted)


def experts(nc, A, K, out):
    NH = H // P
    with ExitStack() as ctx:
        m = Mem(nc, ctx, "experts")
        two = lambda name, shape, dt=f32: [m.sb(f"{name}{k}", shape, dt) for k in range(2)]
        w1, w2 = two("w1", [P, 2, H]), two("w2", [P, NH, D])
        ec, b2 = two("constants", [P, 2 + 2 + NH]), two("b2", [P, D])
        xb, xT, hT, yb = two("x", [P, 2, D]), two("xT", [P, 2, SB]), two("hT", [P, NH, SB]), two("y", [P, 2, D])
        ps_x = [m.ps(f"x{k}") for k in range(2)]
        ps_h = [m.ps(f"h{k}") for k in range(4)]
        ps_y = [m.ps(f"y{k}") for k in range(2)]
        rows_in, loaded = ([m.sem(f"{x}{k}") for k in range(2)] for x in ("rows_in", "loaded"))
        c = {x: m.sem(x) for x in ("turned", "xT", "first", "gelu", "second", "y", "weighted", "copied", "copied_out",
                                   "added", "passed")}
        idx, idx_out = two("idx", [P, 2], i32), two("idx_out", [P, 2], i32)
        raw = m.sb("raw", [P, 2, D])
        block = ctx.enter_context(nc.Block())
        old = lambda n: not (isinstance(n, int) and n < 2)
        LD = 16 * 4

        @block.sync
        def _(sp):
            def body(n, k):
                if old(n):
                    sp.wait_ge(c["y"], n - 1)
                e = sp.value_load(K.block_expert[0:1, bass.ds(n, 1)], min_val=0, max_val=E - 1)
                one = lambda a: a[bass.ds(e, 1), :, :].rearrange("a p n -> (a p) n")
                sp.dma_start(ec[k][:, :], one(A["e_const"])).then_inc(loaded[k], 16)
                sp.dma_start(w1[k][:, :, :].rearrange("p c n -> p (c n)"), one(A["w1"])).then_inc(loaded[k], 16)
                sp.dma_start(b2[k][:, :], one(A["b2"]).to_broadcast([P, D])).then_inc(loaded[k], 16)
                sp.dma_start(w2[k][:, :, :].rearrange("p c n -> p (c n)"), one(A["w2"])).then_inc(loaded[k], 16)
            steps(sp, NSB, 2, 2, body)

        @block.gpsimd
        def _(pool):
            flat = lambda d: d.rearrange("t p d -> (t p) d")
            at = lambda i: bass.IndirectOffsetOnAxis(ap=i, axis=0)
            bounds = dict(bounds_check=N_PAD + P - 1)

            def gather(n, k):
                if old(n):
                    wait_apart(pool, c["passed"], (c["turned"], n - 1))
                nc.gpsimd.tensor_copy(idx[k][:, :], K.slot_token[:, bass.ds(n * 2, 2)]).then_inc(c["copied"], 1)
                wait_apart(pool, c["passed"], (c["copied"], n + 1))
                for s in range(2):
                    nc.gpsimd.indirect_dma_start(out=xb[k][:, s, :], out_offset=None, in_=flat(K.tok_d),
                                                 in_offset=at(idx[k][:, s:s + 1]), oob_is_err=False,
                                                 **bounds).then_inc(rows_in[k], 16)

            def scatter(n, k):
                if old(n):
                    wait_apart(pool, c["passed"], (c["added"], 32 * (n - 1)))
                nc.gpsimd.tensor_copy(idx_out[k][:, :], K.slot_token[:, bass.ds(n * 2, 2)]).then_inc(c["copied_out"], 1)
                wait_apart(pool, c["passed"], (c["copied_out"], n + 1), (c["weighted"], n + 1))
                for s in range(2):
                    if not (isinstance(n, int) and n == 0 and s == 0):
                        wait_apart(pool, c["passed"], (c["added"], n * 32 + 16 * s))
                    nc.gpsimd.indirect_dma_start(out=flat(out), out_offset=at(idx_out[k][:, s:s + 1]), in_=yb[k][:, s, :],
                                                 in_offset=None, compute_op=ALU.add, oob_is_err=True,
                                                 **bounds).then_inc(c["added"], 16)

            def body(n, k):
                gather(n + 2, k)
                scatter(n, k)

            gather(0, 0)
            gather(1, 1)
            steps(pool, NSB - 2, 2, 2, body)
            scatter(NSB - 2, 0)
            scatter(NSB - 1, 1)
            pool.wait_ge(c["added"], 32 * NSB)

        @block.tensor
        def _(pe):
            t = nc.tensor

            def turn(n, k):
                pe.wait_ge(rows_in[k], per(n, k, 32))
                if old(n):
                    pe.wait_ge(c["xT"], n - 1)
                for h in range(2):
                    for s in range(2):
                        x = t.transpose(ps_x[k][:, h * SB + s * P:h * SB + (s + 1) * P], xb[k][:, s, h * P:(h + 1) * P],
                                        K.ident[:, :])
                x.then_inc(c["turned"], 1)

            def layers(n, k, more):
                pe.wait_ge(c["xT"], n + 1)
                pe.wait_ge(loaded[k], per(n, k, LD))
                for j in range(NH):
                    if not (isinstance(n, int) and n == 0 and j < 4):
                        pe.wait_ge(c["gelu"], n * NH + (j - 3))
                    for h in range(2):
                        x = t.matmul(ps_h[j % 4][:, 0:SB], w1[k][:, h, j * P:(j + 1) * P], xT[k][:, h, :],
                                     start=h == 0, stop=h == 1)
                    x.then_inc(c["first"], 1)
                if more:
                    turn(n + 1, 1 - k)
                if not (isinstance(n, int) and n == 0):
                    pe.wait_ge(c["y"], n)
                for j in range(NH):
                    pe.wait_ge(c["gelu"], n * NH + (j + 1))
                    for s in range(2):
                        x = t.matmul(ps_y[s][:, 0:D], hT[k][:, j, s * P:(s + 1) * P], w2[k][:, j, :],
                                     start=j == 0, stop=j == NH - 1)
                x.then_inc(c["second"], 1)

            turn(0, 0)
            steps(pe, NSB - 2, 2, 2, lambda n, k: layers(n, k, True))
            layers(NSB - 2, 0, True)
            layers(NSB - 1, 1, False)

        @block.scalar
        def _(act):
            def shift(n, k):
                act.wait_ge(c["turned"], n + 1)
                act.wait_ge(loaded[k], per(n, k, LD))
                if old(n):
                    act.wait_ge(c["first"], (n - 1) * NH)
                for h in range(2):
                    x = nc.scalar.activation(xT[k][:, h, :], ps_x[k][:, h * SB:(h + 1) * SB], ACT.Identity,
                                             scale=ec[k][:, h:h + 1], bias=ec[k][:, 2 + h:3 + h])
                x.then_inc(c["xT"], 1)

            def gelu(n, k, more):
                if old(n):
                    act.wait_ge(c["second"], n - 1)
                for j in range(NH):
                    act.wait_ge(c["first"], n * NH + (j + 1))
                    nc.scalar.activation(hT[k][:, j, :], ps_h[j % 4][:, 0:SB], ACT.Gelu,
                                         bias=ec[k][:, 4 + j:5 + j]).then_inc(c["gelu"], 1)
                if more:
                    shift(n + 1, 1 - k)

            shift(0, 0)
            steps(act, NSB - 2, 2, 2, lambda n, k: gelu(n, k, True))
            gelu(NSB - 2, 0, True)
            gelu(NSB - 1, 1, False)

        @block.vector
        def _(dve):
            def body(n, k):
                dve.wait_ge(c["second"], n + 1)
                if not (isinstance(n, int) and n == 0):
                    dve.wait_ge(c["weighted"], n)
                for s in range(2):
                    x = nc.vector.tensor_tensor(raw[:, s, :], ps_y[s][:, 0:D], b2[k][:, :], ALU.add)
                x.then_inc(c["y"], 1)
                dve.wait_ge(c["y"], n + 1)
                if old(n):
                    dve.wait_ge(c["added"], 32 * (n - 1))
                for s in range(2):
                    x = nc.vector.tensor_scalar(yb[k][:, s, :], raw[:, s, :], K.slot_weight[:, bass.ds(n * 2 + s, 1)], None,
                                                ALU.mult)
                x.then_inc(c["weighted"], 1)
            steps(dve, NSB, 2, 2, body)


class Shared:
    pass


def program(nc, A, out):
    with ExitStack() as ctx:
        K = Shared()
        sb = Mem(nc, ctx, "k").sb
        dram = lambda name, shape: nc.dram_tensor(name, shape, f32, kind="Internal").ap()
        K.table_d, K.resid_d = dram("gather_table", (NT, P, D)), dram("residual", (NT, P, D))
        K.qT_d = dram("queries_T", (NT, P, D))
        K.el_hi_d, K.el_lo_d = dram("el_hi", (NG, BAS, GE)), dram("el_lo", (NG, BAS, GE))
        K.tok_d = dram("tokens", (NT + 1, P, D))
        K.ident, K.ones, K.iota_f, K.before, K.upto, K.head_mask = (
            sb(x, [P, P]) for x in ("ident", "ones", "iota_f", "before", "upto", "head_mask"))
        K.minus_half, K.eps = sb("minus_half", [P, NT]), sb("eps", [P, 1])
        K.zeros = sb("zeros", [P, 512])
        K.x2 = sb("x2", [P, NT, D])
        K.tok_scale, K.tok_shift = sb("tok_scale", [P, NT]), sb("tok_shift", [P, NT])
        K.valid_row, K.attr, K.dis, K.sc_f, K.sc_m, K.sc_o = (
            sb(x, [P, NT]) for x in ("valid_row", "attr", "dis", "sc_f", "sc_m", "sc_o"))
        K.w_nodeA, K.w_nodeB = sb("w_nodeA", [P, 256]), sb("w_nodeB", [P, 256])
        K.w_kvT, K.w_qT, K.w_projT = sb("w_kvT", [P, 2, 512]), sb("w_qT", [P, 2, 256]), sb("w_projT", [P, 2, 256])
        K.w_e1, K.w_e2 = sb("w_e1", [3 * BAS, HID]), sb("w_e2", [HID, 256])
        K.w_e1s = sb("w_e1s", [3 * BAS, HID], f32r)
        K.w_lo0, K.w_lo1 = sb("w_lo0", [P, MUL]), sb("w_lo1", [P, MUL])
        K.w_r, K.b_r, K.b_proj = sb("w_r", [P, 2, E]), sb("b_r", [P, E]), sb("b_proj", [P, D])
        K.item_group, K.item_block = sb("item_group", [1, NI], i32), sb("item_block", [1, NI], i32)
        K.item_base = sb("item_base", [P, NI])
        K.ctx_bd, K.ksum_bd = sb("ctx_bd", [P, 2, P]), sb("ksum_bd", [P, 2, P // HD])
        K.weight, K.onehot = sb("weight", [P, NT, TOP]), sb("onehot", [P, NT, TOP, E])
        K.block_expert = sb("block_expert", [1, NSB], i32)
        K.slot_token, K.slot_weight = sb("slot_token", [P, NSLOT // P], i32), sb("slot_weight", [P, NSLOT // P])
        setup(nc, A, K)
        items(nc, A, K)
        nodes(nc, A, K)
        with ExitStack() as sums:
            acc = sums.enter_context(nc.sbuf_tensor("accumulators", [P, NB + 1, 512], f32))
            edges(nc, A, K, acc)
            update(nc, A, K, acc, out)
        dispatch(nc, A, K)
        experts(nc, A, K, out)


def kernel(x, src, dst, edge_attr_10, edge_attr_4, node_vec1, L0_gnn_W_li0, L0_gnn_W_li1, L0_gnn_W_lm0, L0_gnn_W_lm1,
           L0_gnn_W_mlp1, L0_gnn_W_mlp2, L0_gnn_W_lo0, L0_gnn_W_lo1, L0_mix_Wq, L0_mix_Wkv, L0_mix_Wproj, L0_mix_bproj,
           L0_ffn_Wr, L0_ffn_br, L0_ffn_ln_g, L0_ffn_ln_b, L0_ffn_W1, L0_ffn_b1, L0_ffn_W2, L0_ffn_b2):
    import numpy as np
    import concourse.bacc as bacc
    from concourse.bass_utils import run_bass_kernel_spmd

    perm = np.concatenate([np.arange(MUL)] + [MUL + 3 * np.arange(MUL) + i for i in range(3)])

    def rows(a, n, fill=0):
        a = np.asarray(a)
        pad = np.full((n - a.shape[0],) + a.shape[1:], fill, a.dtype)
        return np.concatenate([a, pad])

    def diag(a, b):
        z = np.zeros((MUL, MUL), np.asarray(a).dtype)
        return np.block([[np.asarray(a), z], [z, np.asarray(b)]])

    ne = NG * GE
    by_group = lambda a: a.reshape(NG, GC, P, -1).transpose(0, 2, 1, 3).reshape(NG, P, -1)
    dst_p = rows(dst, NGP * GE, N_PAD - 1)
    y = np.asarray(edge_attr_4)
    chunks = lambda w: np.asarray(w).reshape(2, P, -1)
    W_2 = np.asarray(L0_gnn_W_mlp2).reshape(HID, 4, MUL)[:, [0, 3, 1, 2]].reshape(HID, 256)
    swap = lambda w: np.asarray(w).reshape(2, MUL, MUL)[::-1].reshape(P, MUL)
    per_chunk = lambda a: np.asarray(a).reshape(E, -1, P).transpose(0, 2, 1)
    arrays = {
        "x": rows(np.asarray(x)[:, perm], N_PAD).reshape(NT, P, D),
        "attr": rows(node_vec1, N_PAD).reshape(NT, P).T,
        "ends": np.concatenate([by_group(rows(src, ne)), by_group(dst_p[:ne])], 2),
        "dst_cols": dst_p[:NC * P].reshape(NC, P).T,
        "dst_rows": dst_p.reshape(NGP, GE),
        "y": by_group(rows(y, ne)),
        "el": rows(edge_attr_10, ne).reshape(NG, GE, BAS).transpose(0, 2, 1),
        "w_e1": np.concatenate([np.asarray(L0_gnn_W_mlp1)] * 3), "w_e2": W_2,
        "w_nodeA": np.concatenate([diag(L0_gnn_W_li0, L0_gnn_W_li1), diag(L0_gnn_W_lm0, L0_gnn_W_lm1)], 1),
        "w_nodeB": np.concatenate([diag(L0_gnn_W_li1, L0_gnn_W_li1), diag(L0_gnn_W_lm1, L0_gnn_W_lm1)], 1),
        "w_lo0": np.asarray(L0_gnn_W_lo0), "w_lo1": swap(L0_gnn_W_lo1),
        "w_kvT": chunks(np.asarray(L0_mix_Wkv)[:, perm].T), "w_qT": chunks(np.asarray(L0_mix_Wq)[:, perm].T),
        "w_projT": chunks(np.asarray(L0_mix_Wproj)[perm].T), "b_proj": np.asarray(L0_mix_bproj)[perm][None],
        "w_r": chunks(np.asarray(L0_ffn_Wr)[perm]), "b_r": np.asarray(L0_ffn_br)[None],
        "w1": np.asarray(L0_ffn_W1)[:, perm].reshape(E, 2, P, H).transpose(0, 2, 1, 3).reshape(E, P, 2 * H),
        "w2": np.asarray(L0_ffn_W2)[:, :, perm].reshape(E, H // P, P, D).transpose(0, 2, 1, 3).reshape(E, P, -1),
        "e_const": np.concatenate([per_chunk(np.asarray(L0_ffn_ln_g)[:, perm]), per_chunk(np.asarray(L0_ffn_ln_b)[:, perm]),
                                   per_chunk(L0_ffn_b1)], 2),
        "b2": np.asarray(L0_ffn_b2)[:, perm][:, None],
    }
    arrays = {f"in_{k}": np.ascontiguousarray(a) for k, a in arrays.items()}
    nc = bacc.Bacc("TRN2", target_bir_lowering=False, num_devices=1)
    A = {k[3:]: nc.dram_tensor(k, a.shape, mybir.dt.from_np(a.dtype), kind="ExternalInput").ap()
         for k, a in arrays.items()}
    out = nc.dram_tensor("out", (NT + 1, P, D), f32, kind="ExternalOutput").ap()
    program(nc, A, out)
    got = run_bass_kernel_spmd(nc, [arrays], core_ids=[0]).results[0]["out"]
    result = np.empty((N_NODES, D), got.dtype)
    result[:, perm] = got.reshape(-1, D)[:N_NODES]
    return result
```
